# Optimizing a Trainium2 kernel written in Bass

```python
import numpy as np
import jax
import jax.numpy as jnp

def _softmax(x, axis=-1):
    return jax.nn.softmax(x, axis=axis)

def _gelu(x):
    return jax.nn.gelu(x, approximate=True)

def _silu(x):
    return jax.nn.silu(x)

def _sigmoid(x):
    return jax.nn.sigmoid(x)

def _layernorm(x, axis=-1, eps=1e-05):
    m = jnp.mean(x, axis=axis, keepdims=True)
    v = jnp.var(x, axis=axis, keepdims=True)
    return (x - m) / jnp.sqrt(v + eps)

def _scatter_add(tgt, idx, src, axis=0):
    return tgt.at[idx].add(src)

def _segment_sum(src, seg, n):
    return jax.ops.segment_sum(src, seg, n)
kernel_name = 'mk_decoder_preln_d2_seqx_r8_69343b'

def setup_inputs(seed: int=0):
    np.random.seed(seed)
    _w = jnp.asarray

    def _rec_inputs():
        import jax
        import jax.numpy as jnp
        _rk = jax.random.key(seed)
        x = -0.0002928 + 1 * jax.random.normal(jax.random.fold_in(_rk, 1), (4, 512, 128), jnp.float32)
        _lenS = 512 - jax.random.randint(jax.random.fold_in(_rk, 7), (4,), 0, max(1, 512 // 4) + 1, jnp.int32)
        _lenS2 = 154 - jax.random.randint(jax.random.fold_in(_rk, 8), (4,), 0, max(1, 154 // 4) + 1, jnp.int32)
        _ctx_1024P = jax.random.normal(jax.random.fold_in(_rk, 11), (4, 16, 128), jnp.float32)
        _ctx_1024c = jax.random.dirichlet(jax.random.fold_in(_rk, 511), 0.3 * jnp.ones((16,), jnp.float32), (4, 154))
        _ctx_1024t = jnp.einsum('bsk,bkd->bsd', _ctx_1024c, _ctx_1024P)
        _ctx_1024t = _ctx_1024t * jax.lax.rsqrt(jnp.mean(jnp.square(_ctx_1024t)) + 1e-12) * 0.953939
        ctx_1024 = -1.39393e-06 + 0.999914 * (_ctx_1024t + 0.3 * jax.random.normal(jax.random.fold_in(_rk, 611), (4, 154, 128), jnp.float32))
        _validS = jnp.arange(512)[None, :] < _lenS[:, None]
        _validS2 = jnp.arange(154)[None, :] < _lenS2[:, None]
        _causal = jnp.tril(jnp.ones((512, 512), dtype=bool))
        mask_SxS2_bk1 = jnp.broadcast_to(_validS2[0:1, :], (512, 154))
        mask_BxS2_bf0 = jnp.logical_not(jnp.ones((4, 154), dtype=bool))
        return (x, ctx_1024, mask_SxS2_bk1, mask_BxS2_bf0)
    x, ctx_1024, mask_SxS2_bk1, mask_BxS2_bf0 = _rec_inputs()

    def _L0_attn_setup():
        import jax, jax.numpy as jnp
        import numpy as np
        EPS = 1e-06
        N_HEADS = 16

        def _heads(t, B, N, H, Dk):
            return t.reshape(B, N, H, Dk).transpose(0, 2, 1, 3)
        key = jax.random.key(seed)
        ks = jax.random.split(key, 5)
        B, N, D = (64, 64, 128)
        x = jax.random.normal(ks[0], (B, N, D), dtype=jnp.float32)
        s = 0.02
        W_q = jax.random.normal(ks[1], (D, D), dtype=jnp.float32) * s
        W_k = jax.random.normal(ks[2], (D, D), dtype=jnp.float32) * s
        W_v = jax.random.normal(ks[3], (D, D), dtype=jnp.float32) * s
        W_o = jax.random.normal(ks[4], (D, D), dtype=jnp.float32) * s
        z = jnp.zeros((D,), dtype=jnp.float32)
        return {'x': x, 'W_q': W_q, 'b_q': z, 'W_k': W_k, 'b_k': z, 'W_v': W_v, 'b_v': z, 'W_o': W_o, 'b_o': z}
    _L0_attn_all = _L0_attn_setup()
    _L0_attn_in = {k: v for k, v in _L0_attn_all.items() if k in ('W_q', 'b_q', 'W_k', 'b_k', 'W_v', 'b_v', 'W_o', 'b_o')}
    del _L0_attn_all

    def _L0_xattn_setup():
        import jax, jax.numpy as jnp
        import numpy as np
        B, T, D, H = (2, 256, 128, 16)
        DK = D // H
        SCALE = 1.0 / float(np.sqrt(DK))
        key0 = jax.random.key(seed)
        ks = jax.random.split(key0, 12)
        std = 0.02
        inp = {'query': jax.random.normal(ks[0], (B, T, D), jnp.float32), 'key': jax.random.normal(ks[1], (B, T, D), jnp.float32), 'value': jax.random.normal(ks[2], (B, T, D), jnp.float32), 'Wq': jax.random.normal(ks[3], (D, D), jnp.float32) * std, 'bq': jnp.zeros((D,), jnp.float32), 'Wk': jax.random.normal(ks[4], (D, D), jnp.float32) * std, 'bk': jnp.zeros((D,), jnp.float32), 'Wv': jax.random.normal(ks[5], (D, D), jnp.float32) * std, 'bv': jnp.zeros((D,), jnp.float32), 'Wo': jax.random.normal(ks[6], (D, D), jnp.float32) * std, 'bo': jnp.zeros((D,), jnp.float32), 'attn_mask': jnp.triu(jnp.ones((T, T), jnp.bool_), k=1), 'key_padding_mask': jnp.zeros((B, T), jnp.bool_)}
        return inp
    _L0_xattn_all = _L0_xattn_setup()
    _L0_xattn_in = {k: v for k, v in _L0_xattn_all.items() if k in ('Wq', 'bq', 'Wk', 'bk', 'Wv', 'bv', 'Wo', 'bo')}
    del _L0_xattn_all

    def _L0_ffn_setup():
        import jax, jax.numpy as jnp
        import numpy as np
        DIM, HIDDEN, E = (128, 512, 8)
        B, L = (2, 256)
        key = jax.random.key(seed)
        ks = jax.random.split(key, 6)
        s_in = 1.0 / np.sqrt(DIM)
        s_h = 1.0 / np.sqrt(HIDDEN)
        return {'x': jax.random.normal(ks[0], (B, L, DIM), dtype=jnp.float32), 'Wg': jax.random.uniform(ks[1], (E, DIM), jnp.float32, -s_in, s_in), 'W1': jax.random.uniform(ks[2], (E, DIM, HIDDEN), jnp.float32, -s_in, s_in), 'b1': jax.random.uniform(ks[3], (E, HIDDEN), jnp.float32, -s_in, s_in), 'W2': jax.random.uniform(ks[4], (E, HIDDEN, DIM), jnp.float32, -s_h, s_h), 'b2': jax.random.uniform(ks[5], (E, DIM), jnp.float32, -s_h, s_h)}
    _L0_ffn_all = _L0_ffn_setup()
    _L0_ffn_in = {k: v for k, v in _L0_ffn_all.items() if k in ('Wg', 'W1', 'b1', 'W2', 'b2')}
    del _L0_ffn_all

    def _L1_attn_setup():
        import jax, jax.numpy as jnp
        import numpy as np
        NUM_HEADS = 16
        MAX_REL = 128

        def _rel_table_lookup(table, q_len, k_len):
            dist = jnp.arange(q_len)[:, None] - jnp.arange(k_len)[None, :]
            idx = jnp.clip(dist, -MAX_REL, MAX_REL) + MAX_REL
            return table[idx]
        key = jax.random.key(seed)
        ks = jax.random.split(key, 12)
        B, T, E = (4, 128, 128)
        D = E // NUM_HEADS
        s = 0.02
        return {'hidden_states': jax.random.normal(ks[0], (B, T, E), dtype=jnp.float32), 'Wq': jax.random.normal(ks[1], (E, E), dtype=jnp.float32) * s, 'bq': jnp.zeros((E,), dtype=jnp.float32), 'Wk': jax.random.normal(ks[2], (E, E), dtype=jnp.float32) * s, 'bk': jnp.zeros((E,), dtype=jnp.float32), 'Wv': jax.random.normal(ks[3], (E, E), dtype=jnp.float32) * s, 'bv': jnp.zeros((E,), dtype=jnp.float32), 'Wo': jax.random.normal(ks[4], (E, E), dtype=jnp.float32) * s, 'bo': jnp.zeros((E,), dtype=jnp.float32), 'rel_k': jax.random.normal(ks[5], (2 * MAX_REL + 1, D), dtype=jnp.float32) * s, 'rel_v': jax.random.normal(ks[6], (2 * MAX_REL + 1, D), dtype=jnp.float32) * s}
    _L1_attn_all = _L1_attn_setup()
    _L1_attn_in = {k: v for k, v in _L1_attn_all.items() if k in ('Wq', 'bq', 'Wk', 'bk', 'Wv', 'bv', 'Wo', 'bo', 'rel_k', 'rel_v')}
    del _L1_attn_all

    def _L1_xattn_setup():
        import jax, jax.numpy as jnp
        import numpy as np
        NHEADS = 16
        key = jax.random.key(seed)
        ks = jax.random.split(key, 11)
        B, S, D = (2, 256, 128)
        std = 1.0 / np.sqrt(D)
        return {'query': jax.random.normal(ks[0], (B, S, D), jnp.float32), 'key': jax.random.normal(ks[1], (B, S, D), jnp.float32), 'value': jax.random.normal(ks[2], (B, S, D), jnp.float32), 'Wq': jax.random.normal(ks[3], (D, D), jnp.float32) * std, 'bq': jax.random.normal(ks[4], (D,), jnp.float32) * std, 'Wk': jax.random.normal(ks[5], (D, D), jnp.float32) * std, 'bk': jax.random.normal(ks[6], (D,), jnp.float32) * std, 'Wv': jax.random.normal(ks[7], (D, D), jnp.float32) * std, 'bv': jax.random.normal(ks[8], (D,), jnp.float32) * std, 'Wo': jax.random.normal(ks[9], (D, D), jnp.float32) * std, 'bo': jax.random.normal(ks[10], (D,), jnp.float32) * std}
    _L1_xattn_all = _L1_xattn_setup()
    _L1_xattn_in = {k: v for k, v in _L1_xattn_all.items() if k in ('Wq', 'bq', 'Wk', 'bk', 'Wv', 'bv', 'Wo', 'bo')}
    del _L1_xattn_all

    def _L1_ffn_setup():
        import jax, jax.numpy as jnp
        import numpy as np
        D = 128
        HQ = 16
        HKV = 4
        G = HQ // HKV
        K = 64
        V = 64
        E = 8
        TOPK = 2
        HID = 256
        CAP_FRAC = 0.125
        EPS = 1e-06

        def _rmsnorm(x, g):
            return x * jax.lax.rsqrt(jnp.mean(x * x, axis=-1, keepdims=True) + EPS) * g

        def _rotary_tables(t, dim):
            thetas = 10000.0 ** (-np.arange(0, dim, 2, dtype=np.float32) / dim)
            ticks = np.outer(np.arange(t, dtype=np.float32), thetas)
            ticks = np.tile(ticks, (1, 2))[None, :, None, :]
            return (jnp.asarray(np.cos(ticks)), jnp.asarray(np.sin(ticks)))

        def _neg_half(x):
            x1, x2 = jnp.split(x, 2, axis=-1)
            return jnp.concatenate([-x2, x1], axis=-1)

        def _attention(x, wq, wk, wv, wo):
            b, t, _ = x.shape
            q = (x @ wq).reshape(b, t, HQ, K)
            k = (x @ wk).reshape(b, t, HKV, K)
            v = (x @ wv).reshape(b, t, HKV, V)
            cos, sin = _rotary_tables(t, K)
            q = q * cos + _neg_half(q) * sin
            k = k * cos + _neg_half(k) * sin
            qg = q.reshape(b, t, G, HKV, K)
            scores = jnp.einsum('btghk,bThk->bghtT', qg, k)
            mask = jnp.tril(jnp.ones((t, t), bool))
            scores = jnp.where(mask, scores, -jnp.inf) / np.float32(np.sqrt(K))
            p = jax.nn.softmax(scores, axis=-1)
            out = jnp.einsum('bghtT,bThv->btghv', p, v).reshape(b, t, HQ * V)
            return out @ wo

        def _moe(x, router_w, router_b, w1, w2, w3):
            b, t, d = x.shape
            n = b * t
            xf = x.reshape(n, d)
            logits = xf @ router_w + router_b
            vals, idx = jax.lax.top_k(logits, TOPK)
            scores = jax.nn.softmax(vals, axis=-1)
            cap = int(np.floor(n * CAP_FRAC))
            oh = jax.nn.one_hot(idx, E, dtype=jnp.float32)
            pos = jnp.cumsum(jnp.cumsum(oh, axis=0), axis=1).astype(jnp.int32)
            emask = oh * (pos < cap)
            tmask = jnp.sum(emask, axis=-1)
            assign = jnp.einsum('tke,e->tk', emask, jnp.arange(E, dtype=jnp.float32)).astype(jnp.int32)
            m = jnp.max(assign, axis=-1)

            def ff(w1e, w2e, w3e):
                h = jax.nn.gelu(xf @ w2e * (xf @ w1e), approximate=False)
                return h @ w3e
            y_all = jax.vmap(ff)(w1, w2, w3)
            y = y_all[m, jnp.arange(n)]
            slot = jnp.where(tmask[..., None] > 0, y[:, None, :], xf[:, None, :])
            out = jnp.einsum('tkD,tk->tD', slot, scores)
            return out.reshape(b, t, d)
        key = jax.random.key(seed)
        ks = jax.random.split(key, 10)
        w = lambda k, shape: jax.random.normal(k, shape, jnp.float32) * 0.02
        return {'x': jax.random.normal(ks[0], (4, 64, D), jnp.float32), 'g1': jnp.ones((D,), jnp.float32), 'g2': jnp.ones((D,), jnp.float32), 'wq': w(ks[1], (D, HQ * K)), 'wk': w(ks[2], (D, HKV * K)), 'wv': w(ks[3], (D, HKV * V)), 'wo': w(ks[4], (HQ * V, D)), 'router_w': w(ks[5], (D, E)), 'router_b': jnp.zeros((E,), jnp.float32), 'w1': w(ks[6], (E, D, HID)), 'w2': w(ks[7], (E, D, HID)), 'w3': w(ks[8], (E, HID, D))}
    _L1_ffn_all = _L1_ffn_setup()
    _L1_ffn_in = {k: v for k, v in _L1_ffn_all.items() if k in ('g1', 'g2', 'wq', 'wk', 'wv', 'wo', 'router_w', 'router_b', 'w1', 'w2', 'w3')}
    del _L1_ffn_all
    return {'x': x, 'ctx_1024': ctx_1024, 'mask_SxS2_bk1': mask_SxS2_bk1, 'mask_BxS2_bf0': mask_BxS2_bf0, 'L0_attn_W_q': _L0_attn_in['W_q'], 'L0_attn_b_q': _L0_attn_in['b_q'], 'L0_attn_W_k': _L0_attn_in['W_k'], 'L0_attn_b_k': _L0_attn_in['b_k'], 'L0_attn_W_v': _L0_attn_in['W_v'], 'L0_attn_b_v': _L0_attn_in['b_v'], 'L0_attn_W_o': _L0_attn_in['W_o'], 'L0_attn_b_o': _L0_attn_in['b_o'], 'L0_xattn_Wq': _L0_xattn_in['Wq'], 'L0_xattn_bq': _L0_xattn_in['bq'], 'L0_xattn_Wk': _L0_xattn_in['Wk'], 'L0_xattn_bk': _L0_xattn_in['bk'], 'L0_xattn_Wv': _L0_xattn_in['Wv'], 'L0_xattn_bv': _L0_xattn_in['bv'], 'L0_xattn_Wo': _L0_xattn_in['Wo'], 'L0_xattn_bo': _L0_xattn_in['bo'], 'L0_ffn_Wg': _L0_ffn_in['Wg'], 'L0_ffn_W1': _L0_ffn_in['W1'], 'L0_ffn_b1': _L0_ffn_in['b1'], 'L0_ffn_W2': _L0_ffn_in['W2'], 'L0_ffn_b2': _L0_ffn_in['b2'], 'L1_attn_Wq': _L1_attn_in['Wq'], 'L1_attn_bq': _L1_attn_in['bq'], 'L1_attn_Wk': _L1_attn_in['Wk'], 'L1_attn_bk': _L1_attn_in['bk'], 'L1_attn_Wv': _L1_attn_in['Wv'], 'L1_attn_bv': _L1_attn_in['bv'], 'L1_attn_Wo': _L1_attn_in['Wo'], 'L1_attn_bo': _L1_attn_in['bo'], 'L1_attn_rel_k': _L1_attn_in['rel_k'], 'L1_attn_rel_v': _L1_attn_in['rel_v'], 'L1_xattn_Wq': _L1_xattn_in['Wq'], 'L1_xattn_bq': _L1_xattn_in['bq'], 'L1_xattn_Wk': _L1_xattn_in['Wk'], 'L1_xattn_bk': _L1_xattn_in['bk'], 'L1_xattn_Wv': _L1_xattn_in['Wv'], 'L1_xattn_bv': _L1_xattn_in['bv'], 'L1_xattn_Wo': _L1_xattn_in['Wo'], 'L1_xattn_bo': _L1_xattn_in['bo'], 'L1_ffn_g1': _L1_ffn_in['g1'], 'L1_ffn_g2': _L1_ffn_in['g2'], 'L1_ffn_wq': _L1_ffn_in['wq'], 'L1_ffn_wk': _L1_ffn_in['wk'], 'L1_ffn_wv': _L1_ffn_in['wv'], 'L1_ffn_wo': _L1_ffn_in['wo'], 'L1_ffn_router_w': _L1_ffn_in['router_w'], 'L1_ffn_router_b': _L1_ffn_in['router_b'], 'L1_ffn_w1': _L1_ffn_in['w1'], 'L1_ffn_w2': _L1_ffn_in['w2'], 'L1_ffn_w3': _L1_ffn_in['w3']}

def reference(x, ctx_1024, mask_SxS2_bk1, mask_BxS2_bf0, L0_attn_W_q, L0_attn_b_q, L0_attn_W_k, L0_attn_b_k, L0_attn_W_v, L0_attn_b_v, L0_attn_W_o, L0_attn_b_o, L0_xattn_Wq, L0_xattn_bq, L0_xattn_Wk, L0_xattn_bk, L0_xattn_Wv, L0_xattn_bv, L0_xattn_Wo, L0_xattn_bo, L0_ffn_Wg, L0_ffn_W1, L0_ffn_b1, L0_ffn_W2, L0_ffn_b2, L1_attn_Wq, L1_attn_bq, L1_attn_Wk, L1_attn_bk, L1_attn_Wv, L1_attn_bv, L1_attn_Wo, L1_attn_bo, L1_attn_rel_k, L1_attn_rel_v, L1_xattn_Wq, L1_xattn_bq, L1_xattn_Wk, L1_xattn_bk, L1_xattn_Wv, L1_xattn_bv, L1_xattn_Wo, L1_xattn_bo, L1_ffn_g1, L1_ffn_g2, L1_ffn_wq, L1_ffn_wk, L1_ffn_wv, L1_ffn_wo, L1_ffn_router_w, L1_ffn_router_b, L1_ffn_w1, L1_ffn_w2, L1_ffn_w3):
    import jax
    import jax.numpy as jnp

    def _L0_attn_ref(x, W_q, b_q, W_k, b_k, W_v, b_v, W_o, b_o):
        import jax, jax.numpy as jnp
        import numpy as np
        EPS = 1e-06
        N_HEADS = 16

        def _heads(t, B, N, H, Dk):
            return t.reshape(B, N, H, Dk).transpose(0, 2, 1, 3)
        B, N, Dm = x.shape
        H = N_HEADS
        Dk = Dm // H
        q = _heads(x @ W_q.T + b_q, B, N, H, Dk)
        k = _heads(x @ W_k.T + b_k, B, N, H, Dk)
        v = _heads(x @ W_v.T + b_v, B, N, H, Dk)
        dec = jnp.exp(-jnp.arange(N, dtype=jnp.float32) / N)[None, None, :, None]
        qf = jax.nn.relu(q) * dec
        kf = jax.nn.relu(k) * dec
        KV = jnp.einsum('bhnd,bhne->bhde', kf, v)
        Ksum = kf.sum(axis=2)
        denom = jnp.einsum('bhnd,bhd->bhn', qf, Ksum) + EPS
        out = jnp.einsum('bhnd,bhde->bhne', qf, KV) / denom[..., None]
        out = out.transpose(0, 2, 1, 3).reshape(B, N, Dm)
        return out @ W_o.T + b_o

    def _L0_xattn_ref(query, key, value, Wq, bq, Wk, bk, Wv, bv, Wo, bo, attn_mask, key_padding_mask):
        import jax, jax.numpy as jnp
        import numpy as np
        B, T, D, H = (2, 256, 128, 16)
        DK = D // H
        SCALE = 1.0 / float(np.sqrt(DK))
        Bq, Tq, _ = query.shape
        Tk = key.shape[1]
        q = (query @ Wq.T + bq).reshape(Bq, Tq, H, DK)
        k = (key @ Wk.T + bk).reshape(Bq, Tk, H, DK)
        v = (value @ Wv.T + bv).reshape(Bq, Tk, H, DK)
        scores = jnp.einsum('bqhd,bkhd->bhqk', q, k) * jnp.float32(SCALE)
        neg_inf = jnp.float32(-jnp.inf)
        scores = jnp.where(attn_mask[None, None, :, :], neg_inf, scores)
        scores = jnp.where(key_padding_mask[:, None, None, :], neg_inf, scores)
        attn = jax.nn.softmax(scores, axis=-1)
        out = jnp.einsum('bhqk,bkhd->bqhd', attn, v).reshape(Bq, Tq, D)
        return out @ Wo.T + bo

    def _L0_ffn_ref(x, Wg, W1, b1, W2, b2):
        import jax, jax.numpy as jnp
        import numpy as np
        DIM, HIDDEN, E = (128, 512, 8)
        B, L = (2, 256)
        gate_logits = jnp.einsum('bld,ed->ble', x, Wg)
        top1 = jnp.argmax(gate_logits, axis=-1)
        out = jnp.zeros_like(x)
        for e in range(E):
            mask = (top1 == e)[..., None]
            h = jax.nn.gelu(jnp.einsum('bld,dh->blh', x, W1[e]) + b1[e], approximate=False)
            y = jnp.einsum('blh,hd->bld', h, W2[e]) + b2[e]
            out = jnp.where(mask, y, out)
        return out

    def _L1_attn_ref(hidden_states, Wq, bq, Wk, bk, Wv, bv, Wo, bo, rel_k, rel_v):
        import jax, jax.numpy as jnp
        import numpy as np
        NUM_HEADS = 16
        MAX_REL = 128

        def _rel_table_lookup(table, q_len, k_len):
            dist = jnp.arange(q_len)[:, None] - jnp.arange(k_len)[None, :]
            idx = jnp.clip(dist, -MAX_REL, MAX_REL) + MAX_REL
            return table[idx]
        B, T, E = hidden_states.shape
        H = NUM_HEADS
        D = E // H
        scaling = jnp.sqrt(jnp.float32(D))
        q = hidden_states @ Wq.T + bq
        k = hidden_states @ Wk.T + bk
        v = hidden_states @ Wv.T + bv
        q_head = q.reshape(B, T, H, D).transpose(0, 2, 1, 3)
        k_head = k.reshape(B, T, H, D).transpose(0, 2, 1, 3)
        v_head = v.reshape(B, T, H, D).transpose(0, 2, 1, 3)
        score_1 = jnp.einsum('bhqd,bhkd->bhqk', q_head, k_head)
        rpk = _rel_table_lookup(rel_k, T, T)
        q_resh = q_head.reshape(B * H, T, D).transpose(1, 0, 2)
        score_2 = jnp.einsum('qmd,qkd->qmk', q_resh, rpk)
        score_2 = score_2.reshape(T, H, B, T).transpose(2, 1, 0, 3)
        scores = (score_1 + score_2) / scaling
        attn = jax.nn.softmax(scores, axis=-1)
        weight_1 = jnp.einsum('bhqk,bhkd->bhqd', attn, v_head)
        rpv = _rel_table_lookup(rel_v, T, T)
        se = attn.reshape(B * H, T, T).transpose(1, 0, 2)
        weight_2 = jnp.einsum('qmk,qkd->qmd', se, rpv)
        weight_2 = weight_2.reshape(T, H, B, D).transpose(2, 1, 0, 3)
        attn_out = (weight_1 + weight_2).transpose(0, 2, 1, 3).reshape(B, T, E)
        return attn_out @ Wo.T + bo

    def _L1_xattn_ref(query, key, value, Wq, bq, Wk, bk, Wv, bv, Wo, bo):
        import jax, jax.numpy as jnp
        import numpy as np
        NHEADS = 16
        B, Sq, D = query.shape
        Sk = key.shape[1]
        H = NHEADS
        hd = D // H
        q = (query @ Wq + bq).reshape(B, Sq, H, hd)
        k = (key @ Wk + bk).reshape(B, Sk, H, hd)
        v = (value @ Wv + bv).reshape(B, Sk, H, hd)
        score = jnp.einsum('bqhd,bkhd->bhqk', q, k)
        cmask = jnp.triu(jnp.ones((Sq, Sk), dtype=bool), k=1)
        score = jnp.where(cmask, -jnp.inf, score)
        scale = jnp.float32(1.0 / np.sqrt(Sk))
        att = jax.nn.softmax(score * scale, axis=-1)
        ret = jnp.einsum('bhqk,bkhd->bqhd', att, v).reshape(B, Sq, D)
        return ret @ Wo + bo

    def _L1_ffn_ref(x, g1, g2, wq, wk, wv, wo, router_w, router_b, w1, w2, w3):
        import jax, jax.numpy as jnp
        import numpy as np
        D = 128
        HQ = 16
        HKV = 4
        G = HQ // HKV
        K = 64
        V = 64
        E = 8
        TOPK = 2
        HID = 256
        CAP_FRAC = 0.125
        EPS = 1e-06

        def _rmsnorm(x, g):
            return x * jax.lax.rsqrt(jnp.mean(x * x, axis=-1, keepdims=True) + EPS) * g

        def _rotary_tables(t, dim):
            thetas = 10000.0 ** (-np.arange(0, dim, 2, dtype=np.float32) / dim)
            ticks = np.outer(np.arange(t, dtype=np.float32), thetas)
            ticks = np.tile(ticks, (1, 2))[None, :, None, :]
            return (jnp.asarray(np.cos(ticks)), jnp.asarray(np.sin(ticks)))

        def _neg_half(x):
            x1, x2 = jnp.split(x, 2, axis=-1)
            return jnp.concatenate([-x2, x1], axis=-1)

        def _attention(x, wq, wk, wv, wo):
            b, t, _ = x.shape
            q = (x @ wq).reshape(b, t, HQ, K)
            k = (x @ wk).reshape(b, t, HKV, K)
            v = (x @ wv).reshape(b, t, HKV, V)
            cos, sin = _rotary_tables(t, K)
            q = q * cos + _neg_half(q) * sin
            k = k * cos + _neg_half(k) * sin
            qg = q.reshape(b, t, G, HKV, K)
            scores = jnp.einsum('btghk,bThk->bghtT', qg, k)
            mask = jnp.tril(jnp.ones((t, t), bool))
            scores = jnp.where(mask, scores, -jnp.inf) / np.float32(np.sqrt(K))
            p = jax.nn.softmax(scores, axis=-1)
            out = jnp.einsum('bghtT,bThv->btghv', p, v).reshape(b, t, HQ * V)
            return out @ wo

        def _moe(x, router_w, router_b, w1, w2, w3):
            b, t, d = x.shape
            n = b * t
            xf = x.reshape(n, d)
            logits = xf @ router_w + router_b
            vals, idx = jax.lax.top_k(logits, TOPK)
            scores = jax.nn.softmax(vals, axis=-1)
            cap = int(np.floor(n * CAP_FRAC))
            oh = jax.nn.one_hot(idx, E, dtype=jnp.float32)
            pos = jnp.cumsum(jnp.cumsum(oh, axis=0), axis=1).astype(jnp.int32)
            emask = oh * (pos < cap)
            tmask = jnp.sum(emask, axis=-1)
            assign = jnp.einsum('tke,e->tk', emask, jnp.arange(E, dtype=jnp.float32)).astype(jnp.int32)
            m = jnp.max(assign, axis=-1)

            def ff(w1e, w2e, w3e):
                h = jax.nn.gelu(xf @ w2e * (xf @ w1e), approximate=False)
                return h @ w3e
            y_all = jax.vmap(ff)(w1, w2, w3)
            y = y_all[m, jnp.arange(n)]
            slot = jnp.where(tmask[..., None] > 0, y[:, None, :], xf[:, None, :])
            out = jnp.einsum('tkD,tk->tD', slot, scores)
            return out.reshape(b, t, d)
        h = x + _attention(_rmsnorm(x, g1), wq, wk, wv, wo)
        return h + _moe(_rmsnorm(h, g2), router_w, router_b, w1, w2, w3)
    x = x + _L0_attn_ref(_layernorm(x, axis=-1), L0_attn_W_q, L0_attn_b_q, L0_attn_W_k, L0_attn_b_k, L0_attn_W_v, L0_attn_b_v, L0_attn_W_o, L0_attn_b_o)
    x = x + _L0_xattn_ref(_layernorm(x, axis=-1), ctx_1024, ctx_1024, L0_xattn_Wq, L0_xattn_bq, L0_xattn_Wk, L0_xattn_bk, L0_xattn_Wv, L0_xattn_bv, L0_xattn_Wo, L0_xattn_bo, mask_SxS2_bk1, mask_BxS2_bf0)
    x = x + _L0_ffn_ref(_layernorm(x, axis=-1), L0_ffn_Wg, L0_ffn_W1, L0_ffn_b1, L0_ffn_W2, L0_ffn_b2)
    x = x + _L1_attn_ref(_layernorm(x, axis=-1), L1_attn_Wq, L1_attn_bq, L1_attn_Wk, L1_attn_bk, L1_attn_Wv, L1_attn_bv, L1_attn_Wo, L1_attn_bo, L1_attn_rel_k, L1_attn_rel_v)
    x = x + _L1_xattn_ref(_layernorm(x, axis=-1), ctx_1024, ctx_1024, L1_xattn_Wq, L1_xattn_bq, L1_xattn_Wk, L1_xattn_bk, L1_xattn_Wv, L1_xattn_bv, L1_xattn_Wo, L1_xattn_bo)
    x = x + _L1_ffn_ref(_layernorm(x, axis=-1), L1_ffn_g1, L1_ffn_g2, L1_ffn_wq, L1_ffn_wk, L1_ffn_wv, L1_ffn_wo, L1_ffn_router_w, L1_ffn_router_b, L1_ffn_w1, L1_ffn_w2, L1_ffn_w3)
    return x

_drawn_inputs = setup_inputs


def setup_inputs(seed=0):
    import zlib

    import numpy as np

    out = dict(_drawn_inputs(seed))
    spreads = {'L0_attn_b_q': (0.0, 0.512),
     'L0_attn_b_k': (0.0, 0.665),
     'L0_attn_b_v': (0.0, 0.1),
     'L0_attn_b_o': (0.0, 0.1),
     'L0_xattn_bq': (0.0, 0.8),
     'L0_xattn_bk': (0.0, 0.8),
     'L0_xattn_bv': (0.0, 0.1),
     'L0_xattn_bo': (0.0, 0.1),
     'L1_attn_bq': (0.0, 0.8),
     'L1_attn_bk': (0.0, 0.8),
     'L1_attn_bv': (0.0, 0.1),
     'L1_attn_bo': (0.0, 0.1),
     'L1_ffn_g1': (1.0, 0.6),
     'L1_ffn_g2': (1.0, 0.2),
     'L1_ffn_router_b': (0.0, 0.1)}
    factors = {'L0_attn_W_q': 3.131,
     'L0_attn_W_k': 3.252,
     'L0_attn_W_v': 2.706,
     'L0_xattn_Wq': 7.465,
     'L0_xattn_Wk': 8.0,
     'L1_attn_Wq': 8.0,
     'L1_attn_Wk': 8.0,
     'L1_attn_Wv': 3.02,
     'L1_attn_rel_k': 8.0,
     'L1_attn_rel_v': 6.201,
     'L1_xattn_bq': 4.895,
     'L1_xattn_bk': 8.0,
     'L1_ffn_wq': 8.0,
     'L1_ffn_wk': 8.0,
     'L1_ffn_w1': 8.0,
     'L1_ffn_w2': 8.0,
     'L1_ffn_w3': 8.0}
    for name, (base, spread) in spreads.items():
        noise = np.random.default_rng([zlib.crc32(name.encode()), seed]).standard_normal(out[name].shape)
        drawn = base * np.exp(spread * noise) if base else spread * noise
        out[name] = jnp.asarray(drawn.astype(out[name].dtype))
    for name, factor in factors.items():
        out[name] = (out[name] * factor).astype(out[name].dtype)
    return out
```

```python
from contextlib import ExitStack

import concourse.bass as bass
from concourse import mybir

ALU = mybir.AluOpType
ACT = mybir.ActivationFunctionType
AX = mybir.AxisListType
F32 = mybir.dt.float32
BF16 = mybir.dt.bfloat16

P = 128
B = 4
S = 512
NT = S // P
H = 16
DK = P // H
KS = 154
KP = 160
REP = 4
HALF = H // 2 * KP
NCH = HALF // P
NPER = KP // 32
VW = P + H
MASKED = -1e30
LN_EPS = 1e-5
ATT_EPS = 1e-6
RMS_EPS = 1e-6
E1, HID1 = 8, 512
E2, HID2 = 8, 256
CAP = B * S // 8
HQ, HKV, KD = 16, 4, 64
NG = HQ // HKV
NU = S // DK
RELW = NU - 1 + S
RVS = S - P + S
SOFT = 1.0 / DK ** 0.5

COLB = ["A_bq", "B_bq", "B_bk", "D_bq", "D_bk", "E_bq", "E_bk"]
ROWB = ["A_bk", "A_bv", "A_bo", "B_bv", "B_bo", "D_bv", "D_bo", "E_bv", "E_bo", "F_g1", "F_g2", "G_rb", "rank", "index"]
SQW = ["A_q", "A_k", "A_v", "A_o", "B_q", "B_k", "B_v", "B_o", "D_q", "D_k", "D_v", "D_o", "E_q", "E_k", "E_v", "E_o"]
SQC = ["ident", "block", "mask_i", "tri", "ones", "causal"]


class Chain:

    def __init__(self, eng, sem, per_turn):
        self.eng, self.sem, self.per_turn = eng, sem, per_turn

    def turn(self, index):
        self.base, self.n = index * self.per_turn, 0

    def __call__(self, ins):
        self.n += 1
        ins.then_inc(self.sem, 1)
        self.eng.wait_ge(self.sem, self.base + self.n)

    def end(self):
        assert self.n == self.per_turn, (self.n, self.per_turn)


def decoder(nc, t, out, last="G"):
    stages = "ABCDEFG"[: "ABCDEFG".index(last) + 1]
    NX3 = len(stages) - 4
    ctx = ExitStack()
    with ctx:
        def sb(name, shape, dt=F32):
            return ctx.enter_context(nc.sbuf_tensor(name, shape, dt))

        def sem(name):
            return ctx.enter_context(nc.semaphore(name))

        ps = ctx.enter_context(nc.psum_tensor("ps", [P, 8, 512], F32))

        sqw = sb("sqw", [P, len(SQW), P])
        w = {n: sqw[:, i, :] for i, n in enumerate(SQW)}
        sqc = sb("sqc", [P, len(SQC), P])
        c = {n: sqc[:, i, :] for i, n in enumerate(SQC)}
        colb = sb("colb", [P, len(COLB) + E1 * HID1 // P])
        rowb = sb("rowb", [P, len(ROWB), P])
        row = {n: rowb[:, i, :] for i, n in enumerate(ROWB)}
        identb = sb("identb", [P, P], BF16)
        causal = sb("causal", [P, P], BF16)
        dec_row = sb("dec_row", [P, S])
        dec_col = sb("dec_col", [P, NT])
        vmask = sb("vmask", [P, NPER, P + 96])
        rmask = sb("rmask", [P, P + 64])
        xmask = sb("xmask", [P, NT, REP * KP], BF16)
        amask = sb("amask", [P, NT, KP], BF16)
        kmask = sb("kmask", [P, B, KP], BF16)
        rk = sb("rk", [P, RELW])
        rv = sb("rv", [P, RVS * DK])
        cwg = sb("cwg", [P, E1])
        cw1 = sb("cw1", [P, E1, HID1])
        cw2 = sb("cw2", [P, E1 * HID1 // P, P])
        cb2 = sb("cb2", [P, P])
        fwq = sb("fwq", [P, 2, HQ * KD])
        fwk = sb("fwk", [P, 2, HKV * KD])
        fwv = sb("fwv", [P, HKV * KD])
        fwo = sb("fwo", [P, HQ * KD // P, P])
        rot = sb("rot", [P, 4, S])
        gwr = sb("gwr", [P, E2])
        gw1 = sb("gw1", [P, E2, HID2])
        gw2 = sb("gw2", [P, E2, HID2])
        gw3 = sb("gw3", [P, E2 * HID2 // P, P])

        x = sb("x", [P, NT, P])
        xn = sb("xn", [P, NT, P])
        xnT = sb("xnT", [P, S])
        stats = sb("stats", [P, NT, 6])
        mv = sb("mv", [P, NT, 2])
        var = sb("var", [P, NT])
        root = sb("root", [P, NT])
        spare = sb("spare", [P, 1])
        rstd = sb("rstd", [P, NT])
        aoT = sb("aoT", [P, S])
        q_t = sb("q_t", [P, S])
        tmp = sb("tmp", [P, S])
        ctxT = sb("ctxT", [P, 2, KP])
        onehot = sb("onehot", [P, NT, P])
        ohsum = sb("ohsum", [P, 2 * E2])

        ARENA = 11296
        arena = sb("arena", [P, ARENA])
        used = [0]

        def cut(n):
            used[0] += n
            assert used[0] <= ARENA, used[0]
            return arena[:, used[0] - n:used[0]]

        amask_in, kmask_in = (cut(NT * KS).bitcast(mybir.dt.int32).rearrange("p (t k) -> p t k", k=KS) for _ in range(2))

        xmask_in = cut(NT * KP).rearrange("p (t k) -> p t k", k=KP)

        s_const = sem("s_const")
        s_prep = sem("s_prep")
        s_zero = sem("s_zero")
        SH = [{n: sem(f"s_{n}{i}") for n in ("x", "ctx", "xn", "var", "root", "tr", "xT", "ch", "wo")} for i in range(2)]
        s_xout = sem("s_xout")
        s_store = sem("s_store")
        NLN = (4, NX3)
        NNORM = (4, [0, 1, 3, 4][NX3])
        NWO = (2, 1 + (NX3 > 0))
        DH = dict(A=(0, 0), B=(0, 1), C=(0, 2), D=(0, 3), E=(1, 0), F=(1, 1), G=(1, 2))

        s_aq, s_akv, s_aqr, s_akvr, s_akvp, s_abd, s_aout, s_aao = map(sem, (
            "s_aq", "s_akv", "s_aqr", "s_akvr", "s_akvp", "s_abd", "s_aout", "s_aao"))
        XA = {}
        for k in "BE":
            XA[k] = {n: sem(f"s_{k}_{n}") for n in (
                "kv", "kt", "vrep", "kbd", "vs", "qp", "qt", "mask", "sc", "sub", "exp", "pt", "ptc", "pv", "o", "aT", "aTc")}

        NXH = 2 * NT

        def arena_A():
            used[0] = 0
            return dict(qf=cut(S), kf=cut(S), v1=cut(NT * 2 * P), bd=cut(2 * P), den=cut(S))
        TA = arena_A()

        def pe_transpose(pe, b, k, src=xn):
            ph, g = DH[k]
            s = SH[ph]
            pe.wait_ge(s["xn"], b * (NLN[ph] * NT) + (g + 1) * NT)
            for i in range(NT):
                ins = nc.tensor.transpose(ps[:, 0, i * P:(i + 1) * P], src[:, i, :], c["ident"])
            ins.then_inc(s["tr"], 1)
            pe.wait_ge(s["xT"], b * NLN[ph] + g + 1)

        def act_transpose(act, b, k):
            ph, g = DH[k]
            act.wait_ge(SH[ph]["tr"], b * NLN[ph] + g + 1)
            nc.scalar.copy(xnT[:, :], ps[:, 0, :]).then_inc(SH[ph]["xT"], 1)

        def dve_norm(dve, ch, b, k, keep=None):
            ph, g = DH[k]
            s = SH[ph]
            for i in range(NT):
                ins = nc.vector.bn_stats(stats[:, i, :], x[:, i, :])
            ch(ins)
            nc.vector.memset(spare[:, :], 0.0)
            for i in range(NT):
                ins = nc.vector.bn_aggr(mv[:, i, :], stats[:, i, :])
            ch(ins)
            nc.vector.tensor_scalar(var[:, :], mv[:, :, 1], LN_EPS, None, ALU.add).then_inc(s["var"], 1)
            dve.wait_ge(s["root"], b * NNORM[ph] + g + 1)
            ch(nc.vector.reciprocal(rstd[:, :], root[:, :]))
            for i in range(NT):
                ins = nc.vector.tensor_scalar(xn[:, i, :], x[:, i, :], mv[:, i, 0:1], rstd[:, i:i + 1],
                                        ALU.subtract, ALU.mult)
                if keep is None:
                    ins.then_inc(s["xn"], 1)
            if keep is not None:
                keep(ins)

        def act_root(act, b, k, second=0):
            ph, g = DH[k]
            g += second + (k == "G")
            act.wait_ge(SH[ph]["var"], b * NNORM[ph] + g + 1)
            nc.scalar.activation(root[:, :], var[:, :], ACT.Sqrt).then_inc(SH[ph]["root"], 1)

        def pe_project(pe, b, ph, g, wo):
            for i in range(NT):
                ins = nc.tensor.matmul(ps[:, 7, i * P:(i + 1) * P], aoT[:, i * P:(i + 1) * P], wo,
                                       start=True, stop=True)
            ins.then_inc(SH[ph]["wo"], 1)

        def dve_residual(dve, ch, b, ph, g, bo):
            dve.wait_ge(SH[ph]["wo"], b * NWO[ph] + g + 1)
            ch(nc.vector.tensor_tensor(tmp[:, :].rearrange("p (a n) -> p a n", a=NT),
                                       ps[:, 7, :].rearrange("p (a n) -> p a n", a=NT),
                                       bo.unsqueeze(1).to_broadcast([P, NT, P]), ALU.add))
            ch(nc.vector.tensor_tensor(x[:, :, :], x[:, :, :],
                                       tmp[:, :].rearrange("p (a n) -> p a n", a=NT), ALU.add))

        def pe_A(pe, b):
            pe_transpose(pe, b, "A")
            nc.tensor.matmul(ps[:, 1, :], w["A_q"], xnT[:, :], start=True, stop=True).then_inc(s_aq, 1)
            for i in range(NT):
                o = ps[:, 2 + i // 2, (i % 2) * 256:(i % 2) * 256 + 256]
                nc.tensor.matmul(o, xnT[:, i * P:(i + 1) * P], sqw[:, 1:3, :].rearrange("p a n -> p (a n)"),
                                 start=True, stop=True).then_inc(s_akv, 1)
            pe.wait_ge(s_akvr, b * NT + NT)
            for i in range(NT):
                ins = nc.tensor.matmul(ps[:, 4, 0:256], TA["kf"][:, i * P:(i + 1) * P],
                                       TA["v1"][:, i * 256:(i + 1) * 256], start=(i == 0), stop=(i == NT - 1))
            ins.then_inc(s_akvp, 1)
            pe.wait_ge(s_abd, b * 2 + 2)
            for j in range(2):
                nc.tensor.matmul(ps[:, 5 + j, :], TA["bd"][:, j * P:(j + 1) * P], TA["qf"],
                                 start=True, stop=True).then_inc(s_aout, 1)
            pe.wait_ge(s_aao, b + 1)
            pe_project(pe, b, 0, 0, w["A_o"])

        def act_A(act, b):
            act_root(act, b, "A")
            act_transpose(act, b, "A")
            act.wait_ge(s_aq, b + 1)
            nc.scalar.activation(q_t[:, :], ps[:, 1, :], ACT.Relu, bias=colb[:, 0:1]).then_inc(s_aqr, 1)

        def dve_A(dve, ch, b):
            dve_norm(dve, ch, b, "A")
            v1 = TA["v1"].rearrange("p (a n) -> p a n", a=NT)
            for i in range(NT):
                dve.wait_ge(s_akv, b * NT + 2 * (i // 2) + 2)
                o = ps[:, 2 + i // 2, (i % 2) * 256:(i % 2) * 256 + 256]
                ch(nc.vector.tensor_tensor(tmp[:, i * P:(i + 1) * P], o[:, 0:P], row["A_bk"], ALU.add))
                nc.vector.tensor_tensor(v1[:, i, 0:P], o[:, P:2 * P], row["A_bv"], ALU.add)
                nc.vector.memset(v1[:, i, P:2 * P], 1.0)
                nc.vector.tensor_scalar(TA["kf"][:, i * P:(i + 1) * P], tmp[:, i * P:(i + 1) * P], 0.0,
                                        dec_col[:, i:i + 1], ALU.max, ALU.mult).then_inc(s_akvr, 1)
            dve.wait_ge(s_aqr, b + 1)
            nc.vector.tensor_tensor(TA["qf"], q_t[:, :], dec_row[:, :], ALU.mult).then_inc(s_abd, 1)
            dve.wait_ge(s_akvp, b + 1)
            nc.vector.tensor_tensor(TA["bd"].rearrange("p (a n) -> p a n", a=2),
                                    ps[:, 4, 0:256].rearrange("p (a n) -> p a n", a=2),
                                    c["block"].unsqueeze(1).to_broadcast([P, 2, P]), ALU.mult).then_inc(s_abd, 1)
            dve.wait_ge(s_aout, b * 2 + 2)
            ch(nc.vector.tensor_scalar(TA["den"], ps[:, 6, :], ATT_EPS, None, ALU.add))
            ch(nc.vector.reciprocal(TA["den"], TA["den"]))
            nc.vector.tensor_tensor(aoT[:, :], ps[:, 5, :], TA["den"], ALU.mult).then_inc(s_aao, 1)
            dve_residual(dve, ch, b, 0, 0, row["A_bo"])

        used[0] = 0
        TX = dict(kt=cut(KP), kbd=cut(H * KP), vs=cut(2 * NCH * VW), d0=cut(HALF), d1=cut(HALF),
                  pt=cut(HALF), bmask=cut(NT * REP * KP // 2), m=cut(2 * 8), r=cut(2 * 8), g=cut(2 * 8), ao=cut(S))
        TX["vrep"] = TX["d1"][:, 0:NPER * P]
        bmask = TX["bmask"].bitcast(BF16).rearrange("p (t n) -> p t n", t=NT)
        vs = TX["vs"].rearrange("p (c n) -> p c n", c=2 * NCH)

        def pe_X(pe, b, k):
            s = XA[k]
            pe.wait_ge(SH[DH[k][0]]["ctx"], b * 32 + 32)
            flat = ctxT[:, :, :].rearrange("p a n -> p (a n)")
            nc.tensor.matmul(ps[:, 1, 0:KP], w[k + "_k"], flat[:, 0:KP], start=True, stop=True).then_inc(s["kv"], 1)
            for j in range(NPER):
                o = ps[:, 2 + j // 4, (j % 4) * P:(j % 4 + 1) * P]
                ins = nc.tensor.matmul(o, flat[:, j * P % KP:j * P % KP + P], w[k + "_v"], start=True, stop=True)
            ins.then_inc(s["kv"], 1)
            pe_transpose(pe, b, k)
            nc.tensor.matmul(ps[:, 4, :], w[k + "_q"], xnT[:, :], start=True, stop=True).then_inc(s["qp"], 1)
            mask = bmask if k == "B" else xmask
            pe.wait_ge(s["kbd"], b + 1)
            pe.wait_ge(s["vs"], b + 1)
            pe.wait_ge(s["qt"], b + 1)
            if k == "B":
                pe.wait_ge(s["mask"], b + 1)

            rounds = [(0, 4), (4, 8), (8, NCH)]

            def scores(n, first, last):
                i, half, bank = n // 2, n % 2, 3 * (n % 2)
                for j in range(first, last + 1):
                    at, width = j * 512, min(512, HALF - j * 512)
                    nc.tensor.matmul(ps[:, bank + j, 0:width], q_t[:, i * P:(i + 1) * P],
                                     TX["kbd"][:, half * HALF + at:half * HALF + at + width], start=True, stop=False)
                    ins = nc.tensor.matmul(ps[:, bank + j, 0:width], identb[:, :],
                                           mask[:, i, at % KP:at % KP + width], start=False, stop=True)
                if last == 2:
                    ins.then_inc(s["sc"], 1)

            def flip(n, r):
                c0, c1 = rounds[r]
                m = 3 * n + r
                if m >= 2:
                    pe.wait_ge(s["ptc"], b * 3 * NXH + m - 1)
                for cc in range(c0, c1):
                    ins = nc.tensor.transpose(ps[:, 6 + m % 2, (cc - c0) * P:(cc - c0 + 1) * P],
                                              TX["d%d" % (n % 2)][:, cc * P:(cc + 1) * P], c["ident"])
                ins.then_inc(s["pt"], 1)

            scores(0, 0, 2)
            scores(1, 0, 2)
            for n in range(NXH):
                half, bank = n % 2, 3 * (n % 2)
                pe.wait_ge(s["exp"], b * NXH + n + 1)
                flip(n, 0)
                flip(n, 1)
                if n + 2 < NXH:
                    scores(n + 2, 0, 1)
                flip(n, 2)
                for r, (c0, c1) in enumerate(rounds):
                    pe.wait_ge(s["ptc"], b * 3 * NXH + 3 * n + r + 1)
                    for cc in range(c0, c1):
                        ins = nc.tensor.matmul(ps[:, bank + 2, 256:256 + VW], TX["pt"][:, cc * P:(cc + 1) * P],
                                               vs[:, half * NCH + cc, :], start=(cc == 0), stop=(cc == NCH - 1))
                ins.then_inc(s["pv"], 1)
                if n + 2 < NXH:
                    pe.wait_ge(s["o"], b * NXH + n + 1)
                    scores(n + 2, 2, 2)
            pe.wait_ge(s["o"], b * NXH + NXH)
            for i in range(NT):
                ins = nc.tensor.transpose(ps[:, 0, i * P:(i + 1) * P], TX["ao"][:, i * P:(i + 1) * P], c["ident"])
            ins.then_inc(s["aT"], 1)
            pe.wait_ge(s["aTc"], b + 1)
            pe_project(pe, b, DH[k][0], 1, w[k + "_o"])

        def act_X(act, b, k):
            s = XA[k]
            qb, kb = COLB.index(k + "_bq"), COLB.index(k + "_bk")
            act.wait_ge(s["kv"], b * 2 + 1)
            nc.scalar.activation(TX["kt"], ps[:, 1, 0:KP], ACT.Identity, bias=colb[:, kb:kb + 1]).then_inc(s["kt"], 1)
            act_root(act, b, k)
            act_transpose(act, b, k)
            act.wait_ge(s["qp"], b + 1)
            nc.scalar.activation(q_t[:, :], ps[:, 4, :], ACT.Identity, bias=colb[:, qb:qb + 1]).then_inc(s["qt"], 1)
            scale = SOFT if k == "B" else 1.0 / KS ** 0.5

            def exps(n):
                act.wait_ge(s["sub"], b * NXH + n + 1)
                d = TX["d%d" % (n % 2)]
                nc.scalar.activation(d, d, ACT.Exp, scale=scale).then_inc(s["exp"], 1)

            def copy(n, r):
                c0, c1 = [(0, 4), (4, 8), (8, NCH)][r]
                m = 3 * n + r
                if r == 0 and n >= 1:
                    act.wait_ge(s["pv"], b * NXH + n)
                act.wait_ge(s["pt"], b * 3 * NXH + m + 1)
                nc.scalar.copy(TX["pt"][:, c0 * P:c1 * P], ps[:, 6 + m % 2, 0:(c1 - c0) * P]).then_inc(s["ptc"], 1)

            exps(0)
            for n in range(NXH):
                copy(n, 0)
                copy(n, 1)
                if n + 1 < NXH:
                    exps(n + 1)
                copy(n, 2)
            act.wait_ge(s["aT"], b + 1)
            nc.scalar.copy(aoT[:, :], ps[:, 0, :]).then_inc(s["aTc"], 1)

        def dve_X(dve, ch, b, k):
            s = XA[k]
            dve_norm(dve, ch, b, k)
            if k == "B":
                km = kmask[:, bass.ds(b, 1), :].to_broadcast([P, NT, KP])
                for r in range(REP):
                    ins = nc.vector.tensor_tensor(bmask[:, :, r * KP:(r + 1) * KP], amask[:, :, :], km, ALU.min)
                ins.then_inc(s["mask"], 1)
            dve.wait_ge(s["kv"], b * 2 + 2)
            nc.vector.tensor_tensor(TX["vrep"].rearrange("p (a n) -> p a n", a=NPER),
                                    ps[:, 2:4, :].rearrange("p a n -> p (a n)")[:, 0:NPER * P]
                                    .rearrange("p (a n) -> p a n", a=NPER),
                                    row[k + "_bv"].unsqueeze(1).to_broadcast([P, NPER, P]), ALU.add).then_inc(s["vrep"], 1)

            def shift(n):
                bank = 3 * (n % 2)
                sc = ps[:, bank:bank + 3, :].rearrange("p a n -> p (a n)")[:, 0:HALF].rearrange("p (h k) -> p h k", h=8)
                m = TX["m"][:, 8 * (n % 2):8 * (n % 2) + 8]
                dve.wait_ge(s["sc"], b * NXH + n + 1)
                ch(nc.vector.tensor_reduce(m, sc, AX.X, ALU.max))
                if n >= 2:
                    dve.wait_ge(s["pt"], b * 3 * NXH + 3 * (n - 1))
                nc.vector.tensor_tensor(TX["d%d" % (n % 2)].rearrange("p (h k) -> p h k", h=8), sc,
                                        m.unsqueeze(2).to_broadcast([P, 8, KP]), ALU.subtract).then_inc(s["sub"], 1)
                gg = TX["g"][:, 8 * (n % 2):8 * (n % 2) + 8]
                rr = TX["r"][:, 8 * (n % 2):8 * (n % 2) + 8]
                ch(nc.vector.tensor_scalar(gg, m, MASKED / 2, None, ALU.is_gt))
                ch(nc.vector.reciprocal(rr, gg))
                ch(nc.vector.tensor_tensor(gg, gg, rr, ALU.mult))

            def normalise(n):
                i, half, bank = n // 2, n % 2, 3 * (n % 2)
                o = ps[:, bank + 2, 256:256 + VW]
                gg = TX["g"][:, 8 * (n % 2):8 * (n % 2) + 8]
                rr = TX["r"][:, 8 * (n % 2):8 * (n % 2) + 8]
                dve.wait_ge(s["pv"], b * NXH + n + 1)
                ch(nc.vector.reciprocal(rr, o[:, P + 8 * half:P + 8 * half + 8]))
                ch(nc.vector.tensor_tensor(rr, rr, gg, ALU.mult))
                nc.vector.tensor_tensor(
                    TX["ao"][:, i * P + half * 64:i * P + half * 64 + 64].rearrange("p (h e) -> p h e", h=8),
                    o[:, half * 64:half * 64 + 64].rearrange("p (h e) -> p h e", h=8),
                    rr.unsqueeze(2).to_broadcast([P, 8, DK]), ALU.mult).then_inc(s["o"], 1)

            for n in range(NXH + 1):
                if n < NXH:
                    shift(n)
                if n >= 1:
                    normalise(n - 1)
            dve_residual(dve, ch, b, DH[k][0], 1, row[k + "_bo"])

        def pool_X(pool, b, k):
            s = XA[k]
            pool.wait_ge(s["kt"], b + 1)
            nc.gpsimd.tensor_tensor(TX["kbd"].rearrange("p (h k) -> p h k", h=H),
                                    TX["kt"].unsqueeze(1).to_broadcast([P, H, KP]),
                                    c["block"].rearrange("p (h e) -> p h e", h=H)[:, :, 0:1].to_broadcast([P, H, KP]),
                                    ALU.mult).then_inc(s["kbd"], 1)
            pool.wait_ge(s["vrep"], b + 1)
            for j in range(2 * NCH // NPER):
                ins = nc.gpsimd.tensor_tensor(vs[:, j * NPER:(j + 1) * NPER, 0:P],
                                              TX["vrep"].rearrange("p (a n) -> p a n", a=NPER),
                                              vmask[:, :, 96 - 32 * j:96 - 32 * j + P], ALU.mult)
                ins = nc.gpsimd.tensor_copy(vs[:, j * NPER:(j + 1) * NPER, P:VW],
                                            vmask[:, :, 96 - 32 * j:96 - 32 * j + P]
                                            .rearrange("p a (h e) -> p a h e", h=H)[:, :, :, 0])
            ins.then_inc(s["vs"], 1)

        def bc(a, *shape):
            return a.to_broadcast([P, *shape])

        gt = {n: sb("gt_" + n, [P, NT, E1]) for n in ("logit", "eq", "oh1", "oh2", "sel", "pos", "junk")}
        gs = {n: sb("gs_" + n, [P, NT]) for n in ("m1", "m2", "top", "e2", "s1", "s2", "t1", "t2", "a1", "a2", "cy", "cz")}

        def dve_first(ch, logits, best, oh, done=None):
            ch(nc.vector.tensor_reduce(best[:, :], logits, AX.X, ALU.max))
            ch(nc.vector.tensor_tensor(gt["eq"][:, :, :], logits, bc(best[:, :].unsqueeze(2), NT, E1), ALU.is_ge))
            ch(nc.vector.tensor_tensor(gt["eq"][:, :, :], gt["eq"][:, :, :],
                                       bc(row["rank"][:, 0:E1].unsqueeze(1), NT, E1), ALU.mult))
            ch(nc.vector.tensor_reduce(gs["top"][:, :], gt["eq"][:, :, :], AX.X, ALU.max))
            (done or ch)(nc.vector.tensor_tensor(oh, gt["eq"][:, :, :], bc(gs["top"][:, :].unsqueeze(2), NT, E1), ALU.is_equal))

        SC = {n: sem("s_c_" + n) for n in ("gate", "oh", "ohT", "ohTc", "b2", "h", "hs", "y", "acc")}
        used[0] = 0
        TC = dict(h0=cut(4 * S), h1=cut(4 * S), ohT=cut(S))
        NC1 = HID1 // P

        def pe_C(pe, b):
            pe_transpose(pe, b, "C")
            for i in range(NT):
                ins = nc.tensor.matmul(ps[:, 1, i * E1:(i + 1) * E1], xnT[:, i * P:(i + 1) * P], cwg[:, :],
                                       start=True, stop=True)
            ins.then_inc(SC["gate"], 1)

            def hidden(e):
                for j in range(NC1):
                    m = e * NC1 + j
                    if m >= 2:
                        pe.wait_ge(SC["hs"], b * E1 * NC1 + m - 1)
                    nc.tensor.matmul(ps[:, 4 + m % 2, :], cw1[:, e, j * P:(j + 1) * P], xnT[:, :],
                                     start=True, stop=True).then_inc(SC["h"], 1)

            hidden(0)
            pe.wait_ge(SC["oh"], b + 1)
            for i in range(NT):
                ins = nc.tensor.transpose(ps[:, 2, i * P:(i + 1) * P], onehot[:, i, :], c["ident"])
            ins.then_inc(SC["ohT"], 1)
            pe.wait_ge(SC["ohTc"], b + 1)
            for i in range(NT):
                ins = nc.tensor.matmul(ps[:, 3, i * P:(i + 1) * P], TC["ohT"][:, i * P:(i + 1) * P], cb2[:, :],
                                       start=True, stop=True)
            ins.then_inc(SC["b2"], 1)
            for e in range(E1):
                if e + 1 < E1:
                    hidden(e + 1)
                pe.wait_ge(SC["hs"], b * E1 * NC1 + (e + 1) * NC1)
                if e >= 2:
                    pe.wait_ge(SC["acc"], b * E1 + e - 1)
                for i in range(NT):
                    for j in range(NC1):
                        ins = nc.tensor.matmul(ps[:, 6 + e % 2, i * P:(i + 1) * P],
                                               TC["h%d" % (e % 2)][:, j * S + i * P:j * S + (i + 1) * P],
                                               cw2[:, e * NC1 + j, :], start=(j == 0), stop=(j == NC1 - 1))
                ins.then_inc(SC["y"], 1)

        def act_C(act, b):
            act_root(act, b, "C")
            act_transpose(act, b, "C")
            for e in range(E1):
                if e == 1:
                    act.wait_ge(SC["ohT"], b + 1)
                    nc.scalar.copy(TC["ohT"], ps[:, 2, :]).then_inc(SC["ohTc"], 1)
                if e >= 2:
                    act.wait_ge(SC["y"], b * E1 + e - 1)
                for j in range(NC1):
                    m = e * NC1 + j
                    act.wait_ge(SC["h"], b * E1 * NC1 + m + 1)
                    nc.scalar.activation(TC["h%d" % (e % 2)][:, j * S:(j + 1) * S], ps[:, 4 + m % 2, :], ACT.Gelu,
                                         bias=colb[:, len(COLB) + m:len(COLB) + m + 1]).then_inc(SC["hs"], 1)

        def dve_C(dve, ch, b):
            dve_norm(dve, ch, b, "C")
            dve.wait_ge(SC["gate"], b + 1)
            dve_first(ch, ps[:, 1, 0:NT * E1].rearrange("p (i e) -> p i e", i=NT), gs["m1"], onehot[:, :, 0:E1],
                      lambda ins: ins.then_inc(SC["oh"], 1))
            dve.wait_ge(SC["oh"], b + 1)
            dve.wait_ge(SC["b2"], b + 1)
            ch(nc.vector.tensor_tensor(x[:, :, :], ps[:, 3, :].rearrange("p (i n) -> p i n", i=NT), x[:, :, :], ALU.add))
            for e in range(E1):
                dve.wait_ge(SC["y"], b * E1 + e + 1)
                for i in range(NT):
                    ins = nc.vector.scalar_tensor_tensor(x[:, i, :], ps[:, 6 + e % 2, i * P:(i + 1) * P],
                                                         onehot[:, i, e:e + 1], x[:, i, :], ALU.mult, ALU.add)
                ins.then_inc(SC["acc"], 1)
                dve.wait_ge(SC["acc"], b * E1 + e + 1)

        SD = {n: sem("s_d_" + n) for n in ("kp", "kt", "qt", "v", "spill", "ld", "a", "sc", "max", "exp", "t", "ptc", "pv",
                                           "y", "yst", "ch", "ao", "at")}
        used[0] = 0
        RW = P + DK * DK
        TD = dict(kt=cut(S), v=cut(S), vr0=cut(NT * RW), vr1=cut(NT * RW), qi=cut(H * NU), nmax=cut(NU), rsum=cut(NU), y1=cut(S), y2=cut(S), ao2=cut(S),
                  **{n + str(i): cut(z) for n, z in (("a", P), ("p", S), ("pt", S), ("wt", P + 64), ("w", 16), ("r", 1))
                     for i in range(2)})
        ai = sb("ai", [P, 2, P])
        q_s, k_s, v_s, x_s, y1_s, y2_s = (nc.dram_tensor(n, (B, P, S), F32, kind="Internal").ap()
                                          for n in ("q_s", "k_s", "v_s", "x_s", "y1_s", "y2_s"))

        def turns_D(eng, body):
            for u in (0, 1):
                body(u, u, u)
            with eng.Fori(1, NU // 2 - 1) as v:
                for s in (0, 1):
                    body(2 * v + s, s, 2)
            for s in (0, 1):
                body(NU - 2 + s, s, 2)

        def pe_D0(pe, b):
            pe_transpose(pe, b, "D")
            nc.tensor.matmul(ps[:, 4, :], w["D_q"], xnT[:, :], start=True, stop=True).then_inc(SD["kp"], 1)
            nc.tensor.matmul(ps[:, 5, :], w["D_k"], xnT[:, :], start=True, stop=True).then_inc(SD["kp"], 1)
            for i in range(NT):
                ins = nc.tensor.matmul(ps[:, 6, i * P:(i + 1) * P], xnT[:, i * P:(i + 1) * P], w["D_v"],
                                       start=True, stop=True)
            ins.then_inc(SD["kp"], 1)

        def act_D0(act, b):
            act_root(act, b, "D")
            act_transpose(act, b, "D")
            kb = COLB.index("D_bk")
            act.wait_ge(SD["kp"], b * 3 + 2)
            nc.scalar.activation(TD["kt"], ps[:, 5, :], ACT.Identity, bias=colb[:, kb:kb + 1]).then_inc(SD["kt"], 1)

        def dve_D0(dve, ch, b):
            dve_norm(dve, ch, b, "D")
            qb = COLB.index("D_bq")
            dve.wait_ge(SD["kp"], b * 3 + 1)
            nc.vector.tensor_scalar(q_t[:, :], ps[:, 4, :], colb[:, qb:qb + 1], SOFT, ALU.add, ALU.mult)\
                .then_inc(SD["qt"], 1)
            dve.wait_ge(SD["kp"], b * 3 + 3)
            nc.vector.tensor_tensor(TD["v"].rearrange("p (i n) -> p i n", i=NT),
                                    ps[:, 6, :].rearrange("p (i n) -> p i n", i=NT),
                                    row["D_bv"].unsqueeze(1).to_broadcast([P, NT, P]), ALU.add).then_inc(SD["v"], 1)

        def sp_D0(sp, b):
            one = lambda a: a[bass.ds(b, 1)].rearrange("o p n -> p (o n)")
            sp.wait_ge(SD["qt"], b + 1)
            sp.dma_start(one(q_s), q_t[:, :]).then_inc(SD["spill"], 16)
            sp.dma_start(one(x_s), x[:, :, :].rearrange("p i n -> p (i n)")).then_inc(SD["spill"], 16)
            sp.wait_ge(SD["kt"], b + 1)
            sp.dma_start(one(k_s), TD["kt"]).then_inc(SD["spill"], 16)
            sp.wait_ge(SD["v"], b + 1)
            sp.dma_start(one(v_s), TD["v"]).then_inc(SD["spill"], 16)
            sp.wait_ge(SD["spill"], b * 64 + 64)

        LD = 16 * (2 + 2 * NT + DK)

        def sp_D(sp, b):
            one = lambda a: a[bass.ds(b, 1)].rearrange("o p n -> p (o n)")
            sp.dma_start(q_t[:, :], one(q_s)).then_inc(SD["ld"], 16)
            sp.dma_start(TD["kt"], one(k_s)).then_inc(SD["ld"], 16)
            for s in range(2):
                for i in range(NT):
                    o = (NT - 1 - i) * RW
                    sp.dma_start(TD["vr%d" % s][:, o:o + P], one(v_s)[:, i * P:(i + 1) * P]).then_inc(SD["ld"], 16)
            other = q_s.rearrange("c p q -> (c p) q").rearrange("(h b d) q -> b d h q", b=B, d=DK)
            for i in range(DK):
                sp.dma_start(TD["qi"][i * DK:(i + 1) * DK, :].rearrange("d (h u) -> d h u", h=H),
                             other[bass.ds(b, 1), :, :, i * NU:(i + 1) * NU].rearrange("o d h u -> (o d) h u"))\
                    .then_inc(SD["ld"], 16)
            sp.wait_ge(SD["y"], b * NU + NU)
            sp.dma_start(one(y1_s), TD["y1"]).then_inc(SD["yst"], 16)
            sp.dma_start(one(y2_s), TD["y2"]).then_inc(SD["yst"], 16)
            sp.wait_ge(SD["yst"], b * 32 + 32)

        def pe_D(pe, b):
            pe.wait_ge(SD["ld"], b * LD + LD)

            def scores(u, s):
                pe.wait_ge(SD["a"], b * (2 * NU) + u * 2 + 2)
                nc.tensor.matmul(ps[:, s, :], TD["a%d" % s], TD["kt"], start=True, stop=False)
                nc.tensor.matmul(ps[:, s, :], ai[:, s, :], rk[:, bass.ds(NU - 1 - u, S)],
                                 start=False, stop=True).then_inc(SD["sc"], 1)

            def flip(u, s):
                pe.wait_ge(SD["exp"], b * NU + u + 1)
                for j in range(NT):
                    ins = nc.tensor.transpose(ps[:, 2 + s, j * P:(j + 1) * P], TD["p%d" % s][:, j * P:(j + 1) * P],
                                              c["ident"])
                ins.then_inc(SD["t"], 1)

            def values(u, s, first=False):
                pe.wait_ge(SD["ptc"], b * NU + u + 1)
                if not first:
                    pe.wait_ge(SD["y"], b * NU + u - 1)
                for j in range(NT):
                    ins = nc.tensor.matmul(ps[:, 4 + s, 0:RW], TD["pt%d" % s][:, j * P:(j + 1) * P],
                                           TD["vr%d" % s][:, (NT - 1 - j) * RW:(NT - j) * RW],
                                           start=(j == 0), stop=(j == NT - 1))
                ins.then_inc(SD["pv"], 1)

            scores(0, 0)
            scores(1, 1)
            flip(0, 0)
            scores(2, 0)
            flip(1, 1)
            values(0, 0, True)
            scores(3, 1)
            flip(2, 0)
            values(1, 1, True)
            with pe.Fori(1, NU // 2 - 1) as v:
                for s in (1, 0):
                    u = 2 * v + 2 - s
                    scores(u + 1, 1 - s)
                    flip(u, s)
                    values(u - 1, 1 - s)
            flip(NU - 1, 1)
            values(NU - 2, 0)
            values(NU - 1, 1)

        def act_D(act, b):
            rvv = rv[:, :].rearrange("p (a o d) -> p o a d", o=NU, d=DK)

            def body(u, s, nth):
                act.wait_ge(SD["max"], b * NU + u + 1)
                nc.scalar.activation(TD["p%d" % s], ps[:, s, :], ACT.Exp, bias=TD["nmax"][:, bass.ds(u, 1)],
                                     accum_out=TD["rsum"][:, bass.ds(u, 1)]).then_inc(SD["exp"], 1)
                if nth == 2:
                    act.wait_ge(SD["pv"], b * NU + u - 1)
                w0 = rvv[:, bass.ds(u, 1), :, :]
                window = bass.AP(w0.tensor, w0.offset, [list(w0.ap[0]), [2 * NU * DK, NT], [NU * DK, DK], [1, DK]])
                nc.scalar.copy(TD["vr%d" % s].rearrange("p (j n) -> p j n", j=NT)[:, :, P:RW]
                               .rearrange("p j (i d) -> p j i d", i=DK), window)
                act.wait_ge(SD["t"], b * NU + u + 1)
                nc.scalar.copy(TD["pt%d" % s], ps[:, 2 + s, :]).then_inc(SD["ptc"], 1)

            turns_D(act, body)

        def dve_D(dve, b):
            chd = Chain(dve, SD["ch"], 2)
            y1 = TD["y1"].rearrange("p (d u) -> p d u", d=DK)
            y2 = TD["y2"].rearrange("p (d u) -> p d u", d=DK)

            def top(u, s):
                dve.wait_ge(SD["sc"], b * NU + u + 1)
                nc.vector.tensor_reduce(TD["nmax"][:, bass.ds(u, 1)], ps[:, s, :], AX.X, ALU.max, negate=True)\
                    .then_inc(SD["max"], 1)

            def rows(u, s):
                chd.turn(b * NU + u)
                o = ps[:, 4 + s, :]
                wt, wv = TD["wt%d" % s], TD["w%d" % s]
                dve.wait_ge(SD["pv"], b * NU + u + 1)
                nc.vector.reciprocal(TD["r%d" % s], TD["rsum"][:, bass.ds(u, 1)])
                chd(nc.vector.tensor_tensor(wt, o[:, 0:P + 64], rmask[:, :], ALU.mult))
                nc.vector.tensor_reduce(wv[:, 0:DK], wt[:, 0:P].rearrange("p (h e) -> p e h", h=H), AX.X, ALU.add)
                chd(nc.vector.tensor_reduce(wv[:, DK:16], wt[:, P:P + 64].rearrange("p (i d) -> p d i", i=DK), AX.X, ALU.add))
                nc.vector.tensor_scalar(y1[:, :, bass.ds(u, 1)].rearrange("p d o -> p (d o)"), wv[:, 0:DK],
                                        TD["r%d" % s], None, ALU.mult)
                nc.vector.tensor_scalar(y2[:, :, bass.ds(u, 1)].rearrange("p d o -> p (d o)"), wv[:, DK:16],
                                        TD["r%d" % s], None, ALU.mult).then_inc(SD["y"], 1)
                chd.end()

            top(0, 0)
            top(1, 1)
            top(2, 0)
            rows(0, 0)
            with dve.Fori(1, NU // 2 - 1) as v:
                for s in (1, 0):
                    u = 2 * v + 2 - s
                    top(u, s)
                    rows(u - 2, s)
            top(NU - 1, 1)
            rows(NU - 3, 1)
            rows(NU - 2, 0)
            rows(NU - 1, 1)

        def pool_D(pool, b):
            pool.wait_ge(SD["ld"], b * LD + LD)
            qu = q_t[:, :].rearrange("p (i u) -> p u i", i=DK)
            qi = TD["qi"].rearrange("p (h u) -> p h u", h=H)

            def spread(u, s, nth):
                if nth == 2:
                    pool.wait_ge(SD["sc"], b * NU + u - 1)
                nc.gpsimd.tensor_tensor(TD["a%d" % s].rearrange("p (h i) -> p h i", h=H),
                                        qu[:, bass.ds(u, 1), :].to_broadcast([P, H, DK]),
                                        c["block"].rearrange("p (h i) -> p h i", h=H), ALU.mult).then_inc(SD["a"], 1)
                nc.gpsimd.tensor_tensor(ai[0:64, s, :].rearrange("p (h i) -> p h i", h=H),
                                        qi[0:64, :, bass.ds(u, 1)].to_broadcast([64, H, DK]),
                                        c["mask_i"][0:64, :].rearrange("p (h i) -> p h i", h=H), ALU.mult)\
                    .then_inc(SD["a"], 1)

            turns_D(pool, spread)

        def sp_D1(sp, b):
            own = y1_s[bass.ds(b, 1)].rearrange("o (h i) (d u) -> (o h) d i u", i=DK, d=DK)
            other = y2_s.rearrange("c p n -> (c p) n").rearrange("(h z i) (d u) -> z h d i u", z=B, i=DK, d=DK)[bass.ds(b, 1)]
            other = other.rearrange("o h d i u -> (o h) d i u")
            for h in range(H):
                for dst, src in ((aoT[:, :], own), (TD["ao2"], other)):
                    sp.dma_start(dst[h * DK:(h + 1) * DK, :].rearrange("d (i u) -> d i u", i=DK),
                                 src[h:h + 1].rearrange("o d i u -> (o d) i u")).then_inc(SD["ao"], 16)

        def pe_D1(pe, b):
            pe.wait_ge(SD["at"], b + 1)
            pe_project(pe, b, 1, 0, w["D_o"])

        def dve_D1(dve, ch, b):
            dve.wait_ge(SD["ao"], b * (2 * H * 16) + 2 * H * 16)
            nc.vector.tensor_tensor(aoT[:, :], aoT[:, :], TD["ao2"], ALU.add).then_inc(SD["at"], 1)
            dve_residual(dve, ch, b, 1, 0, row["D_bo"])

        SF = {n: sem("s_f_" + n) for n in ("kp", "kt", "kr", "vp", "v", "qp", "qm", "qr", "sc", "max", "exp", "nrm", "t",
                                           "ptc", "pv", "ao", "wo")}
        used[0] = 0
        TF = dict(t0=cut(S), t1=cut(S), u0=cut(S), u1=cut(S), v=cut(NT * HKV * KD), nmax=cut(4), rsum=cut(4), rinv=cut(4),
                  **{f"{n}{i}": cut(S) for n in ("p", "pt") for i in range(2)}, **{f"q{i}": cut(S) for i in range(4)},
                  **{f"ao{i}": cut(S) for i in range(2)})
        krz = cut(HKV * S).rearrange("p (h s) -> p h s", h=HKV)
        yn = sb("yn", [P, NT, P])
        NTQ = HQ * KD // P

        def FS(n):
            return (0, 1, 6)[n % 3]

        def FQ(a, m):
            return (5, 6, 7, 0)[2 * a + m] if a < 2 else 5

        NUF = HQ * NT

        def dve_rms(dve, ch, b, g, src, dst, gamma):
            s = SH[1]
            ch(nc.vector.tensor_tensor(tmp[:, :].rearrange("p (i n) -> p i n", i=NT), src, src, ALU.mult))
            ch(nc.vector.tensor_reduce(mv[:, :, 0], tmp[:, :].rearrange("p (i n) -> p i n", i=NT), AX.X, ALU.add))
            nc.vector.tensor_scalar(var[:, :], mv[:, :, 0], 1.0 / P, RMS_EPS, ALU.mult, ALU.add).then_inc(s["var"], 1)
            dve.wait_ge(s["root"], b * NNORM[1] + g + 1)
            ch(nc.vector.reciprocal(rstd[:, :], root[:, :]))
            for i in range(NT):
                nc.vector.scalar_tensor_tensor(dst[:, i, :], src[:, i, :], rstd[:, i:i + 1], gamma,
                                               ALU.mult, ALU.mult).then_inc(s["xn"], 1)

        def pe_F(pe, b):
            pe_transpose(pe, b, "F", yn)
            for a in range(HKV * KD // P):
                for m in range(2):
                    nc.tensor.matmul(ps[:, 1 + 2 * a + m, :], fwk[:, m, a * P:(a + 1) * P], xnT[:, :],
                                     start=True, stop=True).then_inc(SF["kp"], 1)
            for i in range(NT):
                ins = nc.tensor.matmul(ps[:, 5 + i // 2, i % 2 * 256:i % 2 * 256 + 256], xnT[:, i * P:(i + 1) * P],
                                       fwv[:, :], start=True, stop=True)
            ins.then_inc(SF["vp"], 1)

            def queries(a, m):
                if a == 0:
                    pe.wait_ge(SF["v"], b + 1)
                elif a > 1:
                    pe.wait_ge(SF["qm"], b * 2 * NTQ + 2 * a + m)
                nc.tensor.matmul(ps[:, FQ(a, m), :], fwq[:, m, a * P:(a + 1) * P], xnT[:, :],
                                 start=True, stop=True).then_inc(SF["qp"], 1)

            def scores(n):
                h, i = n // NT, n % NT
                if i == 0:
                    pe.wait_ge(SF["qr"], b * NTQ + h // 2 + 1)
                wd = (i + 1) * P
                o = ps[:, FS(n), :]
                nc.tensor.matmul(o[:, 0:wd], TF["q%d" % (h // 2 % 4)][:, i * P:(i + 1) * P],
                                 krz[:, h % HKV, 0:wd], start=True, stop=False, skip_group_check=True)
                nc.tensor.matmul(o[:, i * P:wd], identb[:, :], causal[:, :], start=False, stop=True,
                                 skip_group_check=True).then_inc(SF["sc"], 1)

            def flip(n):
                i = n % NT
                pe.wait_ge(SF["nrm"], b * NUF + n + 1)
                for j in range(i + 1):
                    ins = nc.tensor.transpose(ps[:, 2 + n % 2, j * P:(j + 1) * P], TF["p%d" % (n % 2)][:, j * P:(j + 1) * P],
                                              c["ident"])
                ins.then_inc(SF["t"], 1)

            def values(n):
                h, i = n // NT, n % NT
                pe.wait_ge(SF["ptc"], b * NUF + n + 1)
                if n % (2 * NT) == 0 and n:
                    pe.wait_ge(SF["ao"], b * NTQ + h // 2)
                r0 = h % 2 * KD
                for j in range(i + 1):
                    v0 = j * HKV * KD + h % HKV * KD
                    ins = nc.tensor.matmul(ps[r0:r0 + KD, 4, i * P:(i + 1) * P], TF["v"][:, v0:v0 + KD],
                                           TF["pt%d" % (n % 2)][:, j * P:(j + 1) * P], start=(j == 0), stop=(j == i),
                                           skip_group_check=True)
                ins.then_inc(SF["pv"], 1)

            def project(a):
                pe.wait_ge(SF["ao"], b * NTQ + a + 1)
                for i in range(NT):
                    ins = nc.tensor.matmul(ps[:, 7, i * P:(i + 1) * P], TF["ao%d" % (a % 2)][:, i * P:(i + 1) * P],
                                           fwo[:, a, :], start=(a == 0 and i == 0), stop=(a == NTQ - 1),
                                           skip_group_check=True)
                ins.then_inc(SF["wo"], 1)

            for a in range(2):
                for m in range(2):
                    queries(a, m)
            pe.wait_ge(SF["kr"], b * 2 + 2)
            pe.wait_ge(SF["qm"], b * 2 * NTQ + 4)
            scores(0)
            scores(1)
            for n in range(NUF):
                if n + 2 < NUF:
                    scores(n + 2)
                a, r = n // (2 * NT), n % (2 * NT)
                if r in (2, 5) and a + 2 < NTQ:
                    queries(a + 2, r // 4)
                flip(n)
                if n >= 1:
                    values(n - 1)
                if r == 3 and a >= 1:
                    project(a - 1)
            values(NUF - 1)
            project(NTQ - 1)

        def act_F(act, b):
            act_root(act, b, "F")
            act_root(act, b, "F", 1)
            act_transpose(act, b, "F")

            def exps(n):
                wd = (n % NT + 1) * P
                act.wait_ge(SF["max"], b * NUF + n + 1)
                if n >= 2:
                    act.wait_ge(SF["t"], b * NUF + n - 1)
                nc.scalar.activation(TF["p%d" % (n % 2)][:, 0:wd], ps[:, FS(n), 0:wd], ACT.Exp,
                                     bias=TF["nmax"][:, n % 4:n % 4 + 1],
                                     accum_out=TF["rsum"][:, n % 4:n % 4 + 1]).then_inc(SF["exp"], 1)

            def copy(n):
                wd = (n % NT + 1) * P
                act.wait_ge(SF["t"], b * NUF + n + 1)
                if n >= 2:
                    act.wait_ge(SF["pv"], b * NUF + n - 1)
                nc.scalar.copy(TF["pt%d" % (n % 2)][:, 0:wd], ps[:, 2 + n % 2, 0:wd]).then_inc(SF["ptc"], 1)

            exps(0)
            for n in range(NUF):
                if n % (2 * NT) == 1 and n > 2 * NT:
                    gather(act, b, n // (2 * NT) - 1)
                if n + 1 < NUF:
                    exps(n + 1)
                copy(n)
            gather(act, b, NTQ - 1)

        def gather(act, b, a):
            act.wait_ge(SF["pv"], b * NUF + (a + 1) * 2 * NT)
            if a >= 2:
                act.wait_ge(SF["wo"], b * NTQ + a - 1)
            nc.scalar.copy(TF["ao%d" % (a % 2)], ps[:, 4, :]).then_inc(SF["ao"], 1)

        def dve_F(dve, ch, b):
            dve_norm(dve, ch, b, "F", ch)
            dve_rms(dve, ch, b, 2, xn[:, :, :], yn, row["F_g1"])
            for a in range(HKV * KD // P):
                dve.wait_ge(SF["kp"], b * 4 + 2 * a + 2)
                nc.vector.tensor_tensor(TF["t%d" % a], ps[:, 1 + 2 * a, :], rot[:, 2, :], ALU.mult)
                ch(nc.vector.tensor_tensor(TF["u%d" % a], ps[:, 2 + 2 * a, :], rot[:, 3, :], ALU.mult))
                for m in range(2):
                    r0 = m * KD
                    nc.vector.memset(krz[KD - r0:2 * KD - r0, 2 * a + m, :], 0.0)
                    ins = nc.vector.tensor_tensor(krz[r0:r0 + KD, 2 * a + m, :], TF["t%d" % a][r0:r0 + KD, :],
                                                  TF["u%d" % a][r0:r0 + KD, :], ALU.add)
                ins.then_inc(SF["kr"], 1)
            dve.wait_ge(SF["vp"], b + 1)
            nc.vector.tensor_copy(TF["v"], ps[:, 5:7, :].rearrange("p a n -> p (a n)")).then_inc(SF["v"], 1)

            def rotate(a, m):
                dve.wait_ge(SF["qp"], b * 2 * NTQ + 2 * a + m + 1)
                if a >= 2 and m == 0:
                    dve.wait_ge(SF["qr"], b * NTQ + a - 1)
                elif a < 2 and m == 0:
                    dve.wait_ge(SF["kr"], b * 2 + a + 1)
                nc.vector.tensor_tensor(TF["tu"[m] + str(a % 2)], ps[:, FQ(a, m), :], rot[:, m, :], ALU.mult)\
                    .then_inc(SF["qm"], 1)

            def top(n):
                wd = (n % NT + 1) * P
                dve.wait_ge(SF["sc"], b * NUF + n + 1)
                nc.vector.tensor_reduce(TF["nmax"][:, n % 4:n % 4 + 1], ps[:, FS(n), 0:wd], AX.X, ALU.max, negate=True)\
                    .then_inc(SF["max"], 1)

            def norm(n):
                wd = (n % NT + 1) * P
                k4 = slice(n % 4, n % 4 + 1)
                dve.wait_ge(SF["exp"], b * NUF + n + 1)
                ch(nc.vector.reciprocal(TF["rinv"][:, k4], TF["rsum"][:, k4]))
                nc.vector.tensor_scalar(TF["p%d" % (n % 2)][:, 0:wd], TF["p%d" % (n % 2)][:, 0:wd],
                                        TF["rinv"][:, k4], None, ALU.mult).then_inc(SF["nrm"], 1)

            for a in range(2):
                for m in range(2):
                    rotate(a, m)
            top(0)
            top(1)
            norm(0)
            for n in range(NUF):
                if n + 2 < NUF:
                    top(n + 2)
                a, r = n // (2 * NT), n % (2 * NT)
                if r in (2, 5) and a + 2 < NTQ:
                    rotate(a + 2, r // 4)
                if n + 1 < NUF:
                    norm(n + 1)
            dve.wait_ge(SF["wo"], b * NTQ + NTQ)
            ch(nc.vector.tensor_tensor(xn[:, :, :], ps[:, 7, :].rearrange("p (i n) -> p i n", i=NT), xn[:, :, :], ALU.add))
            ch(nc.vector.tensor_tensor(x[:, :, :], x[:, :, :], xn[:, :, :], ALU.add))

        def pool_F(pool, b):
            for a in range(NTQ):
                pool.wait_ge(SF["qm"], b * 2 * NTQ + 2 * a + 2)
                if a >= 4:
                    pool.wait_ge(SF["pv"], b * NUF + (a - 3) * 2 * NT)
                nc.gpsimd.tensor_tensor(TF["q%d" % (a % 4)], TF["t%d" % (a % 2)], TF["u%d" % (a % 2)], ALU.add)\
                    .then_inc(SF["qr"], 1)

        SG = {n: sem("s_g_" + n) for n in ("gate", "d", "e2", "pre", "cum", "h", "a", "p", "hs", "y", "acc")}
        used[0] = 0
        TG = dict(**{n + str(i): cut(S) for n in ("a", "p") for i in range(2)}, h0=cut(2 * S), h1=cut(2 * S),
                  oh=cut(NT * 2 * E2), pre=cut(NT * 2 * E2))
        NC2 = HID2 // P
        NM2 = E2 * NC2

        def pe_G(pe, b):
            pe_transpose(pe, b, "G", yn)
            for i in range(NT):
                ins = nc.tensor.matmul(ps[:, 1, i * E2:(i + 1) * E2], xnT[:, i * P:(i + 1) * P], gwr[:, :],
                                       start=True, stop=True)
            ins.then_inc(SG["gate"], 1)

            def hidden(e):
                for j in range(NC2):
                    m = e * NC2 + j
                    if m >= 2:
                        pe.wait_ge(SG["a"], b * NM2 + m - 1)
                    nc.tensor.matmul(ps[:, 2 + m % 2, :], gw2[:, e, j * P:(j + 1) * P], xnT[:, :],
                                     start=True, stop=True).then_inc(SG["h"], 1)
                    if m >= 2:
                        pe.wait_ge(SG["p"], b * NM2 + m - 1)
                    nc.tensor.matmul(ps[:, 4 + m % 2, :], gw1[:, e, j * P:(j + 1) * P], xnT[:, :],
                                     start=True, stop=True).then_inc(SG["h"], 1)

            hidden(0)
            pe.wait_ge(SG["pre"], b + 1)
            for i in range(NT):
                o = ps[:, 1, 64 + i * 2 * E2:64 + (i + 1) * 2 * E2]
                at = slice(i * 2 * E2, (i + 1) * 2 * E2)
                nc.tensor.matmul(o, c["tri"], TG["oh"][:, at], start=True, stop=False)
                ins = nc.tensor.matmul(o, c["ones"], TG["pre"][:, at], start=False, stop=True)
            ins.then_inc(SG["cum"], 1)
            for e in range(E2):
                if e + 1 < E2:
                    hidden(e + 1)
                pe.wait_ge(SG["hs"], b * NM2 + (e + 1) * NC2)
                if e >= 2:
                    pe.wait_ge(SG["acc"], b * E2 + e - 1)
                for i in range(NT):
                    for j in range(NC2):
                        ins = nc.tensor.matmul(ps[:, 6 + e % 2, i * P:(i + 1) * P],
                                               TG["h%d" % (e % 2)][:, j * S + i * P:j * S + (i + 1) * P],
                                               gw3[:, e * NC2 + j, :], start=(j == 0), stop=(j == NC2 - 1))
                ins.then_inc(SG["y"], 1)

        def act_G(act, b):
            act_root(act, b, "G")
            act_transpose(act, b, "G")

            def linear(m):
                act.wait_ge(SG["h"], b * 2 * NM2 + 2 * m + 1)
                if m >= 2:
                    act.wait_ge(SG["p"], b * NM2 + m - 1)
                nc.scalar.copy(TG["a%d" % (m % 2)], ps[:, 2 + m % 2, :]).then_inc(SG["a"], 1)

            linear(0)
            act.wait_ge(SG["d"], b + 1)
            nc.scalar.activation(gs["e2"][:, :], gs["t1"][:, :], ACT.Exp).then_inc(SG["e2"], 1)
            for m in range(NM2):
                if m + 1 < NM2:
                    linear(m + 1)
                e = m // NC2
                if m % NC2 == 0 and e >= 2:
                    act.wait_ge(SG["y"], b * E2 + e - 1)
                act.wait_ge(SG["p"], b * NM2 + m + 1)
                nc.scalar.activation(TG["h%d" % (e % 2)][:, m % NC2 * S:(m % NC2 + 1) * S], TG["p%d" % (m % 2)],
                                     ACT.Gelu).then_inc(SG["hs"], 1)

        def dve_G(dve, ch, b):
            V = nc.vector
            dve_rms(dve, ch, b, 3, xn[:, :, :], yn, row["F_g2"])
            dve.wait_ge(SG["gate"], b + 1)
            lg, oh1, oh2, pos, junk, sel = (gt[n][:, :, :] for n in ("logit", "oh1", "oh2", "pos", "junk", "sel"))
            S_ = {n: a[:, :] for n, a in gs.items()}
            wide = lambda a: a.unsqueeze(2).to_broadcast([P, NT, E2])
            ohk = TG["oh"].rearrange("p (i k e) -> p i k e", i=NT, k=2)
            pre = TG["pre"].rearrange("p (i n) -> p i n", i=NT)
            ch(V.tensor_tensor(lg, ps[:, 1, 0:NT * E2].rearrange("p (i e) -> p i e", i=NT),
                               row["G_rb"][:, 0:E2].unsqueeze(1).to_broadcast([P, NT, E2]), ALU.add))
            dve_first(ch, lg, gs["m1"], oh1)
            ch(V.tensor_scalar(junk, oh1, -3e38, None, ALU.mult))
            ch(V.tensor_tensor(junk, junk, lg, ALU.add))
            dve_first(ch, junk, gs["m2"], oh2)
            V.tensor_tensor(S_["t1"], S_["m2"], S_["m1"], ALU.subtract).then_inc(SG["d"], 1)
            V.tensor_copy(ohk[:, :, 0, :], oh1)
            ch(V.tensor_copy(ohk[:, :, 1, :], oh2))
            ch(V.tensor_copy(pre[:, 0, :], ohsum[:, :]))
            for i in range(NT):
                o = pre[:, i + 1, :] if i + 1 < NT else ohsum[:, :]
                ins = V.tensor_tensor(o, pre[:, i, :], ohk[:, i, :, :].rearrange("p k e -> p (k e)"), ALU.add)
                if i + 1 < NT:
                    ch(ins)
            ins.then_inc(SG["pre"], 1)

            def product(m):
                dve.wait_ge(SG["a"], b * NM2 + m + 1)
                dve.wait_ge(SG["h"], b * 2 * NM2 + 2 * m + 2)
                if m >= 2:
                    dve.wait_ge(SG["hs"], b * NM2 + m - 1)
                V.tensor_tensor(TG["p%d" % (m % 2)], ps[:, 4 + m % 2, :], TG["a%d" % (m % 2)], ALU.mult)\
                    .then_inc(SG["p"], 1)

            product(0)
            product(1)
            dve.wait_ge(SG["e2"], b + 1)
            ch(V.tensor_scalar(S_["t1"], S_["e2"], 1.0, None, ALU.add))
            ch(V.reciprocal(S_["s1"], S_["t1"]))
            ch(V.tensor_tensor(S_["s2"], S_["e2"], S_["s1"], ALU.mult))
            dve.wait_ge(SG["cum"], b + 1)
            cum = ps[:, 1, 64:64 + NT * 2 * E2].rearrange("p (i k e) -> p i k e", i=NT, k=2)
            ch(V.tensor_copy(pos, cum[:, :, 0, :]))
            ch(V.tensor_tensor(junk, pos, cum[:, :, 1, :], ALU.add))
            ch(V.tensor_scalar(pos, pos, float(CAP), None, ALU.is_lt))
            ch(V.tensor_tensor(oh1, oh1, pos, ALU.mult))
            ch(V.tensor_scalar(junk, junk, float(CAP), None, ALU.is_lt))
            ch(V.tensor_tensor(oh2, oh2, junk, ALU.mult))
            idx = row["index"][:, 0:E2].unsqueeze(1).to_broadcast([P, NT, E2])
            ch(V.tensor_reduce(S_["t1"], oh1, AX.X, ALU.add))
            ch(V.tensor_reduce(S_["t2"], oh2, AX.X, ALU.add))
            ch(V.tensor_tensor(oh1, oh1, idx, ALU.mult))
            ch(V.tensor_tensor(oh2, oh2, idx, ALU.mult))
            ch(V.tensor_reduce(S_["a1"], oh1, AX.X, ALU.add))
            ch(V.tensor_reduce(S_["a2"], oh2, AX.X, ALU.add))
            ch(V.tensor_tensor(S_["a1"], S_["a1"], S_["a2"], ALU.max))
            ch(V.tensor_tensor(S_["cy"], S_["s1"], S_["t1"], ALU.mult))
            ch(V.tensor_tensor(S_["a2"], S_["s2"], S_["t2"], ALU.mult))
            ch(V.tensor_tensor(S_["s1"], S_["s1"], S_["cy"], ALU.subtract))
            ch(V.tensor_tensor(S_["s2"], S_["s2"], S_["a2"], ALU.subtract))
            ch(V.tensor_tensor(S_["cy"], S_["cy"], S_["a2"], ALU.add))
            ch(V.tensor_tensor(S_["cz"], S_["s1"], S_["s2"], ALU.add))
            ch(V.tensor_tensor(sel, idx, wide(S_["a1"]), ALU.is_equal))
            ch(V.tensor_tensor(sel, sel, wide(S_["cy"]), ALU.mult))
            for i in range(NT):
                ins = V.scalar_tensor_tensor(x[:, i, :], yn[:, i, :], gs["cz"][:, i:i + 1], x[:, i, :], ALU.mult, ALU.add)
            ch(ins)
            for e in range(E2):
                for m in range(NC2 * (e + 1), NC2 * (e + 2)):
                    if m < NM2:
                        product(m)
                dve.wait_ge(SG["y"], b * E2 + e + 1)
                for i in range(NT):
                    ins = V.scalar_tensor_tensor(x[:, i, :], ps[:, 6 + e % 2, i * P:(i + 1) * P],
                                                 sel[:, i, e:e + 1], x[:, i, :], ALU.mult, ALU.add)
                ins.then_inc(SG["acc"], 1)
                dve.wait_ge(SG["acc"], b * E2 + e + 1)

        block = ctx.enter_context(nc.Block())
        CONST = ["sqw", "sqc", "colb", "rowb", "dec_row", "dec_col", "vmask", "rmask", "xmask_in",
                 "amask_in", "kmask_in", "rk", "rv", "cwg", "cw1", "cw2", "cb2", "fwq", "fwk", "fwv", "fwo", "rot", "gwr",
                 "gw1", "gw2", "gw3"]
        tiles = dict(sqw=sqw, sqc=sqc, colb=colb, rowb=rowb, dec_row=dec_row,
                     dec_col=dec_col, vmask=vmask, rmask=rmask, xmask_in=xmask_in, amask_in=amask_in, kmask_in=kmask_in, rk=rk, rv=rv,
                     cwg=cwg, cw1=cw1, cw2=cw2, cb2=cb2, fwq=fwq, fwk=fwk, fwv=fwv, fwo=fwo, rot=rot, gwr=gwr,
                     gw1=gw1, gw2=gw2, gw3=gw3)
        NCONST = 16 * len(CONST)

        @block.sync
        def _(sp):
            for name in CONST:
                if name in ("rowb", "kmask_in"):
                    src = t[name].unsqueeze(0).to_broadcast([P] + list(t[name].shape))
                else:
                    src = t[name]
                dst = tiles[name]
                sp.dma_start(dst[tuple(slice(None) for _ in dst.shape)], src).then_inc(s_const, 16)
            def load_ctx(b, ph):
                for a in range(2):
                    sp.dma_start(ctxT[:, a, :], t["ctxT"][bass.ds(b, 1)].rearrange("o d k -> d (o k)"))\
                        .then_inc(SH[ph]["ctx"], 16)

            for b in range(B):
                sp.dma_start(x[:, :, :], t["x"][bass.ds(b, 1)].rearrange("o (t p) d -> p (o t) d", p=P))\
                    .then_inc(SH[0]["x"], 16)
                load_ctx(b, 0)
                sp_D0(sp, b)
            for b in range(B):
                sp_D(sp, b)
            for b in range(B):
                sp.dma_start(x[:, :, :].rearrange("p i n -> p (i n)"),
                             x_s[bass.ds(b, 1)].rearrange("o p n -> p (o n)")).then_inc(SH[1]["x"], 16)
                load_ctx(b, 1)
                sp_D1(sp, b)
                if last == "G":
                    sp.wait_ge(SG["acc"], b * E2 + E2)
                else:
                    sp.wait_ge(s_xout, b + 1)
                sp.dma_start(out[bass.ds(b, 1)].rearrange("o (t p) d -> p (o t) d", p=P), x[:, :, :]).then_inc(s_store, 16)
                sp.wait_ge(s_store, b * 16 + 16)

        @block.tensor
        def _(pe):
            pe.wait_ge(s_const, NCONST)
            pe.wait_ge(s_zero, 1)
            pe.wait_ge(s_prep, 1)
            with pe.Fori(0, B) as b:
                pe_A(pe, b)
                pe_X(pe, b, "B")
                pe_C(pe, b)
                pe_D0(pe, b)
            with pe.Fori(0, B) as b:
                pe_D(pe, b)
            with pe.Fori(0, B) as b:
                pe_D1(pe, b)
                if "E" in stages:
                    pe_X(pe, b, "E")
                if "F" in stages:
                    pe_F(pe, b)
                if "G" in stages:
                    pe_G(pe, b)

        @block.scalar
        def _(act):
            act.wait_ge(s_const, NCONST)
            with act.Fori(0, B) as b:
                act_A(act, b)
                act_X(act, b, "B")
                act_C(act, b)
                act_D0(act, b)
            with act.Fori(0, B) as b:
                act_D(act, b)
            with act.Fori(0, B) as b:
                if "E" in stages:
                    act_X(act, b, "E")
                if "F" in stages:
                    act_F(act, b)
                if "G" in stages:
                    act_G(act, b)

        @block.vector
        def _(dve):
            dve.wait_ge(s_const, NCONST)
            nc.vector.tensor_copy(identb[:, :], c["ident"])
            nc.vector.tensor_copy(causal[:, :], c["causal"])
            for r in range(REP):
                nc.vector.tensor_copy(xmask[:, :, r * KP:(r + 1) * KP], xmask_in)
            nc.vector.memset(amask[:, :, KS:KP], MASKED)
            nc.vector.memset(kmask[:, :, KS:KP], MASKED)
            nc.vector.tensor_scalar(amask[:, :, 0:KS], amask_in[:, :, :], MASKED, None, ALU.mult)
            nc.vector.tensor_scalar(kmask[:, :, 0:KS], kmask_in[:, :, :], MASKED, None, ALU.mult).then_inc(s_prep, 1)
            dve.wait_ge(s_prep, 1)
            dve.wait_ge(s_zero, 1)
            ch = Chain(dve, SH[0]["ch"], CH["first"])
            with dve.Fori(0, B) as b:
                ch.turn(b)
                dve.wait_ge(SH[0]["x"], b * 16 + 16)
                dve_A(dve, ch, b)
                dve_X(dve, ch, b, "B")
                dve_C(dve, ch, b)
                dve_D0(dve, ch, b)
                ch.end()
            with dve.Fori(0, B) as b:
                dve_D(dve, b)
            ch = Chain(dve, SH[1]["ch"], CH[last])
            with dve.Fori(0, B) as b:
                ch.turn(b)
                dve.wait_ge(SH[1]["x"], b * 16 + 16)
                dve_D1(dve, ch, b)
                if "E" in stages:
                    dve_X(dve, ch, b, "E")
                if "F" in stages:
                    dve_F(dve, ch, b)
                if "G" in stages:
                    dve_G(dve, ch, b)
                if last != "G":
                    nc.vector.tensor_copy(tmp[:, 0:1], x[:, 0, 0:1]).then_inc(s_xout, 1)
                ch.end()

        @block.gpsimd
        def _(pool):
            pool.wait_ge(s_const, NCONST)
            nc.gpsimd.memset(onehot[:, :, :], 0.0)
            nc.gpsimd.memset(ohsum[:, :], 0.0)
            nc.gpsimd.memset(ai[:, :, :], 0.0).then_inc(s_zero, 1)
            with pool.Fori(0, B) as b:
                pool_X(pool, b, "B")
            with pool.Fori(0, B) as b:
                pool_D(pool, b)
            with pool.Fori(0, B) as b:
                if "E" in stages:
                    pool_X(pool, b, "E")
                if "F" in stages:
                    pool_F(pool, b)


CH = {"first": 75, "D": 2, "E": 55, "F": 130, "G": 176}


def arrays_of(inputs):
    import numpy as np

    g = {k: np.asarray(v) for k, v in inputs.items()}
    f = np.float32
    d = {}
    d["x"] = g["x"]
    ctxT = np.zeros((B, P, KP), f)
    ctxT[:, :, :KS] = g["ctx_1024"].transpose(0, 2, 1)
    d["ctxT"] = ctxT
    sq = {"A_q": g["L0_attn_W_q"].T, "A_k": g["L0_attn_W_k"].T, "A_v": g["L0_attn_W_v"].T, "A_o": g["L0_attn_W_o"].T}
    for k, n, tr in (("B", "L0_xattn", True), ("D", "L1_attn", True), ("E", "L1_xattn", False)):
        for m in "qkvo":
            a = g[f"{n}_W{m}"]
            sq[f"{k}_{m}"] = a.T if tr else a
    d["sqw"] = np.stack([sq[n] for n in SQW], 1)
    r = np.arange(P)
    con = {"ident": np.eye(P), "block": r[:, None] // DK == r[None] // DK,
           "mask_i": (r[:, None] // DK == r[None] % DK) & (r[:, None] < 64),
           "tri": r[:, None] <= r[None], "ones": np.ones((P, P)),
           "causal": np.where(r[:, None] < r[None], MASKED, 0.0)}
    d["sqc"] = np.stack([con[n] for n in SQC], 1).astype(f)
    names = {"A": "L0_attn_b_", "B": "L0_xattn_b", "D": "L1_attn_b", "E": "L1_xattn_b"}
    vec = {f"{k}_b{m}": g[names[k] + m] for k in names for m in "qkvo"}
    d["colb"] = np.concatenate([np.stack([vec[n] for n in COLB], 1),
                                g["L0_ffn_b1"].reshape(-1, P).T], 1)
    rb = np.zeros(P, f)
    rb[:E2] = g["L1_ffn_router_b"]
    vec.update(F_g1=g["L1_ffn_g1"], F_g2=g["L1_ffn_g2"], G_rb=rb, rank=(E1 - r).astype(f), index=r.astype(f))
    d["rowb"] = np.stack([vec[n] for n in ROWB], 0)
    dec = np.exp(-np.arange(S, dtype=f) / S).astype(f)
    d["dec_row"] = np.broadcast_to(dec, (P, S))
    d["dec_col"] = dec.reshape(NT, P).T
    vm = np.zeros((P, NPER, P + 96), f)
    for j in range(NPER):
        at = j * P + r
        vm[:, j, 96:] = ((at // KP)[:, None] == (r // DK)[None]) & ((at % KP) < KS)[:, None]
    d["vmask"] = vm
    rm = np.zeros((P, P + 64), f)
    rm[:, :P] = con["block"]
    rm[:, P:] = (r % DK)[:, None] == (np.arange(64) // DK)[None]
    d["rmask"] = rm
    q = np.arange(S)
    xm = np.full((S, KP), MASKED, f)
    xm[:, :KS] = np.where(np.arange(KS)[None] > q[:, None], MASKED, 0.0)
    d["xmask_in"] = xm.reshape(NT, P, KP).transpose(1, 0, 2)
    d["amask_in"] = g["mask_SxS2_bk1"].astype(np.int32).reshape(NT, P, KS).transpose(1, 0, 2)
    d["kmask_in"] = g["mask_BxS2_bf0"].astype(np.int32)
    M = (len(g["L1_attn_rel_k"]) - 1) // 2
    dist = NU * np.arange(DK)[:, None] + (NU - 1) - np.arange(RELW)[None]
    rk = np.zeros((P, RELW), f)
    rk[:DK * DK] = g["L1_attn_rel_k"][np.clip(dist, -M, M) + M].transpose(0, 2, 1).reshape(DK * DK, RELW)
    d["rk"] = rk
    dist = np.arange(RVS)[None] - r[:, None] - (S - P)
    d["rv"] = g["L1_attn_rel_v"][np.clip(dist, -M, M) + M].reshape(P, RVS * DK)
    d["cwg"] = g["L0_ffn_Wg"].T
    d["cw1"] = g["L0_ffn_W1"].transpose(1, 0, 2)
    d["cw2"] = g["L0_ffn_W2"].reshape(-1, P, P).transpose(1, 0, 2)
    cb2 = np.zeros((P, P), f)
    cb2[:E1] = g["L0_ffn_b2"]
    d["cb2"] = cb2
    half = KD // 2
    swap = lambda a: a.reshape(P, -1, 2, half)[:, :, ::-1].reshape(P, -1)
    d["fwq"] = np.stack([g["L1_ffn_wq"], swap(g["L1_ffn_wq"])], 1)
    d["fwk"] = np.stack([g["L1_ffn_wk"], swap(g["L1_ffn_wk"])], 1)
    d["fwv"] = g["L1_ffn_wv"]
    d["fwo"] = g["L1_ffn_wo"].reshape(-1, P, P).transpose(1, 0, 2)
    th = 10000.0 ** (-np.arange(0, KD, 2, dtype=f) / KD)
    tick = np.tile(np.outer(np.arange(S, dtype=f), th), (1, 2)).astype(f).T
    sign = np.where(np.arange(KD) < half, -1.0, 1.0)[:, None].astype(f)
    cos, sin = np.cos(tick), np.sin(tick) * sign
    two = lambda a: np.concatenate([a, a], 0)
    d["rot"] = np.stack([two(cos) / 8, two(sin) / 8, two(cos), two(sin)], 1).astype(f)
    d["gwr"] = g["L1_ffn_router_w"]
    for n in ("1", "2"):
        d["gw" + n] = g["L1_ffn_w" + n].transpose(1, 0, 2)
    d["gw3"] = g["L1_ffn_w3"].reshape(-1, P, P).transpose(1, 0, 2)
    return {k: np.ascontiguousarray(v) for k, v in d.items()}


def program(nc, arrays, last="G"):
    t = {n: nc.dram_tensor(f"in_{n}", a.shape, mybir.dt.from_np(a.dtype), kind="ExternalInput").ap()
         for n, a in arrays.items()}
    out = nc.dram_tensor("out", (B, S, P), F32, kind="ExternalOutput").ap()
    decoder(nc, t, out, last)


def kernel(**inputs):
    import concourse.bacc as _bacc
    from concourse.bass_utils import run_bass_kernel_spmd as _run

    arrays = arrays_of(inputs)
    nc = _bacc.Bacc("TRN2", target_bir_lowering=False, num_devices=1)
    program(nc, arrays)
    r = _run(nc, [{f"in_{n}": a for n, a in arrays.items()}], core_ids=[0])
    return r.results[0]["out"]
```

```python
from contextlib import ExitStack

import concourse.bass as bass
from concourse import mybir

ALU = mybir.AluOpType
ACT = mybir.ActivationFunctionType
AX = mybir.AxisListType
F32 = mybir.dt.float32
BF16 = mybir.dt.bfloat16

P = 128
B = 4
S = 512
NT = S // P
H = 16
DK = P // H
KS = 154
KP = 160
REP = 4
HALF = H // 2 * KP
NCH = HALF // P
NPER = KP // 32
VH = P // 2
VW = VH + H // 2
MASKED = -1e30
LN_EPS = 1e-5
ATT_EPS = 1e-6
RMS_EPS = 1e-6
E1, HID1 = 8, 512
E2, HID2 = 8, 256
CAP = B * S // 8
HQ, HKV, KD = 16, 4, 64
NG = HQ // HKV
NU = S // DK
RELW = NU - 1 + S
RVS = S - P + S
SOFT = 1.0 / DK ** 0.5

COLB = ["A_bq", "B_bq", "B_bk", "D_bq", "D_bk", "E_bq", "E_bk"]
ROWB = ["A_bk", "A_bv", "A_bo", "B_bv", "B_bo", "D_bv", "D_bo", "E_bv", "E_bo", "F_g1", "F_g2", "G_rb", "rank", "index"]
SQW = ["A_q", "A_k", "A_v", "A_o", "B_q", "B_k", "B_v", "B_o", "D_q", "D_k", "D_v", "D_o", "E_q", "E_k", "E_v", "E_o"]
SQC = ["ident", "block", "mask_i", "tri", "ones", "causal"]


class Chain:

    def __init__(self, eng, sem, per_turn):
        self.eng, self.sem, self.per_turn = eng, sem, per_turn

    def turn(self, index):
        self.base, self.n = index * self.per_turn, 0

    def __call__(self, ins):
        self.n += 1
        ins.then_inc(self.sem, 1)
        self.eng.wait_ge(self.sem, self.base + self.n)

    def end(self):
        assert self.n == self.per_turn, (self.n, self.per_turn)


def decoder(nc, t, out, last="G"):
    stages = "ABCDEFG"[: "ABCDEFG".index(last) + 1]
    NX3 = len(stages) - 4
    ctx = ExitStack()
    with ctx:
        def sb(name, shape, dt=F32):
            return ctx.enter_context(nc.sbuf_tensor(name, shape, dt))

        def sem(name):
            return ctx.enter_context(nc.semaphore(name))

        ps = ctx.enter_context(nc.psum_tensor("ps", [P, 8, 512], F32))

        sqw = sb("sqw", [P, len(SQW), P])
        w = {n: sqw[:, i, :] for i, n in enumerate(SQW)}
        sqc = sb("sqc", [P, len(SQC), P])
        c = {n: sqc[:, i, :] for i, n in enumerate(SQC)}
        colb = sb("colb", [P, len(COLB) + E1 * HID1 // P])
        rowb = sb("rowb", [P, len(ROWB), P])
        row = {n: rowb[:, i, :] for i, n in enumerate(ROWB)}
        identb = sb("identb", [P, P], BF16)
        causal = sb("causal", [P, P], BF16)
        dec_row = sb("dec_row", [P, S])
        dec_col = sb("dec_col", [P, NT])
        vmask = sb("vmask", [P, NPER, P + 96])
        rmask = sb("rmask", [P, P + 64])
        xmask = sb("xmask", [P, NT, REP * KP], BF16)
        amask = sb("amask", [P, NT, KP], BF16)
        kmask = sb("kmask", [P, B, KP], BF16)
        rk = sb("rk", [P, RELW])
        rv = sb("rv", [P, RVS * DK])
        cwg = sb("cwg", [P, E1])
        cw1 = sb("cw1", [P, E1, HID1])
        cw2 = sb("cw2", [P, E1 * HID1 // P, P])
        cb2 = sb("cb2", [P, P])
        fwq = sb("fwq", [P, 2, HQ * KD])
        fwk = sb("fwk", [P, 2, HKV * KD])
        fwv = sb("fwv", [P, HKV * KD])
        fwo = sb("fwo", [P, HQ * KD // P, P])
        rot = sb("rot", [P, 4, S])
        gwr = sb("gwr", [P, E2])
        gw1 = sb("gw1", [P, E2, HID2])
        gw2 = sb("gw2", [P, E2, HID2])
        gw3 = sb("gw3", [P, E2 * HID2 // P, P])

        x = sb("x", [P, NT, P])
        xn = sb("xn", [P, NT, P])
        xnT = sb("xnT", [P, S])
        stats = sb("stats", [P, NT, 6])
        mv = sb("mv", [P, NT, 2])
        var = sb("var", [P, NT])
        root = sb("root", [P, NT])
        spare = sb("spare", [P, 1])
        spare2 = sb("spare2", [P, 2])
        warm = sb("warm", [P, 20])
        rstd = sb("rstd", [P, NT])
        aoT = sb("aoT", [P, S])
        q_t = sb("q_t", [P, S])
        tmp = sb("tmp", [P, S])
        ctxT = sb("ctxT", [P, 2, KP])
        onehot = sb("onehot", [P, NT, P])
        ohsum = sb("ohsum", [P, 2 * E2])

        ARENA = 11296
        arena = sb("arena", [P, ARENA])
        used = [0]

        def cut(n):
            used[0] += n
            assert used[0] <= ARENA, used[0]
            return arena[:, used[0] - n:used[0]]

        amask_in, kmask_in = (cut(NT * KS).bitcast(mybir.dt.int32).rearrange("p (t k) -> p t k", k=KS) for _ in range(2))

        xmask_in = cut(NT * KP).rearrange("p (t k) -> p t k", k=KP)

        s_const = [sem("s_const%d" % i) for i in range(5)]
        s_prep = sem("s_prep")
        s_zero = sem("s_zero")
        SH = [{n: sem(f"s_{n}{i}") for n in ("x", "ctx", "xn", "var", "root", "tr", "xT", "ch", "wo")} for i in range(2)]
        s_store = sem("s_store")
        s_xout = sem("s_xout")
        NLN = (4, NX3)
        NNORM = (4, [0, 1, 3, 4][NX3])
        NWO = (2, 1 + (NX3 > 0))
        DH = dict(A=(0, 0), B=(0, 1), C=(0, 2), D=(0, 3), E=(1, 0), F=(1, 1), G=(1, 2))

        s_aq, s_akv, s_aqr, s_akvr, s_akvp, s_abd, s_aout, s_aao, s_aT, s_aTc = map(sem, (
            "s_aq", "s_akv", "s_aqr", "s_akvr", "s_akvp", "s_abd", "s_aout", "s_aao",
            "s_aT", "s_aTc"))
        XA = {}
        for k in "BE":
            XA[k] = {n: sem(f"s_{k}_{n}") for n in (
                "kv", "kt", "vrep", "kbd", "vs", "qp", "qt", "mask", "sc", "sub", "exp", "pt", "ptc", "pv", "o", "aT", "aTc")}

        NXH = 2 * NT

        used[0] = 0
        TX = dict(kt=cut(KP), kbd=cut(H * KP), vs=cut(2 * NCH * VW), vrep=cut(NPER * P), bmask=cut(NT * REP * KP // 2),
                  m=cut(2 * 8), r=cut(2 * 8), g=cut(2 * 8), ao=cut(S))
        X_KEEP = used[0]
        TX.update(d0=cut(HALF), d1=cut(HALF), pt=cut(HALF))
        X_END = used[0]
        xin = cut(NT * P).rearrange("p (i n) -> p i n", i=NT)
        bmask = TX["bmask"].bitcast(BF16).rearrange("p (t n) -> p t n", t=NT)
        vs = TX["vs"].rearrange("p (c n) -> p c n", c=2 * NCH)

        AW = P + H
        used[0] = X_KEEP
        TA = dict(qf=cut(S), kf=cut(S), v1=cut(NT * AW), bd=cut(AW), den=cut(NT * H), ao=cut(S))
        assert used[0] <= X_END

        FILL = dict(A=(8, 0), B=(14, 0), C=(14, 0), D=(14, 0), E=(14, 4), F=(28, 0), G=(14, 0))

        def pe_transpose(pe, b, k, src=xn):
            ph, g = DH[k]
            s = SH[ph]
            for _ in range(FILL[k][0]):
                nc.tensor.matmul(ps[:, FILL[k][1], :], identb[:, :], xmask[:, 0, 0:512], start=True, stop=True)
            pe.wait_ge(s["xn"], b * (NLN[ph] * NT) + (g + 1) * NT)
            for i in range(NT):
                ins = nc.tensor.transpose(ps[:, 0, i * P:(i + 1) * P], src[:, i, :], c["ident"])
            ins.then_inc(s["tr"], 1)
            pe.wait_ge(s["xT"], b * NLN[ph] + g + 1)

        def act_transpose(act, b, k):
            ph, g = DH[k]
            act.wait_ge(SH[ph]["tr"], b * NLN[ph] + g + 1)
            nc.scalar.copy(xnT[:, :], ps[:, 0, :]).then_inc(SH[ph]["xT"], 1)

        def dve_norm(dve, ch, b, k, keep=None, src=x):
            ph, g = DH[k]
            s = SH[ph]
            for i in range(NT):
                ins = nc.vector.bn_stats(stats[:, i, :], src[:, i, :])
            ch(ins)
            nc.vector.memset(spare[:, :], 0.0)
            for i in range(NT):
                ins = nc.vector.bn_aggr(mv[:, i, :], stats[:, i, :])
            ch(ins)
            nc.vector.tensor_scalar(var[:, :], mv[:, :, 1], LN_EPS, None, ALU.add).then_inc(s["var"], 1)
            dve.wait_ge(s["root"], b * NNORM[ph] + g + 1)
            ch(nc.vector.reciprocal(rstd[:, :], root[:, :]))
            for i in range(NT):
                ins = nc.vector.tensor_scalar(xn[:, i, :], src[:, i, :], mv[:, i, 0:1], rstd[:, i:i + 1],
                                        ALU.subtract, ALU.mult)
                if keep is None:
                    ins.then_inc(s["xn"], 1)
            if keep is not None:
                keep(ins)

        def act_root(act, b, k, second=0, then=None):
            ph, g = DH[k]
            g += second + (k == "G")
            nc.scalar.activation(warm[:, 2 * (ph * 5 + g):2 * (ph * 5 + g) + 1], c["ones"][:, 0:1], ACT.Sqrt)
            act.wait_ge(SH[ph]["var"], b * NNORM[ph] + g + 1)
            nc.scalar.activation(root[:, :], var[:, :], ACT.Sqrt).then_inc(SH[ph]["root"], 1)
            if then is not None:
                nc.scalar.activation(warm[:, 2 * (ph * 5 + g) + 1:2 * (ph * 5 + g) + 2], c["ones"][:, 0:1], then)

        OB = {(0, 0): 7, (0, 1): 7, (1, 0): 0, (1, 1): 7}

        def pe_project(pe, b, ph, g, wo):
            for i in range(NT):
                nc.tensor.matmul(ps[:, OB[ph, g], i * P:(i + 1) * P], aoT[:, i * P:(i + 1) * P], wo,
                                 start=False, stop=True, skip_group_check=True).then_inc(SH[ph]["wo"], 1)

        def pe_bias(ph, g, bo):
            nc.tensor.matmul(ps[:, OB[ph, g], :].rearrange("p (i n) -> p i n", i=NT), c["ones"][0:1, :],
                             row[bo][0:1, :].unsqueeze(1).to_broadcast([1, NT, P]), start=True, stop=False,
                             skip_group_check=True)

        def dve_residual(dve, ch, b, ph, g, src=x):
            dve.wait_ge(SH[ph]["wo"], b * NWO[ph] * NT + (g + 1) * NT)
            ch(nc.vector.tensor_tensor(x[:, :, :], ps[:, OB[ph, g], :].rearrange("p (a n) -> p a n", a=NT), src[:, :, :], ALU.add))

        def pe_A(pe, b):
            pe_X_context(pe, b, "B")
            pe_transpose(pe, b, "A")
            nc.tensor.matmul(ps[:, 1, :], w["A_q"], xnT[:, :], start=True, stop=True).then_inc(s_aq, 1)
            for i in range(NT):
                o = ps[:, 2 + i // 2, (i % 2) * 256:(i % 2) * 256 + 256]
                nc.tensor.matmul(o, xnT[:, i * P:(i + 1) * P], sqw[:, 1:3, :].rearrange("p a n -> p (a n)"),
                                 start=True, stop=True).then_inc(s_akv, 1)
            pe.wait_ge(XA["B"]["kt"], b + 1)
            pe.wait_ge(XA["B"]["vrep"], b + 1)
            for i in range(NT):
                pe.wait_ge(s_akvr, b * NT + i + 1)
                ins = nc.tensor.matmul(ps[:, 4, 0:AW], TA["kf"][:, i * P:(i + 1) * P],
                                       TA["v1"][:, i * AW:(i + 1) * AW], start=(i == 0), stop=(i == NT - 1))
            ins.then_inc(s_akvp, 1)
            pe_bias(0, 0, "A_bo")
            pe.wait_ge(s_abd, b * 3 + 3)
            for i in range(NT):
                o = ps[:, 5 + i // 2, (i % 2) * 256:(i % 2) * 256 + AW]
                ins = nc.tensor.matmul(o, TA["qf"][:, i * P:(i + 1) * P], TA["bd"], start=True, stop=True)
            ins.then_inc(s_aout, 1)
            for i in range(NT):
                pe.wait_ge(s_aao, b * NT + i + 1)
                ins = nc.tensor.transpose(ps[:, 1, i * P:(i + 1) * P], TA["ao"][:, i * P:(i + 1) * P], c["ident"])
            ins.then_inc(s_aT, 1)
            pe.wait_ge(s_aTc, b + 1)
            pe_project(pe, b, 0, 0, w["A_o"])

        def act_A(act, b):
            act_root(act, b, "A")
            act_X_keys(act, b, "B")
            act_transpose(act, b, "A")
            act.wait_ge(SD["spill"], b * 64 + 64)
            act.wait_ge(s_aq, b + 1)
            nc.scalar.activation(q_t[:, :], ps[:, 1, :], ACT.Relu, bias=colb[:, 0:1]).then_inc(s_aqr, 1)
            act.wait_ge(s_aT, b + 1)
            nc.scalar.copy(aoT[:, :], ps[:, 1, :]).then_inc(s_aTc, 1)

        def dve_A(dve, ch, b):
            dve_norm(dve, ch, b, "A", src=xin)
            dve_X_values(dve, b, "B")
            v1 = TA["v1"].rearrange("p (a n) -> p a n", a=NT)
            nc.vector.memset(v1[:, :, P:AW], 1.0)
            for z in range(2):
                dve.wait_ge(s_akv, b * NT + 2 * z + 2)
                o = ps[:, 2 + z, :].rearrange("p (a n) -> p a n", a=2)
                wide = lambda n: row[n].unsqueeze(1).to_broadcast([P, 2, P])
                ch(nc.vector.tensor_tensor(tmp[:, 2 * z * P:2 * (z + 1) * P].rearrange("p (a n) -> p a n", a=2),
                                           o[:, :, 0:P], wide("A_bk"), ALU.add))
                nc.vector.tensor_tensor(v1[:, 2 * z:2 * z + 2, 0:P], o[:, :, P:2 * P], wide("A_bv"), ALU.add)
                for i in (2 * z, 2 * z + 1):
                    nc.vector.tensor_scalar(TA["kf"][:, i * P:(i + 1) * P], tmp[:, i * P:(i + 1) * P], 0.0,
                                            dec_col[:, i:i + 1], ALU.max, ALU.mult).then_inc(s_akvr, 1)
            dve.wait_ge(s_aqr, b + 1)
            nc.vector.tensor_tensor(TA["qf"], q_t[:, :], dec_row[:, :], ALU.mult).then_inc(s_abd, 1)
            dve.wait_ge(s_akvp, b + 1)
            nc.vector.tensor_tensor(TA["bd"][:, 0:P], ps[:, 4, 0:P], c["block"], ALU.mult).then_inc(s_abd, 1)
            nc.vector.tensor_tensor(TA["bd"][:, P:AW], ps[:, 4, P:AW],
                                    c["block"].rearrange("p (h e) -> p h e", h=H)[:, :, 0], ALU.mult).then_inc(s_abd, 1)
            dve.wait_ge(s_aout, b + 1)
            den = TA["den"].rearrange("p (i h) -> p i h", i=NT)
            o = ps[:, 5:7, :].rearrange("p a (z n) -> p (a z) n", z=2)
            ch(nc.vector.tensor_scalar(den, o[:, :, P:AW], ATT_EPS, None, ALU.add))
            ch(nc.vector.reciprocal(TA["den"], TA["den"]))
            for i in range(NT):
                nc.vector.tensor_tensor(TA["ao"][:, i * P:(i + 1) * P].rearrange("p (h e) -> p h e", h=H),
                                        o[:, i, 0:P].rearrange("p (h e) -> p h e", h=H),
                                        den[:, i, :].unsqueeze(2).to_broadcast([P, H, DK]), ALU.mult).then_inc(s_aao, 1)
            km = kmask[:, bass.ds(b, 1), :].to_broadcast([P, NT, KP])
            for r in range(REP):
                ins = nc.vector.tensor_tensor(bmask[:, :, r * KP:(r + 1) * KP], amask[:, :, :], km, ALU.min)
            ins.then_inc(XA["B"]["mask"], 1)
            dve_residual(dve, ch, b, 0, 0, src=xin)

        XBANK = dict(B=4, E=1)

        def pe_X_context(pe, b, k):
            s = XA[k]
            pe.wait_ge(SH[DH[k][0]]["ctx"], b * 32 + 32)
            flat = ctxT[:, :, :].rearrange("p a n -> p (a n)")
            nc.tensor.matmul(ps[:, XBANK[k], 0:KP], w[k + "_k"], flat[:, 0:KP], start=True, stop=True).then_inc(s["kv"], 1)
            for j in range(NPER):
                o = ps[:, XBANK[k] + 1 + j // 4, (j % 4) * P:(j % 4 + 1) * P]
                ins = nc.tensor.matmul(o, flat[:, j * P % KP:j * P % KP + P], w[k + "_v"], start=True, stop=True)
            ins.then_inc(s["kv"], 1)

        def pe_X(pe, b, k):
            s = XA[k]
            pe_transpose(pe, b, k)
            nc.tensor.matmul(ps[:, 4, :], w[k + "_q"], xnT[:, :], start=True, stop=True).then_inc(s["qp"], 1)
            mask = bmask if k == "B" else xmask
            pe.wait_ge(s["kbd"], b + 1)
            pe.wait_ge(s["vs"], b + 1)
            pe.wait_ge(s["qt"], b + 1)
            if k == "B":
                pe.wait_ge(s["mask"], b + 1)

            rounds = [(0, 4), (4, 8), (8, NCH)]

            def scores(n, first, last):
                i, half, bank = n // 2, n % 2, 3 * (n % 2)
                for j in range(first, last + 1):
                    at, width = j * 512, min(512, HALF - j * 512)
                    nc.tensor.matmul(ps[:, bank + j, 0:width], q_t[:, i * P:(i + 1) * P],
                                     TX["kbd"][:, half * HALF + at:half * HALF + at + width], start=True, stop=False)
                    ins = nc.tensor.matmul(ps[:, bank + j, 0:width], identb[:, :],
                                           mask[:, i, at % KP:at % KP + width], start=False, stop=True)
                if last == 2:
                    ins.then_inc(s["sc"], 1)

            def flip(n, r):
                c0, c1 = rounds[r]
                m = 3 * n + r
                if m >= 2:
                    pe.wait_ge(s["ptc"], b * 3 * NXH + m - 1)
                for cc in range(c0, c1):
                    ins = nc.tensor.transpose(ps[:, 6 + m % 2, (cc - c0) * P:(cc - c0 + 1) * P],
                                              TX["d%d" % (n % 2)][:, cc * P:(cc + 1) * P], c["ident"])
                ins.then_inc(s["pt"], 1)

            scores(0, 0, 2)
            scores(1, 0, 2)
            for n in range(NXH):
                half, bank = n % 2, 3 * (n % 2)
                for r in (0, 1):
                    pe.wait_ge(s["exp"], b * 2 * NXH + 2 * n + r + 1)
                    flip(n, r)
                if 1 <= n < NXH - 1:
                    pe.wait_ge(s["o"], b * NXH + n)
                    scores(n + 1, 2, 2)
                if n + 2 < NXH:
                    scores(n + 2, 0, 1)
                flip(n, 2)
                for r, (c0, c1) in enumerate(rounds):
                    pe.wait_ge(s["ptc"], b * 3 * NXH + 3 * n + r + 1)
                    for cc in range(c0, c1):
                        ins = nc.tensor.matmul(ps[:, bank + 2, 256:256 + VW], TX["pt"][:, cc * P:(cc + 1) * P],
                                               vs[:, half * NCH + cc, :], start=(cc == 0), stop=(cc == NCH - 1))
                ins.then_inc(s["pv"], 1)
            pe_bias(DH[k][0], 1, k + "_bo")
            pe.wait_ge(s["o"], b * NXH + NXH)
            for i in range(NT):
                ins = nc.tensor.transpose(ps[:, 0, i * P:(i + 1) * P], TX["ao"][:, i * P:(i + 1) * P], c["ident"])
            ins.then_inc(s["aT"], 1)
            pe.wait_ge(s["aTc"], b + 1)
            pe_project(pe, b, DH[k][0], 1, w[k + "_o"])

        def act_X_keys(act, b, k):
            s = XA[k]
            kb = COLB.index(k + "_bk")
            act.wait_ge(s["kv"], b * 2 + 1)
            nc.scalar.activation(TX["kt"], ps[:, XBANK[k], 0:KP], ACT.Identity, bias=colb[:, kb:kb + 1])\
                .then_inc(s["kt"], 1)

        def act_X(act, b, k):
            s = XA[k]
            qb = COLB.index(k + "_bq")
            act_root(act, b, k, then=ACT.Exp)
            act_transpose(act, b, k)
            act.wait_ge(s["qp"], b + 1)
            nc.scalar.activation(q_t[:, :], ps[:, 4, :], ACT.Identity, bias=colb[:, qb:qb + 1]).then_inc(s["qt"], 1)
            scale = SOFT if k == "B" else 1.0 / KS ** 0.5

            def exps(n):
                for z in range(2):
                    act.wait_ge(s["sub"], b * 2 * NXH + 2 * n + z + 1)
                    d = TX["d%d" % (n % 2)][:, z * HALF // 2:(z + 1) * HALF // 2]
                    nc.scalar.activation(d, d, ACT.Exp, scale=scale).then_inc(s["exp"], 1)

            def copy(n, r):
                c0, c1 = [(0, 4), (4, 8), (8, NCH)][r]
                m = 3 * n + r
                if r == 0 and n >= 1:
                    act.wait_ge(s["pv"], b * NXH + n)
                act.wait_ge(s["pt"], b * 3 * NXH + m + 1)
                nc.scalar.copy(TX["pt"][:, c0 * P:c1 * P], ps[:, 6 + m % 2, 0:(c1 - c0) * P]).then_inc(s["ptc"], 1)

            exps(0)
            for n in range(NXH):
                for r in range(3):
                    copy(n, r)
                if n + 1 < NXH:
                    exps(n + 1)
            act.wait_ge(s["aT"], b + 1)
            nc.scalar.copy(aoT[:, :], ps[:, 0, :]).then_inc(s["aTc"], 1)

        def dve_X_values(dve, b, k):
            s = XA[k]
            dve.wait_ge(s["kv"], b * 2 + 2)
            nc.vector.tensor_tensor(TX["vrep"].rearrange("p (a n) -> p a n", a=NPER),
                                    ps[:, XBANK[k] + 1:XBANK[k] + 3, :].rearrange("p a n -> p (a n)")[:, 0:NPER * P]
                                    .rearrange("p (a n) -> p a n", a=NPER),
                                    row[k + "_bv"].unsqueeze(1).to_broadcast([P, NPER, P]), ALU.add).then_inc(s["vrep"], 1)

        def dve_X(dve, ch, b, k):
            s = XA[k]
            dve_norm(dve, ch, b, k)

            def shift(n):
                bank = 3 * (n % 2)
                sc = ps[:, bank:bank + 3, :].rearrange("p a n -> p (a n)")[:, 0:HALF].rearrange("p (h k) -> p h k", h=8)
                m = TX["m"][:, 8 * (n % 2):8 * (n % 2) + 8]
                dve.wait_ge(s["sc"], b * NXH + n + 1)
                ch(nc.vector.tensor_reduce(m, sc, AX.X, ALU.max))
                if n >= 2:
                    dve.wait_ge(s["pt"], b * 3 * NXH + 3 * (n - 1))
                for z in range(2):
                    hh = slice(4 * z, 4 * z + 4)
                    nc.vector.tensor_tensor(TX["d%d" % (n % 2)].rearrange("p (h k) -> p h k", h=8)[:, hh, :],
                                            sc[:, hh, :], m[:, hh].unsqueeze(2).to_broadcast([P, 4, KP]), ALU.subtract)\
                        .then_inc(s["sub"], 1)
                gg = TX["g"][:, 8 * (n % 2):8 * (n % 2) + 8]
                rr = TX["r"][:, 8 * (n % 2):8 * (n % 2) + 8]
                ch(nc.vector.tensor_scalar(gg, m, MASKED / 2, None, ALU.is_gt))
                ch(nc.vector.reciprocal(rr, gg))
                ch(nc.vector.tensor_tensor(gg, gg, rr, ALU.mult))

            def normalise(n):
                i, half, bank = n // 2, n % 2, 3 * (n % 2)
                o = ps[:, bank + 2, 256:256 + VW]
                gg = TX["g"][:, 8 * (n % 2):8 * (n % 2) + 8]
                rr = TX["r"][:, 8 * (n % 2):8 * (n % 2) + 8]
                dve.wait_ge(s["pv"], b * NXH + n + 1)
                ch(nc.vector.reciprocal(rr, o[:, VH:VW]))
                ch(nc.vector.tensor_tensor(rr, rr, gg, ALU.mult))
                nc.vector.tensor_tensor(
                    TX["ao"][:, i * P + half * 64:i * P + half * 64 + 64].rearrange("p (h e) -> p h e", h=8),
                    o[:, 0:VH].rearrange("p (h e) -> p h e", h=8),
                    rr.unsqueeze(2).to_broadcast([P, 8, DK]), ALU.mult).then_inc(s["o"], 1)

            for n in range(NXH + 1):
                if n < NXH:
                    shift(n)
                if n >= 1:
                    normalise(n - 1)
            dve_residual(dve, ch, b, DH[k][0], 1)

        def pool_X(pool, b, k):
            s = XA[k]
            pool.wait_ge(s["kt"], b + 1)
            nc.gpsimd.tensor_tensor(TX["kbd"].rearrange("p (h k) -> p h k", h=H),
                                    TX["kt"].unsqueeze(1).to_broadcast([P, H, KP]),
                                    c["block"].rearrange("p (h e) -> p h e", h=H)[:, :, 0:1].to_broadcast([P, H, KP]),
                                    ALU.mult).then_inc(s["kbd"], 1)
            pool.wait_ge(s["vrep"], b + 1)
            for j in range(2 * NCH // NPER):
                half = j * NPER // NCH
                mask = vmask[:, :, 96 - 32 * j + VH * half:96 - 32 * j + VH * half + VH]
                ins = nc.gpsimd.tensor_tensor(vs[:, j * NPER:(j + 1) * NPER, 0:VH],
                                              TX["vrep"].rearrange("p (a n) -> p a n", a=NPER)
                                              [:, :, half * VH:(half + 1) * VH], mask, ALU.mult)
                ins = nc.gpsimd.tensor_copy(vs[:, j * NPER:(j + 1) * NPER, VH:VW],
                                            mask.rearrange("p a (h e) -> p a h e", h=H // 2)[:, :, :, 0])
            ins.then_inc(s["vs"], 1)

        def bc(a, *shape):
            return a.to_broadcast([P, *shape])

        gt = {n: sb("gt_" + n, [P, NT, E1]) for n in ("logit", "eq", "oh1", "oh2", "sel", "pos", "junk")}
        gs = {n: sb("gs_" + n, [P, NT]) for n in ("m1", "m2", "top", "e2", "s1", "s2", "t1", "t2", "a1", "a2", "cy", "cz")}

        def dve_first(ch, logits, best, oh, done=None):
            ch(nc.vector.tensor_reduce(best[:, :], logits, AX.X, ALU.max))
            ch(nc.vector.tensor_tensor(gt["eq"][:, :, :], logits, bc(best[:, :].unsqueeze(2), NT, E1), ALU.is_ge))
            ch(nc.vector.tensor_tensor(gt["eq"][:, :, :], gt["eq"][:, :, :],
                                       bc(row["rank"][:, 0:E1].unsqueeze(1), NT, E1), ALU.mult))
            ch(nc.vector.tensor_reduce(gs["top"][:, :], gt["eq"][:, :, :], AX.X, ALU.max))
            (done or ch)(nc.vector.tensor_tensor(oh, gt["eq"][:, :, :], bc(gs["top"][:, :].unsqueeze(2), NT, E1), ALU.is_equal))

        SC = {n: sem("s_c_" + n) for n in ("gate", "oh", "ohT", "ohTc", "b2", "h", "hs", "y", "acc")}
        used[0] = 0
        TC = dict(h0=cut(4 * S), h1=cut(4 * S), ohT=cut(S))
        NC1 = HID1 // P

        def pe_C(pe, b):
            pe_transpose(pe, b, "C")
            for i in range(NT):
                ins = nc.tensor.matmul(ps[:, 1, i * E1:(i + 1) * E1], xnT[:, i * P:(i + 1) * P], cwg[:, :],
                                       start=True, stop=True)
            ins.then_inc(SC["gate"], 1)

            def hidden(e):
                for j in range(NC1):
                    m = e * NC1 + j
                    if m >= 2:
                        pe.wait_ge(SC["hs"], b * E1 * NC1 + m - 1)
                    nc.tensor.matmul(ps[:, 4 + m % 2, :], cw1[:, e, j * P:(j + 1) * P], xnT[:, :],
                                     start=True, stop=True).then_inc(SC["h"], 1)

            hidden(0)
            pe.wait_ge(SC["oh"], b + 1)
            for i in range(NT):
                ins = nc.tensor.transpose(ps[:, 2, i * P:(i + 1) * P], onehot[:, i, :], c["ident"])
            ins.then_inc(SC["ohT"], 1)
            pe.wait_ge(SC["ohTc"], b + 1)
            for i in range(NT):
                ins = nc.tensor.matmul(ps[:, 3, i * P:(i + 1) * P], TC["ohT"][:, i * P:(i + 1) * P], cb2[:, :],
                                       start=True, stop=True)
            ins.then_inc(SC["b2"], 1)
            for e in range(E1):
                if e + 1 < E1:
                    hidden(e + 1)
                pe.wait_ge(SC["hs"], b * E1 * NC1 + (e + 1) * NC1)
                if e >= 2:
                    pe.wait_ge(SC["acc"], b * E1 + e - 1)
                for i in range(NT):
                    for j in range(NC1):
                        ins = nc.tensor.matmul(ps[:, 6 + e % 2, i * P:(i + 1) * P],
                                               TC["h%d" % (e % 2)][:, j * S + i * P:j * S + (i + 1) * P],
                                               cw2[:, e * NC1 + j, :], start=(j == 0), stop=(j == NC1 - 1))
                ins.then_inc(SC["y"], 1)

        def act_C(act, b):
            act_root(act, b, "C", then=ACT.Gelu)
            act_transpose(act, b, "C")
            for e in range(E1):
                if e == 1:
                    act.wait_ge(SC["ohT"], b + 1)
                    nc.scalar.copy(TC["ohT"], ps[:, 2, :]).then_inc(SC["ohTc"], 1)
                if e >= 2:
                    act.wait_ge(SC["y"], b * E1 + e - 1)
                for j in range(NC1):
                    m = e * NC1 + j
                    act.wait_ge(SC["h"], b * E1 * NC1 + m + 1)
                    nc.scalar.activation(TC["h%d" % (e % 2)][:, j * S:(j + 1) * S], ps[:, 4 + m % 2, :], ACT.Gelu,
                                         bias=colb[:, len(COLB) + m:len(COLB) + m + 1]).then_inc(SC["hs"], 1)

        def dve_C(dve, ch, b):
            dve_norm(dve, ch, b, "C")
            dve.wait_ge(SC["gate"], b + 1)
            dve_first(ch, ps[:, 1, 0:NT * E1].rearrange("p (i e) -> p i e", i=NT), gs["m1"], onehot[:, :, 0:E1],
                      lambda ins: ins.then_inc(SC["oh"], 1))
            dve.wait_ge(SC["oh"], b + 1)
            dve.wait_ge(SC["b2"], b + 1)
            ch(nc.vector.tensor_tensor(x[:, :, :], ps[:, 3, :].rearrange("p (i n) -> p i n", i=NT), x[:, :, :], ALU.add))
            for e in range(E1):
                dve.wait_ge(SC["y"], b * E1 + e + 1)
                for i in range(NT):
                    ins = nc.vector.scalar_tensor_tensor(x[:, i, :], ps[:, 6 + e % 2, i * P:(i + 1) * P],
                                                         onehot[:, i, e:e + 1], x[:, i, :], ALU.mult, ALU.add)
                ins.then_inc(SC["acc"], 1)
                dve.wait_ge(SC["acc"], b * E1 + e + 1)

        SD = {n: sem("s_d_" + n) for n in ("kp", "kt", "qt", "v", "spill", "ld", "a", "sc", "max", "exp", "t", "ptc", "pv",
                                           "y", "yst", "ch", "ao", "at")}
        used[0] = 0
        RW = P + DK * DK
        TD = [dict(q=q, kt=cut(S), vr0=cut(NT * RW), vr1=cut(NT * RW), qi=cut(H * NU), y1=cut(S), y2=cut(S)) for q in (q_t, xnT)]
        TD0 = dict(kt=TX["ao"], v=TX["bmask"][:, 0:S])
        TU = dict(nmax=cut(NU), rsum=cut(NU),
                  **{n + str(i): cut(z) for n, z in (("a", P), ("p", S), ("pt", S), ("wt", P + 64), ("w", 16), ("r", 1))
                     for i in range(2)})
        ai = sb("ai", [P, 2, P])
        q_s, k_s, v_s, x_s, y1_s, y2_s = (nc.dram_tensor(n, (B, P, S), F32, kind="Internal").ap()
                                          for n in ("q_s", "k_s", "v_s", "x_s", "y1_s", "y2_s"))

        def turns_D(eng, body):
            with eng.Fori(0, NU // 4) as v:
                for s in range(4):
                    body(4 * v + s, s)

        def DS(s):
            return (0, 1, 6, 7)[s % 4]

        def pe_D0(pe, b):
            pe_transpose(pe, b, "D")
            nc.tensor.matmul(ps[:, 1, :], w["D_q"], xnT[:, :], start=True, stop=True).then_inc(SD["kp"], 1)
            nc.tensor.matmul(ps[:, 2, :], w["D_k"], xnT[:, :], start=True, stop=True).then_inc(SD["kp"], 1)
            for i in range(NT):
                o = (NT - 1 - i) * P
                ins = nc.tensor.matmul(ps[:, 3, o:o + P], xnT[:, i * P:(i + 1) * P], w["D_v"],
                                       start=True, stop=True)
            ins.then_inc(SD["kp"], 1)

        def act_D0(act, b):
            act_root(act, b, "D")
            act_transpose(act, b, "D")
            kb = COLB.index("D_bk")
            act.wait_ge(SD["kp"], b * 3 + 2)
            nc.scalar.activation(TD0["kt"], ps[:, 2, :], ACT.Identity, bias=colb[:, kb:kb + 1]).then_inc(SD["kt"], 1)

        def dve_D0(dve, ch, b):
            dve_norm(dve, ch, b, "D")
            qb = COLB.index("D_bq")
            dve.wait_ge(SD["kp"], b * 3 + 1)
            nc.vector.tensor_scalar(q_t[:, :], ps[:, 1, :], colb[:, qb:qb + 1], SOFT, ALU.add, ALU.mult)\
                .then_inc(SD["qt"], 1)
            dve.wait_ge(SD["kp"], b * 3 + 3)
            nc.vector.tensor_tensor(TD0["v"].rearrange("p (i n) -> p i n", i=NT),
                                    ps[:, 3, :].rearrange("p (i n) -> p i n", i=NT),
                                    row["D_bv"].unsqueeze(1).to_broadcast([P, NT, P]), ALU.add).then_inc(SD["v"], 1)

        def sp_D0(sp, b):
            one = lambda a: a[bass.ds(b, 1)].rearrange("o p n -> p (o n)")
            sp.wait_ge(SD["qt"], b + 1)
            sp.dma_start(one(q_s), q_t[:, :]).then_inc(SD["spill"], 16)
            sp.dma_start(one(x_s), x[:, :, :].rearrange("p i n -> p (i n)")).then_inc(SD["spill"], 16)
            sp.wait_ge(SD["kt"], b + 1)
            sp.dma_start(one(k_s), TD0["kt"]).then_inc(SD["spill"], 16)
            sp.wait_ge(SD["v"], b + 1)
            sp.dma_start(one(v_s), TD0["v"]).then_inc(SD["spill"], 16)
            sp.wait_ge(SD["spill"], b * 64 + 128)

        LD = 16 * (4 + DK)

        def sp_D_load(sp, b):
            T = TD[b % 2]
            one = lambda a: a[b:b + 1].rearrange("o p n -> p (o n)")
            other = q_s.rearrange("c p q -> (c p) q").rearrange("(h b d) q -> b d h q", b=B, d=DK)
            for i in range(DK):
                sp.dma_start(T["qi"][i * DK:(i + 1) * DK, :].rearrange("d (h u) -> d h u", h=H),
                             other[b:b + 1, :, :, i * NU:(i + 1) * NU].rearrange("o d h u -> (o d) h u"))\
                    .then_inc(SD["ld"], 16)
            sp.dma_start(T["q"][:, :], one(q_s)).then_inc(SD["ld"], 16)
            sp.dma_start(T["kt"], one(k_s)).then_inc(SD["ld"], 16)
            for s in range(2):
                sp.dma_start(T["vr%d" % s].rearrange("p (j n) -> p j n", j=NT)[:, :, 0:P],
                             one(v_s).rearrange("p (j n) -> p j n", j=NT)).then_inc(SD["ld"], 16)
            sp.wait_ge(SD["ld"], b * LD + LD)

        def sp_D_store(sp, b):
            T = TD[b % 2]
            one = lambda a: a[b:b + 1].rearrange("o p n -> p (o n)")
            sp.wait_ge(SD["y"], b * NU + NU + 2)
            sp.dma_start(one(y1_s), T["y1"]).then_inc(SD["yst"], 16)
            sp.dma_start(one(y2_s), T["y2"]).then_inc(SD["yst"], 16)
            sp.wait_ge(SD["yst"], b * 32 + 32)

        def pe_D(pe, b, slot):
            T = TD[slot]
            pe.wait_ge(SD["ld"], b * LD + LD)

            def scores(u, s):
                pe.wait_ge(SD["a"], b * (2 * NU) + u * 2 + 2)
                nc.tensor.matmul(ps[:, DS(s), :], TU["a%d" % (s % 2)], T["kt"], start=True, stop=False)
                nc.tensor.matmul(ps[:, DS(s), :], ai[:, s % 2, :], rk[:, bass.ds(NU - 1 - u, S)],
                                 start=False, stop=True).then_inc(SD["sc"], 1)

            def flip(u, s):
                pe.wait_ge(SD["exp"], b * NU + u + 1)
                for j in range(NT):
                    ins = nc.tensor.transpose(ps[:, 2 + s % 2, j * P:(j + 1) * P],
                                              TU["p%d" % (s % 2)][:, j * P:(j + 1) * P], c["ident"])
                ins.then_inc(SD["t"], 1)

            def values(u, s):
                pe.wait_ge(SD["ptc"], b * NU + u + 1)
                pe.wait_ge(SD["y"], b * NU + u + 1)
                for j in range(NT):
                    ins = nc.tensor.matmul(ps[:, 4 + s % 2, 0:RW], TU["pt%d" % (s % 2)][:, j * P:(j + 1) * P],
                                           T["vr%d" % (s % 2)][:, (NT - 1 - j) * RW:(NT - j) * RW],
                                           start=(j == 0), stop=(j == NT - 1))
                ins.then_inc(SD["pv"], 1)

            for u in range(3):
                scores(u, u)
            flip(0, 0)
            scores(3, 3)
            flip(1, 1)
            values(0, 0)
            with pe.Fori(0, NU // 4 - 1) as v:
                for k in range(4):
                    u, s = 4 * v + 2 + k, 2 + k
                    scores(u + 2, s + 2)
                    flip(u, s)
                    values(u - 1, s - 1)
            for u in (NU - 2, NU - 1):
                flip(u, u)
                values(u - 1, u - 1)
            values(NU - 1, NU - 1)

        def act_D(act, b, slot):
            T = TD[slot]
            rvv = rv[:, :].rearrange("p (a o d) -> p o a d", o=NU, d=DK)

            def body(u, s):
                act.wait_ge(SD["max"], b * NU + u + 1)
                nc.scalar.activation(TU["p%d" % (s % 2)], ps[:, DS(s), :], ACT.Exp, bias=TU["nmax"][:, bass.ds(u, 1)],
                                     accum_out=TU["rsum"][:, bass.ds(u, 1)]).then_inc(SD["exp"], 1)
                act.wait_ge(SD["pv"], b * NU + u + 1)
                w0 = rvv[:, bass.ds(u, 1), :, :]
                window = bass.AP(w0.tensor, w0.offset, [list(w0.ap[0]), [2 * NU * DK, NT], [NU * DK, DK], [1, DK]])
                nc.scalar.copy(T["vr%d" % (s % 2)].rearrange("p (j n) -> p j n", j=NT)[:, :, P:RW]
                               .rearrange("p j (i d) -> p j i d", i=DK), window)
                act.wait_ge(SD["t"], b * NU + u + 1)
                nc.scalar.copy(TU["pt%d" % (s % 2)], ps[:, 2 + s % 2, :]).then_inc(SD["ptc"], 1)

            turns_D(act, body)

        def dve_D(dve, b, slot):
            T = TD[slot]
            chd = Chain(dve, SD["ch"], 2)
            y1 = T["y1"].rearrange("p (d u) -> p d u", d=DK)
            y2 = T["y2"].rearrange("p (d u) -> p d u", d=DK)

            def top(u, s):
                dve.wait_ge(SD["sc"], b * NU + u + 3)
                nc.vector.tensor_reduce(TU["nmax"][:, bass.ds(u, 1)], ps[:, DS(s), :], AX.X, ALU.max, negate=True)\
                    .then_inc(SD["max"], 1)

            def rows(u, s):
                chd.turn(b * NU + u)
                o = ps[:, 4 + s % 2, :]
                wt, wv = TU["wt%d" % (s % 2)], TU["w%d" % (s % 2)]
                dve.wait_ge(SD["pv"], b * NU + u + 3)
                nc.vector.reciprocal(TU["r%d" % (s % 2)], TU["rsum"][:, bass.ds(u, 1)])
                chd(nc.vector.tensor_tensor(wt, o[:, 0:P + 64], rmask[:, :], ALU.mult))
                nc.vector.tensor_reduce(wv[:, 0:DK], wt[:, 0:P].rearrange("p (h e) -> p e h", h=H), AX.X, ALU.add)
                chd(nc.vector.tensor_reduce(wv[:, DK:16], wt[:, P:P + 64].rearrange("p (i d) -> p d i", i=DK), AX.X, ALU.add))
                nc.vector.tensor_scalar(y1[:, :, bass.ds(u, 1)].rearrange("p d o -> p (d o)"), wv[:, 0:DK],
                                        TU["r%d" % (s % 2)], None, ALU.mult)
                nc.vector.tensor_scalar(y2[:, :, bass.ds(u, 1)].rearrange("p d o -> p (d o)"), wv[:, DK:16],
                                        TU["r%d" % (s % 2)], None, ALU.mult).then_inc(SD["y"], 1)
                chd.end()

            for u in range(3):
                top(u, u)
            rows(0, 0)
            with dve.Fori(0, NU // 4 - 1) as v:
                for k in range(4):
                    top(4 * v + 3 + k, 3 + k)
                    rows(4 * v + 1 + k, 1 + k)
            top(NU - 1, NU - 1)
            for u in range(NU - 3, NU):
                rows(u, u)

        def pool_D(pool, b, slot):
            T = TD[slot]
            qu = T["q"][:, :].rearrange("p (i u) -> p u i", i=DK)
            qi = T["qi"].rearrange("p (h u) -> p h u", h=H)

            def spread(u, s):
                pool.wait_ge(SD["ld"], b * LD + LD)
                pool.wait_ge(SD["sc"], b * NU + u + 1)
                nc.gpsimd.tensor_tensor(TU["a%d" % (s % 2)].rearrange("p (h i) -> p h i", h=H),
                                        qu[:, bass.ds(u, 1), :].to_broadcast([P, H, DK]),
                                        c["block"].rearrange("p (h i) -> p h i", h=H), ALU.mult).then_inc(SD["a"], 1)
                nc.gpsimd.tensor_tensor(ai[0:64, s % 2, :].rearrange("p (h i) -> p h i", h=H),
                                        qi[0:64, :, bass.ds(u, 1)].to_broadcast([64, H, DK]),
                                        c["mask_i"][0:64, :].rearrange("p (h i) -> p h i", h=H), ALU.mult)\
                    .then_inc(SD["a"], 1)

            turns_D(pool, spread)

        own4, other4, x4 = (rv[:, i * B * S:(i + 1) * B * S] for i in range(3))
        D1 = 16 * (2 * DK + 1)

        def sp_D1(sp, b):
            own = y1_s[b:b + 1].rearrange("o (h i) (d u) -> i (o h) d u", i=DK, d=DK)
            other = y2_s.rearrange("c p n -> (c p) n").rearrange("(h z i) (d u) -> z i h d u", z=B, i=DK, d=DK)[b:b + 1]
            other = other.rearrange("o i h d u -> i (o h) d u")
            for dst, src in ((own4, own), (other4, other)):
                for i in range(DK):
                    sp.dma_start(dst[:, b * S + i * NU:b * S + (i + 1) * NU],
                                 src[i:i + 1].rearrange("o h d u -> (o h) d u")).then_inc(SD["ao"], 16)
            sp.dma_start(x4[:, b * S:(b + 1) * S], x_s[b:b + 1].rearrange("o p n -> p (o n)")).then_inc(SD["ao"], 16)
            sp.wait_ge(SD["ao"], b * D1 + D1)

        def pe_D1(pe, b):
            pe_X_context(pe, b, "E")
            pe_bias(1, 0, "D_bo")
            pe.wait_ge(SD["at"], b + 1)
            pe_project(pe, b, 1, 0, w["D_o"])

        def pool_D1(pool, b):
            pool.wait_ge(SD["ao"], b * D1 + D1)
            nc.gpsimd.tensor_tensor(aoT[:, :], own4[:, bass.ds(b * S, S)], other4[:, bass.ds(b * S, S)], ALU.add)\
                .then_inc(SD["at"], 1)

        def dve_D1(dve, ch, b):
            dve_X_values(dve, b, "E")
            dve_residual(dve, ch, b, 1, 0, src=x4[:, bass.ds(b * S, S)].rearrange("p (i n) -> p i n", i=NT))

        SF = {n: sem("s_f_" + n) for n in ("kp", "kt", "kr", "vp", "v", "qp", "qm", "qr", "sc", "max", "exp", "nrm", "t",
                                           "ptc", "pv", "ao", "wo")}
        used[0] = 0
        TF = dict(t0=cut(S), t1=cut(S), u0=cut(S), u1=cut(S), v=cut(NT * HKV * KD), nmax=cut(4), rsum=cut(4), rinv=cut(4),
                  **{f"{n}{i}": cut(S) for n in ("p", "pt") for i in range(2)}, **{f"q{i}": cut(S) for i in range(4)},
                  **{f"ao{i}": cut(S) for i in range(2)})
        krz = cut(HKV * S).rearrange("p (h s) -> p h s", h=HKV)
        yn = sb("yn", [P, NT, P])
        NTQ = HQ * KD // P

        def FS(n):
            return (1, 6, 0)[n % 3]

        def FQ(a, m):
            return (7, 0, 5, 7)[2 * a + m] if a < 2 else 5

        NUF = HQ * NT
        ORDER = [(0, 0), (0, 3), (1, 0), (1, 3), (0, 1), (0, 2), (1, 1), (1, 2)]

        def unit(n):
            hh, i = ORDER[n % len(ORDER)]
            return 2 * (n // len(ORDER)) + hh, i

        def dve_rms(dve, ch, b, g, src, dst, gamma):
            s = SH[1]
            ch(nc.vector.tensor_tensor(tmp[:, :].rearrange("p (i n) -> p i n", i=NT), src, src, ALU.mult))
            ch(nc.vector.tensor_reduce(mv[:, :, 0], tmp[:, :].rearrange("p (i n) -> p i n", i=NT), AX.X, ALU.add))
            nc.vector.tensor_scalar(var[:, :], mv[:, :, 0], 1.0 / P, RMS_EPS, ALU.mult, ALU.add).then_inc(s["var"], 1)
            dve.wait_ge(s["root"], b * NNORM[1] + g + 1)
            ch(nc.vector.reciprocal(rstd[:, :], root[:, :]))
            for i in range(NT):
                nc.vector.scalar_tensor_tensor(dst[:, i, :], src[:, i, :], rstd[:, i:i + 1], gamma,
                                               ALU.mult, ALU.mult).then_inc(s["xn"], 1)

        def pe_F(pe, b):
            pe_transpose(pe, b, "F", yn)
            for a in range(HKV * KD // P):
                for m in range(2):
                    nc.tensor.matmul(ps[:, 1 + 2 * a + m, :], fwk[:, m, a * P:(a + 1) * P], xnT[:, :],
                                     start=True, stop=True).then_inc(SF["kp"], 1)
            for i in range(NT):
                ins = nc.tensor.matmul(ps[:, 5 + i // 2, i % 2 * 256:i % 2 * 256 + 256], xnT[:, i * P:(i + 1) * P],
                                       fwv[:, :], start=True, stop=True)
            ins.then_inc(SF["vp"], 1)

            def queries(a, m):
                if (a, m) == (1, 0):
                    pe.wait_ge(SF["v"], b + 1)
                elif (a, m) == (1, 1):
                    pe.wait_ge(SF["qm"], b * 2 * NTQ + 1)
                elif a > 1:
                    pe.wait_ge(SF["qm"], b * 2 * NTQ + 2 * a + m)
                nc.tensor.matmul(ps[:, FQ(a, m), :], fwq[:, m, a * P:(a + 1) * P], xnT[:, :],
                                 start=True, stop=True).then_inc(SF["qp"], 1)

            def scores(n):
                h, i = unit(n)
                if n % len(ORDER) == 0:
                    pe.wait_ge(SF["qr"], b * NTQ + h // 2 + 1)
                wd = (i + 1) * P
                o = ps[:, FS(n), :]
                nc.tensor.matmul(o[:, 0:wd], TF["q%d" % (h // 2 % 4)][:, i * P:(i + 1) * P],
                                 krz[:, h % HKV, 0:wd], start=True, stop=False, skip_group_check=True)
                nc.tensor.matmul(o[:, i * P:wd], identb[:, :], causal[:, :], start=False, stop=True,
                                 skip_group_check=True).then_inc(SF["sc"], 1)

            def flip(n):
                i = unit(n)[1]
                pe.wait_ge(SF["nrm"], b * NUF + n + 1)
                for j in range(i + 1):
                    ins = nc.tensor.transpose(ps[:, 2 + n % 2, j * P:(j + 1) * P], TF["p%d" % (n % 2)][:, j * P:(j + 1) * P],
                                              c["ident"])
                ins.then_inc(SF["t"], 1)

            def values(n):
                h, i = unit(n)
                pe.wait_ge(SF["ptc"], b * NUF + n + 1)
                if n % (2 * NT) == 0 and n:
                    pe.wait_ge(SF["ao"], b * NTQ + h // 2)
                r0 = h % 2 * KD
                for j in range(i + 1):
                    v0 = j * HKV * KD + h % HKV * KD
                    ins = nc.tensor.matmul(ps[r0:r0 + KD, 4, i * P:(i + 1) * P], TF["v"][:, v0:v0 + KD],
                                           TF["pt%d" % (n % 2)][:, j * P:(j + 1) * P], start=(j == 0), stop=(j == i),
                                           skip_group_check=True)
                ins.then_inc(SF["pv"], 1)

            def project(a):
                pe.wait_ge(SF["ao"], b * NTQ + a + 1)
                for i in range(NT):
                    ins = nc.tensor.matmul(ps[:, 7, i * P:(i + 1) * P], TF["ao%d" % (a % 2)][:, i * P:(i + 1) * P],
                                           fwo[:, a, :], start=(a == 0 and i == 0), stop=(a == NTQ - 1),
                                           skip_group_check=True)
                ins.then_inc(SF["wo"], 1)

            for a in range(2):
                for m in range(2):
                    queries(a, m)
            pe.wait_ge(SF["kr"], b * 2 + 2)
            scores(0)
            scores(1)
            for n in range(NUF):
                if n + 2 < NUF:
                    scores(n + 2)
                a, r = n // (2 * NT), n % (2 * NT)
                if r in (2, 5) and a + 2 < NTQ:
                    queries(a + 2, r // 4)
                flip(n)
                if n >= 1:
                    values(n - 1)
                if r == 3 and a >= 1:
                    project(a - 1)
            values(NUF - 1)
            project(NTQ - 1)

        def act_F(act, b):
            act_root(act, b, "F")
            act_root(act, b, "F", 1, then=ACT.Exp)
            act_transpose(act, b, "F")
            act.wait_ge(SF["vp"], b + 1)
            nc.scalar.copy(TF["v"], ps[:, 5:7, :].rearrange("p a n -> p (a n)")).then_inc(SF["v"], 1)

            def exps(n):
                wd = (unit(n)[1] + 1) * P
                act.wait_ge(SF["max"], b * NUF + n + 1)
                if n >= 2:
                    act.wait_ge(SF["t"], b * NUF + n - 1)
                nc.scalar.activation(TF["p%d" % (n % 2)][:, 0:wd], ps[:, FS(n), 0:wd], ACT.Exp,
                                     bias=TF["nmax"][:, n % 4:n % 4 + 1],
                                     accum_out=TF["rsum"][:, n % 4:n % 4 + 1]).then_inc(SF["exp"], 1)

            def copy(n):
                wd = (unit(n)[1] + 1) * P
                act.wait_ge(SF["t"], b * NUF + n + 1)
                if n >= 2:
                    act.wait_ge(SF["pv"], b * NUF + n - 1)
                nc.scalar.copy(TF["pt%d" % (n % 2)][:, 0:wd], ps[:, 2 + n % 2, 0:wd]).then_inc(SF["ptc"], 1)

            exps(0)
            for n in range(NUF):
                if n % (2 * NT) == 1 and n > 2 * NT:
                    gather(act, b, n // (2 * NT) - 1)
                if n + 1 < NUF:
                    exps(n + 1)
                copy(n)
            gather(act, b, NTQ - 1)

        def gather(act, b, a):
            act.wait_ge(SF["pv"], b * NUF + (a + 1) * 2 * NT)
            if a >= 2:
                act.wait_ge(SF["wo"], b * NTQ + a - 1)
            nc.scalar.copy(TF["ao%d" % (a % 2)], ps[:, 4, :]).then_inc(SF["ao"], 1)

        def dve_F(dve, ch, b):
            dve_norm(dve, ch, b, "F", ch)
            dve_rms(dve, ch, b, 2, xn[:, :, :], yn, row["F_g1"])
            for m in range(2):
                nc.vector.memset(krz[KD - m * KD:2 * KD - m * KD, m:HKV:2, :], 0.0)
            for a in range(HKV * KD // P):
                dve.wait_ge(SF["kp"], b * 4 + 2 * a + 2)
                nc.vector.tensor_tensor(TF["t%d" % a], ps[:, 1 + 2 * a, :], rot[:, 2, :], ALU.mult)
                ch(nc.vector.tensor_tensor(TF["u%d" % a], ps[:, 2 + 2 * a, :], rot[:, 3, :], ALU.mult))
                for m in range(2):
                    r0 = m * KD
                    ins = nc.vector.tensor_tensor(krz[r0:r0 + KD, 2 * a + m, :], TF["t%d" % a][r0:r0 + KD, :],
                                                  TF["u%d" % a][r0:r0 + KD, :], ALU.add)
                ins.then_inc(SF["kr"], 1)

            def rotate(a, m):
                dve.wait_ge(SF["qp"], b * 2 * NTQ + 2 * a + m + 1)
                if a >= 2 and m == 0:
                    dve.wait_ge(SF["qr"], b * NTQ + a - 1)
                elif a < 2 and m == 0:
                    dve.wait_ge(SF["kr"], b * 2 + a + 1)
                nc.vector.tensor_tensor(TF["tu"[m] + str(a % 2)], ps[:, FQ(a, m), :], rot[:, m, :], ALU.mult)\
                    .then_inc(SF["qm"], 1)

            def top(n):
                wd = (unit(n)[1] + 1) * P
                dve.wait_ge(SF["sc"], b * NUF + n + 1)
                nc.vector.tensor_reduce(TF["nmax"][:, n % 4:n % 4 + 1], ps[:, FS(n), 0:wd], AX.X, ALU.max, negate=True)\
                    .then_inc(SF["max"], 1)

            def norm(n):
                wd = (unit(n)[1] + 1) * P
                k4 = slice(n % 4, n % 4 + 1)
                dve.wait_ge(SF["exp"], b * NUF + n + 1)
                ch(nc.vector.reciprocal(TF["rinv"][:, k4], TF["rsum"][:, k4]))
                nc.vector.tensor_scalar(TF["p%d" % (n % 2)][:, 0:wd], TF["p%d" % (n % 2)][:, 0:wd],
                                        TF["rinv"][:, k4], None, ALU.mult).then_inc(SF["nrm"], 1)

            for m in range(2):
                rotate(0, m)
            top(0)
            top(1)
            norm(0)
            for n in range(NUF):
                if n + 2 < NUF:
                    top(n + 2)
                if n < 2:
                    rotate(1, n)
                a, r = n // (2 * NT), n % (2 * NT)
                if r in (2, 5) and a + 2 < NTQ:
                    rotate(a + 2, r // 4)
                if n + 1 < NUF:
                    norm(n + 1)
            dve.wait_ge(SF["wo"], b * NTQ + NTQ)
            ch(nc.vector.tensor_tensor(xn[:, :, :], ps[:, 7, :].rearrange("p (i n) -> p i n", i=NT), xn[:, :, :], ALU.add))

        def pool_F(pool, b):
            for a in range(NTQ):
                pool.wait_ge(SF["qm"], b * 2 * NTQ + 2 * a + 2)
                if a >= 4:
                    pool.wait_ge(SF["pv"], b * NUF + (a - 3) * 2 * NT)
                nc.gpsimd.tensor_tensor(TF["q%d" % (a % 4)], TF["t%d" % (a % 2)], TF["u%d" % (a % 2)], ALU.add)\
                    .then_inc(SF["qr"], 1)

        SG = {n: sem("s_g_" + n) for n in ("gate", "d", "e2", "pre", "cum", "h", "a", "p", "hs", "y", "acc")}
        used[0] = 0
        TG = dict(**{n + str(i): cut(S) for n in ("a", "p") for i in range(2)}, h0=cut(2 * S), h1=cut(2 * S),
                  oh=cut(NT * 2 * E2), pre=cut(NT * 2 * E2))
        NC2 = HID2 // P
        NM2 = E2 * NC2

        def pe_G(pe, b):
            pe_transpose(pe, b, "G", yn)
            for i in range(NT):
                ins = nc.tensor.matmul(ps[:, 1, i * E2:(i + 1) * E2], xnT[:, i * P:(i + 1) * P], gwr[:, :],
                                       start=True, stop=True)
            ins.then_inc(SG["gate"], 1)

            def hidden(e):
                for j in range(NC2):
                    m = e * NC2 + j
                    if m >= 2:
                        pe.wait_ge(SG["a"], b * NM2 + m - 1)
                    nc.tensor.matmul(ps[:, 2 + m % 2, :], gw2[:, e, j * P:(j + 1) * P], xnT[:, :],
                                     start=True, stop=True).then_inc(SG["h"], 1)
                    if m >= 2:
                        pe.wait_ge(SG["p"], b * NM2 + m - 1)
                    nc.tensor.matmul(ps[:, 4 + m % 2, :], gw1[:, e, j * P:(j + 1) * P], xnT[:, :],
                                     start=True, stop=True).then_inc(SG["h"], 1)

            hidden(0)
            hidden(1)
            pe.wait_ge(SG["pre"], b + 1)
            for i in range(NT):
                o = ps[:, 1, 64 + i * 2 * E2:64 + (i + 1) * 2 * E2]
                at = slice(i * 2 * E2, (i + 1) * 2 * E2)
                nc.tensor.matmul(o, c["tri"], TG["oh"][:, at], start=True, stop=False)
                ins = nc.tensor.matmul(o, c["ones"], TG["pre"][:, at], start=False, stop=True)
            ins.then_inc(SG["cum"], 1)
            for e in range(E2):
                if 1 <= e < E2 - 1:
                    hidden(e + 1)
                pe.wait_ge(SG["hs"], b * NM2 + (e + 1) * NC2)
                if e >= 2:
                    pe.wait_ge(SG["acc"], b * E2 + e - 1)
                for i in range(NT):
                    for j in range(NC2):
                        ins = nc.tensor.matmul(ps[:, 6 + e % 2, i * P:(i + 1) * P],
                                               TG["h%d" % (e % 2)][:, j * S + i * P:j * S + (i + 1) * P],
                                               gw3[:, e * NC2 + j, :], start=(j == 0), stop=(j == NC2 - 1))
                ins.then_inc(SG["y"], 1)

        def act_G(act, b):
            act_root(act, b, "G", then=ACT.Exp)
            act_transpose(act, b, "G")

            def linear(m):
                act.wait_ge(SG["h"], b * 2 * NM2 + 2 * m + 1)
                if m >= 2:
                    act.wait_ge(SG["p"], b * NM2 + m - 1)
                nc.scalar.copy(TG["a%d" % (m % 2)], ps[:, 2 + m % 2, :]).then_inc(SG["a"], 1)

            linear(0)
            linear(1)
            act.wait_ge(SG["d"], b + 1)
            nc.scalar.activation(gs["e2"][:, :], gs["t1"][:, :], ACT.Exp).then_inc(SG["e2"], 1)
            nc.scalar.activation(warm[:, 19:20], c["ones"][:, 0:1], ACT.Gelu)
            for m in range(NM2):
                if 1 <= m < NM2 - 1:
                    linear(m + 1)
                e = m // NC2
                if m % NC2 == 0 and e >= 2:
                    act.wait_ge(SG["y"], b * E2 + e - 1)
                act.wait_ge(SG["p"], b * NM2 + m + 1)
                nc.scalar.activation(TG["h%d" % (e % 2)][:, m % NC2 * S:(m % NC2 + 1) * S], TG["p%d" % (m % 2)],
                                     ACT.Gelu).then_inc(SG["hs"], 1)

        def dve_G(dve, ch, b):
            V = nc.vector
            dve_rms(dve, ch, b, 3, xn[:, :, :], yn, row["F_g2"])
            ch(nc.vector.tensor_tensor(x[:, :, :], x[:, :, :], xn[:, :, :], ALU.add))
            dve.wait_ge(SG["gate"], b + 1)
            lg, oh1, oh2, pos, junk, sel = (gt[n][:, :, :] for n in ("logit", "oh1", "oh2", "pos", "junk", "sel"))
            S_ = {n: a[:, :] for n, a in gs.items()}
            wide = lambda a: a.unsqueeze(2).to_broadcast([P, NT, E2])
            ohk = TG["oh"].rearrange("p (i k e) -> p i k e", i=NT, k=2)
            pre = TG["pre"].rearrange("p (i n) -> p i n", i=NT)
            def product(m):
                dve.wait_ge(SG["a"], b * NM2 + m + 1)
                dve.wait_ge(SG["h"], b * 2 * NM2 + 2 * m + 2)
                if m >= 2:
                    dve.wait_ge(SG["hs"], b * NM2 + m - 1)
                V.tensor_tensor(TG["p%d" % (m % 2)], ps[:, 4 + m % 2, :], TG["a%d" % (m % 2)], ALU.mult)\
                    .then_inc(SG["p"], 1)

            product(0)
            product(1)
            ch(V.tensor_tensor(lg, ps[:, 1, 0:NT * E2].rearrange("p (i e) -> p i e", i=NT),
                               row["G_rb"][:, 0:E2].unsqueeze(1).to_broadcast([P, NT, E2]), ALU.add))
            dve_first(ch, lg, gs["m1"], oh1)
            ch(V.tensor_scalar(junk, oh1, -3e38, None, ALU.mult))
            ch(V.tensor_tensor(junk, junk, lg, ALU.add))
            dve_first(ch, junk, gs["m2"], oh2)
            V.tensor_tensor(S_["t1"], S_["m2"], S_["m1"], ALU.subtract).then_inc(SG["d"], 1)
            V.tensor_copy(ohk[:, :, 0, :], oh1)
            ch(V.tensor_copy(ohk[:, :, 1, :], oh2))
            ch(V.tensor_copy(pre[:, 0, :], ohsum[:, :]))
            for i in range(NT):
                o = pre[:, i + 1, :] if i + 1 < NT else ohsum[:, :]
                ins = V.tensor_tensor(o, pre[:, i, :], ohk[:, i, :, :].rearrange("p k e -> p (k e)"), ALU.add)
                if i + 1 < NT:
                    ch(ins)
            ins.then_inc(SG["pre"], 1)

            product(2)
            product(3)
            dve.wait_ge(SG["e2"], b + 1)
            ch(V.tensor_scalar(S_["t1"], S_["e2"], 1.0, None, ALU.add))
            ch(V.reciprocal(S_["s1"], S_["t1"]))
            ch(V.tensor_tensor(S_["s2"], S_["e2"], S_["s1"], ALU.mult))
            dve.wait_ge(SG["cum"], b + 1)
            cum = ps[:, 1, 64:64 + NT * 2 * E2].rearrange("p (i k e) -> p i k e", i=NT, k=2)
            ch(V.tensor_copy(pos, cum[:, :, 0, :]))
            ch(V.tensor_tensor(junk, pos, cum[:, :, 1, :], ALU.add))
            ch(V.tensor_scalar(pos, pos, float(CAP), None, ALU.is_lt))
            ch(V.tensor_tensor(oh1, oh1, pos, ALU.mult))
            ch(V.tensor_scalar(junk, junk, float(CAP), None, ALU.is_lt))
            ch(V.tensor_tensor(oh2, oh2, junk, ALU.mult))
            idx = row["index"][:, 0:E2].unsqueeze(1).to_broadcast([P, NT, E2])
            ch(V.tensor_reduce(S_["t1"], oh1, AX.X, ALU.add))
            ch(V.tensor_reduce(S_["t2"], oh2, AX.X, ALU.add))
            ch(V.tensor_tensor(oh1, oh1, idx, ALU.mult))
            ch(V.tensor_tensor(oh2, oh2, idx, ALU.mult))
            ch(V.tensor_reduce(S_["a1"], oh1, AX.X, ALU.add))
            ch(V.tensor_reduce(S_["a2"], oh2, AX.X, ALU.add))
            ch(V.tensor_tensor(S_["a1"], S_["a1"], S_["a2"], ALU.max))
            ch(V.tensor_tensor(S_["cy"], S_["s1"], S_["t1"], ALU.mult))
            ch(V.tensor_tensor(S_["a2"], S_["s2"], S_["t2"], ALU.mult))
            ch(V.tensor_tensor(S_["s1"], S_["s1"], S_["cy"], ALU.subtract))
            ch(V.tensor_tensor(S_["s2"], S_["s2"], S_["a2"], ALU.subtract))
            ch(V.tensor_tensor(S_["cy"], S_["cy"], S_["a2"], ALU.add))
            ch(V.tensor_tensor(S_["cz"], S_["s1"], S_["s2"], ALU.add))
            ch(V.tensor_tensor(sel, idx, wide(S_["a1"]), ALU.is_equal))
            ch(V.tensor_tensor(sel, sel, wide(S_["cy"]), ALU.mult))
            for i in range(NT):
                ins = V.scalar_tensor_tensor(x[:, i, :], yn[:, i, :], gs["cz"][:, i:i + 1], x[:, i, :], ALU.mult, ALU.add)
            ch(ins)
            for e in range(E2):
                for m in range(NC2 * (e + 1), NC2 * (e + 2)):
                    if 4 <= m < NM2:
                        product(m)
                dve.wait_ge(SG["y"], b * E2 + e + 1)
                for i in range(NT):
                    o = x[:, i, :] if e + 1 < E2 else x4[:, bass.ds(b * S + i * P, P)]
                    ins = V.scalar_tensor_tensor(o, ps[:, 6 + e % 2, i * P:(i + 1) * P],
                                                 sel[:, i, e:e + 1], x[:, i, :], ALU.mult, ALU.add)
                ins.then_inc(SG["acc"], 1)
                dve.wait_ge(SG["acc"], b * E2 + e + 1)

        block = ctx.enter_context(nc.Block())
        GROUPS = [["sqc", "sqw_a", "colb", "rowb", "amask_in", "kmask_in", "xmask_in", "dec_row", "dec_col"],
                  ["sqw_b", "vmask"], ["cwg", "cw1", "cw2", "cb2"], ["rmask", "rk", "rv"],
                  ["fwq", "fwk", "fwv", "fwo", "rot", "gwr", "gw1", "gw2", "gw3"]]
        tiles = dict(sqw_a=sqw[:, 0:4, :], sqw_b=sqw[:, 4:len(SQW), :], sqc=sqc, colb=colb, rowb=rowb, dec_row=dec_row,
                     dec_col=dec_col, vmask=vmask, rmask=rmask, xmask_in=xmask_in, amask_in=amask_in, kmask_in=kmask_in, rk=rk, rv=rv,
                     cwg=cwg, cw1=cw1, cw2=cw2, cb2=cb2, fwq=fwq, fwk=fwk, fwv=fwv, fwo=fwo, rot=rot, gwr=gwr,
                     gw1=gw1, gw2=gw2, gw3=gw3)

        @block.sync
        def _(sp):
            def load_ctx(b, ph):
                for a in range(2):
                    sp.dma_start(ctxT[:, a, :], t["ctxT"][b:b + 1].rearrange("o d k -> d (o k)"))\
                        .then_inc(SH[ph]["ctx"], 16)

            def load_x(b):
                sp.dma_start(xin[:, :, :], t["x"][b:b + 1].rearrange("o (t p) d -> p (o t) d", p=P))\
                    .then_inc(SH[0]["x"], 16)

            load_x(0)
            load_ctx(0, 0)
            for names, landed in zip(GROUPS, s_const):
                for name in names:
                    if name in ("rowb", "kmask_in"):
                        src = t[name].unsqueeze(0).to_broadcast([P] + list(t[name].shape))
                    else:
                        src = t[name]
                    dst = tiles[name]
                    sp.dma_start(dst[tuple(slice(None) for _ in dst.shape)], src).then_inc(landed, 16)
            for b in range(B):
                if b + 1 < B:
                    sp.wait_ge(SH[0]["xn"], (b * NLN[0] + DH["B"][1]) * NT + 1)
                    load_x(b + 1)
                    load_ctx(b + 1, 0)
                sp_D0(sp, b)
            sp_D_load(sp, 0)
            load_ctx(0, 1)
            sp_D_load(sp, 1)
            for b in range(B):
                sp_D_store(sp, b)
                if b + 2 < B:
                    sp_D_load(sp, b + 2)
            for b in range(B):
                sp_D1(sp, b)
            for b in range(B):
                if b + 1 < B:
                    sp.wait_ge(XA["E"]["kv"], b * 2 + 2)
                    load_ctx(b + 1, 1)
                if last == "G":
                    sp.wait_ge(SG["acc"], b * E2 + E2)
                else:
                    sp.wait_ge(s_xout, b + 1)
                sp.dma_start(out[b:b + 1].rearrange("o (t p) d -> p (o t) d", p=P),
                             x4[:, b * S:(b + 1) * S].rearrange("p (i n) -> p i n", i=NT)).then_inc(s_store, 16)
            sp.wait_ge(s_store, B * 16)

        @block.tensor
        def _(pe):
            pe.wait_ge(s_const[0], 16 * len(GROUPS[0]))
            pe.wait_ge(s_zero, 1)
            pe.wait_ge(s_prep, 1)
            pe.wait_ge(s_const[1], 16 * len(GROUPS[1]))
            with pe.Fori(0, B) as b:
                pe_A(pe, b)
                pe_X(pe, b, "B")
                pe.wait_ge(s_const[2], 16 * len(GROUPS[2]))
                pe_C(pe, b)
                pe_D0(pe, b)
            pe.wait_ge(s_const[3], 16 * len(GROUPS[3]))
            with pe.Fori(0, B // 2) as bb:
                for s in range(2):
                    pe_D(pe, 2 * bb + s, s)
            pe.wait_ge(s_const[4], 16 * len(GROUPS[4]))
            with pe.Fori(0, B) as b:
                pe_D1(pe, b)
                if "E" in stages:
                    pe_X(pe, b, "E")
                if "F" in stages:
                    pe_F(pe, b)
                if "G" in stages:
                    pe_G(pe, b)

        @block.scalar
        def _(act):
            act.wait_ge(s_const[0], 16 * len(GROUPS[0]))
            with act.Fori(0, B) as b:
                act_A(act, b)
                act_X(act, b, "B")
                act_C(act, b)
                act_D0(act, b)
            act.wait_ge(s_const[3], 16 * len(GROUPS[3]))
            with act.Fori(0, B // 2) as bb:
                for s in range(2):
                    act_D(act, 2 * bb + s, s)
            with act.Fori(0, B) as b:
                act_X_keys(act, b, "E")
                if "E" in stages:
                    act_X(act, b, "E")
                if "F" in stages:
                    act_F(act, b)
                if "G" in stages:
                    act_G(act, b)

        @block.vector
        def _(dve):
            dve.wait_ge(s_const[0], 16 * len(GROUPS[0]))
            nc.vector.tensor_copy(identb[:, :], c["ident"])
            nc.vector.tensor_copy(causal[:, :], c["causal"])
            for r in range(REP):
                nc.vector.tensor_copy(xmask[:, :, r * KP:(r + 1) * KP], xmask_in)
            nc.vector.memset(amask[:, :, KS:KP], MASKED)
            nc.vector.memset(kmask[:, :, KS:KP], MASKED)
            nc.vector.tensor_scalar(amask[:, :, 0:KS], amask_in[:, :, :], MASKED, None, ALU.mult)
            nc.vector.tensor_scalar(kmask[:, :, 0:KS], kmask_in[:, :, :], MASKED, None, ALU.mult).then_inc(s_prep, 1)
            dve.wait_ge(s_prep, 1)
            dve.wait_ge(s_zero, 1)
            ch = Chain(dve, SH[0]["ch"], CH["first"])
            with dve.Fori(0, B) as b:
                ch.turn(b)
                dve.wait_ge(SH[0]["x"], b * 16 + 16)
                dve_A(dve, ch, b)
                dve_X(dve, ch, b, "B")
                dve_C(dve, ch, b)
                dve_D0(dve, ch, b)
                ch.end()
            dve.wait_ge(s_const[3], 16 * len(GROUPS[3]))
            with dve.Fori(0, B // 2) as bb:
                for s in range(2):
                    dve_D(dve, 2 * bb + s, s)
            dve.wait_ge(s_const[4], 16 * len(GROUPS[4]))
            ch = Chain(dve, SH[1]["ch"], CH[last])
            with dve.Fori(0, B) as b:
                ch.turn(b)
                dve_D1(dve, ch, b)
                if "E" in stages:
                    dve_X(dve, ch, b, "E")
                if "F" in stages:
                    dve_F(dve, ch, b)
                if "G" in stages:
                    dve_G(dve, ch, b)
                if last != "G":
                    nc.vector.tensor_copy(tmp[:, 0:1], x[:, 0, 0:1]).then_inc(s_xout, 1)
                ch.end()

        @block.gpsimd
        def _(pool):
            pool.wait_ge(s_const[0], 16 * len(GROUPS[0]))
            nc.gpsimd.memset(onehot[:, :, :], 0.0).then_inc(SD["sc"], 2)
            nc.gpsimd.memset(ohsum[:, :], 0.0).then_inc(SD["pv"], 2)
            nc.gpsimd.memset(ai[:, :, :], 0.0).then_inc(s_zero, 1)
            nc.gpsimd.memset(spare2[:, 0:1], 0.0).then_inc(SD["y"], 2)
            nc.gpsimd.memset(spare2[:, 1:2], 0.0).then_inc(SD["spill"], 64)
            pool.wait_ge(s_const[1], 16 * len(GROUPS[1]))
            with pool.Fori(0, B) as b:
                pool_X(pool, b, "B")
            with pool.Fori(0, B // 2) as bb:
                for s in range(2):
                    pool_D(pool, 2 * bb + s, s)
            with pool.Fori(0, B) as b:
                pool_D1(pool, b)
                if "E" in stages:
                    pool_X(pool, b, "E")
                if "F" in stages:
                    pool_F(pool, b)


CH = {"first": 71, "D": 2, "E": 55, "F": 130, "G": 174}


def arrays_of(inputs):
    import numpy as np

    g = {k: np.asarray(v) for k, v in inputs.items()}
    f = np.float32
    d = {}
    d["x"] = g["x"]
    ctxT = np.zeros((B, P, KP), f)
    ctxT[:, :, :KS] = g["ctx_1024"].transpose(0, 2, 1)
    d["ctxT"] = ctxT
    sq = {"A_q": g["L0_attn_W_q"].T, "A_k": g["L0_attn_W_k"].T, "A_v": g["L0_attn_W_v"].T, "A_o": g["L0_attn_W_o"].T}
    for k, n, tr in (("B", "L0_xattn", True), ("D", "L1_attn", True), ("E", "L1_xattn", False)):
        for m in "qkvo":
            a = g[f"{n}_W{m}"]
            sq[f"{k}_{m}"] = a.T if tr else a
    sqw = np.stack([sq[n] for n in SQW], 1)
    d["sqw_a"], d["sqw_b"] = sqw[:, :4], sqw[:, 4:]
    r = np.arange(P)
    con = {"ident": np.eye(P), "block": r[:, None] // DK == r[None] // DK,
           "mask_i": (r[:, None] // DK == r[None] % DK) & (r[:, None] < 64),
           "tri": r[:, None] <= r[None], "ones": np.ones((P, P)),
           "causal": np.where(r[:, None] < r[None], MASKED, 0.0)}
    d["sqc"] = np.stack([con[n] for n in SQC], 1).astype(f)
    names = {"A": "L0_attn_b_", "B": "L0_xattn_b", "D": "L1_attn_b", "E": "L1_xattn_b"}
    vec = {f"{k}_b{m}": g[names[k] + m] for k in names for m in "qkvo"}
    d["colb"] = np.concatenate([np.stack([vec[n] for n in COLB], 1),
                                g["L0_ffn_b1"].reshape(-1, P).T], 1)
    rb = np.zeros(P, f)
    rb[:E2] = g["L1_ffn_router_b"]
    vec.update(F_g1=g["L1_ffn_g1"], F_g2=g["L1_ffn_g2"], G_rb=rb, rank=(E1 - r).astype(f), index=r.astype(f))
    d["rowb"] = np.stack([vec[n] for n in ROWB], 0)
    dec = np.exp(-np.arange(S, dtype=f) / S).astype(f)
    d["dec_row"] = np.broadcast_to(dec, (P, S))
    d["dec_col"] = dec.reshape(NT, P).T
    vm = np.zeros((P, NPER, P + 96), f)
    for j in range(NPER):
        at = j * P + r
        vm[:, j, 96:] = ((at // KP)[:, None] == (r // DK)[None]) & ((at % KP) < KS)[:, None]
    d["vmask"] = vm
    rm = np.zeros((P, P + 64), f)
    rm[:, :P] = con["block"]
    rm[:, P:] = (r % DK)[:, None] == (np.arange(64) // DK)[None]
    d["rmask"] = rm
    q = np.arange(S)
    xm = np.full((S, KP), MASKED, f)
    xm[:, :KS] = np.where(np.arange(KS)[None] > q[:, None], MASKED, 0.0)
    d["xmask_in"] = xm.reshape(NT, P, KP).transpose(1, 0, 2)
    d["amask_in"] = g["mask_SxS2_bk1"].astype(np.int32).reshape(NT, P, KS).transpose(1, 0, 2)
    d["kmask_in"] = g["mask_BxS2_bf0"].astype(np.int32)
    M = (len(g["L1_attn_rel_k"]) - 1) // 2
    dist = NU * np.arange(DK)[:, None] + (NU - 1) - np.arange(RELW)[None]
    rk = np.zeros((P, RELW), f)
    rk[:DK * DK] = g["L1_attn_rel_k"][np.clip(dist, -M, M) + M].transpose(0, 2, 1).reshape(DK * DK, RELW)
    d["rk"] = rk
    dist = np.arange(RVS)[None] - r[:, None] - (S - P)
    d["rv"] = g["L1_attn_rel_v"][np.clip(dist, -M, M) + M].reshape(P, RVS * DK)
    d["cwg"] = g["L0_ffn_Wg"].T
    d["cw1"] = g["L0_ffn_W1"].transpose(1, 0, 2)
    d["cw2"] = g["L0_ffn_W2"].reshape(-1, P, P).transpose(1, 0, 2)
    cb2 = np.zeros((P, P), f)
    cb2[:E1] = g["L0_ffn_b2"]
    d["cb2"] = cb2
    half = KD // 2
    swap = lambda a: a.reshape(P, -1, 2, half)[:, :, ::-1].reshape(P, -1)
    d["fwq"] = np.stack([g["L1_ffn_wq"], swap(g["L1_ffn_wq"])], 1)
    d["fwk"] = np.stack([g["L1_ffn_wk"], swap(g["L1_ffn_wk"])], 1)
    d["fwv"] = g["L1_ffn_wv"]
    d["fwo"] = g["L1_ffn_wo"].reshape(-1, P, P).transpose(1, 0, 2)
    th = 10000.0 ** (-np.arange(0, KD, 2, dtype=f) / KD)
    tick = np.tile(np.outer(np.arange(S, dtype=f), th), (1, 2)).astype(f).T
    sign = np.where(np.arange(KD) < half, -1.0, 1.0)[:, None].astype(f)
    cos, sin = np.cos(tick), np.sin(tick) * sign
    two = lambda a: np.concatenate([a, a], 0)
    d["rot"] = np.stack([two(cos) / 8, two(sin) / 8, two(cos), two(sin)], 1).astype(f)
    d["gwr"] = g["L1_ffn_router_w"]
    for n in ("1", "2"):
        d["gw" + n] = g["L1_ffn_w" + n].transpose(1, 0, 2)
    d["gw3"] = g["L1_ffn_w3"].reshape(-1, P, P).transpose(1, 0, 2)
    return {k: np.ascontiguousarray(v) for k, v in d.items()}


def program(nc, arrays, last="G"):
    t = {n: nc.dram_tensor(f"in_{n}", a.shape, mybir.dt.from_np(a.dtype), kind="ExternalInput").ap()
         for n, a in arrays.items()}
    out = nc.dram_tensor("out", (B, S, P), F32, kind="ExternalOutput").ap()
    decoder(nc, t, out, last)


def kernel(**inputs):
    import concourse.bacc as _bacc
    from concourse.bass_utils import run_bass_kernel_spmd as _run

    arrays = arrays_of(inputs)
    nc = _bacc.Bacc("TRN2", target_bir_lowering=False, num_devices=1)
    program(nc, arrays)
    r = _run(nc, [{f"in_{n}": a for n, a in arrays.items()}], core_ids=[0])
    return r.results[0]["out"]
```

```python
from contextlib import ExitStack

import concourse.bass as bass
from concourse import mybir

ALU = mybir.AluOpType
ACT = mybir.ActivationFunctionType
AX = mybir.AxisListType
F32 = mybir.dt.float32
BF16 = mybir.dt.bfloat16

P = 128
B = 4
S = 512
NT = S // P
H = 16
DK = P // H
KS = 154
KP = 160
REP = 4
HALF = H // 2 * KP
NCH = HALF // P
NPER = KP // 32
VH = P // 2
VW = VH + H // 2
MASKED = -1e30
LN_EPS = 1e-5
ATT_EPS = 1e-6
RMS_EPS = 1e-6
E1, HID1 = 8, 512
E2, HID2 = 8, 256
CAP = B * S // 8
HQ, HKV, KD = 16, 4, 64
NG = HQ // HKV
NU = S // DK
REL0 = S - P - DK * (NU // 2 - P // DK)
RELW = S - DK
RVS = S - P + S
SOFT = 1.0 / DK ** 0.5

COLB = ["A_bq", "B_bq", "B_bk", "D_bq", "D_bk", "E_bq", "E_bk"]
ROWB = ["A_bk", "A_bv", "A_bo", "B_bv", "B_bo", "D_bv", "D_bo", "E_bv", "E_bo", "F_g1", "F_g2", "G_rb", "rank", "index"]
SQW = ["A_q", "A_k", "A_v", "A_o", "B_q", "B_k", "B_v", "B_o", "D_q", "D_k", "D_v", "D_o", "E_q", "E_k", "E_v", "E_o"]
SQC = ["ident", "block", "mask_i", "tri", "ones", "causal"]


class Chain:

    def __init__(self, eng, sem, per_turn):
        self.eng, self.sem, self.per_turn = eng, sem, per_turn
        self.parts = []

    def turn(self, index):
        self.base, self.n = index * self.per_turn, 0

    def __call__(self, ins):
        self.n += 1
        ins.then_inc(self.sem, 1)
        self.eng.wait_ge(self.sem, self.base + self.n)

    def mark(self, ins):
        self.n += 1
        ins.then_inc(self.sem, 1)
        return self.n

    def wait(self, n):
        self.eng.wait_ge(self.sem, self.base + n)

    def end(self):
        assert self.n == self.per_turn, (self.n, self.per_turn)


def decoder(nc, t, out, last="G"):
    stages = "ABCDEFG"[: "ABCDEFG".index(last) + 1]
    NX3 = len(stages) - 4
    ctx = ExitStack()
    with ctx:
        def sb(name, shape, dt=F32):
            return ctx.enter_context(nc.sbuf_tensor(name, shape, dt))

        def sem(name):
            return ctx.enter_context(nc.semaphore(name))

        ps = ctx.enter_context(nc.psum_tensor("ps", [P, 8, 512], F32))

        sqw = sb("sqw", [P, len(SQW), P])
        w = {n: sqw[:, i, :] for i, n in enumerate(SQW)}
        sqc = sb("sqc", [P, len(SQC), P])
        c = {n: sqc[:, i, :] for i, n in enumerate(SQC)}
        colb = sb("colb", [P, len(COLB) + E1 * HID1 // P])
        rowb = sb("rowb", [P, len(ROWB), P])
        row = {n: rowb[:, i, :] for i, n in enumerate(ROWB)}
        identb = sb("identb", [P, P], BF16)
        causal = sb("causal", [P, P], BF16)
        dec_row = sb("dec_row", [P, S])
        dec_col = sb("dec_col", [P, NT])
        vmask = sb("vmask", [P, NPER, P + 96])
        rmask = sb("rmask", [P, P + 64])
        xmask = sb("xmask", [P, NT, REP * KP], BF16)
        amask = sb("amask", [P, NT, KP], BF16)
        kmask = sb("kmask", [P, B, KP], BF16)
        rk = sb("rk", [P, 2, RELW])
        rkc = sb("rkc", [P, 2])
        rvc = sb("rvc", [P, 2, DK])
        rv = sb("rv", [P, RVS * DK])
        cwg = sb("cwg", [P, E1])
        cw1 = sb("cw1", [P, E1, HID1])
        cw2 = sb("cw2", [P, E1 * HID1 // P, P])
        cb2 = sb("cb2", [P, P])
        fwq = sb("fwq", [P, 2, HQ * KD])
        fwk = sb("fwk", [P, 2, HKV * KD])
        fwv = sb("fwv", [P, HKV * KD])
        fwo = sb("fwo", [P, HQ * KD // P, P])
        rot = sb("rot", [P, 4, S])
        gwr = sb("gwr", [P, E2])
        gw1 = sb("gw1", [P, E2, HID2])
        gw2 = sb("gw2", [P, E2, HID2])
        gw3 = sb("gw3", [P, E2 * HID2 // P, P])

        x = sb("x", [P, NT, P])
        xn = sb("xn", [P, NT, P])
        xnT = sb("xnT", [P, S])
        stats = sb("stats", [P, NT, 6])
        mv = sb("mv", [P, NT, 2])
        var = sb("var", [P, NT])
        root = sb("root", [P, NT])
        spare = sb("spare", [P, 2])
        spare2 = sb("spare2", [P, 2])
        warm = sb("warm", [P, 20])
        rstd = sb("rstd", [P, NT])
        aoT = sb("aoT", [P, S])
        q_t = sb("q_t", [P, S])
        tmp = sb("tmp", [P, S])
        ctxT = sb("ctxT", [P, 2, KP])
        onehot = sb("onehot", [P, NT, P])
        ohsum = sb("ohsum", [P, 2 * E2])

        ARENA = 11296
        arena = sb("arena", [P, ARENA])
        used = [0]

        def cut(n):
            used[0] += n
            assert used[0] <= ARENA, used[0]
            return arena[:, used[0] - n:used[0]]

        amask_in, kmask_in = (cut(NT * KS).bitcast(mybir.dt.int32).rearrange("p (t k) -> p t k", k=KS) for _ in range(2))

        xmask_in = cut(NT * KP).rearrange("p (t k) -> p t k", k=KP)

        s_const = [sem("s_const%d" % i) for i in range(5)]
        s_prep = sem("s_prep")
        s_zero = sem("s_zero")
        SH = [{n: sem(f"s_{n}{i}") for n in ("x", "ctx", "xn", "var", "root", "tr", "xT", "ch", "wo")} for i in range(2)]
        s_store = sem("s_store")
        s_xout = sem("s_xout")
        NLN = (4, NX3)
        NNORM = (4, [0, 1, 3, 4][NX3])
        NWO = (2, 1 + (NX3 > 0))
        DH = dict(A=(0, 0), B=(0, 1), C=(0, 2), D=(0, 3), E=(1, 0), F=(1, 1), G=(1, 2))

        s_aq, s_akv, s_aqr, s_akvr, s_akvp, s_abd, s_aout, s_aao, s_aT, s_aTc = map(sem, (
            "s_aq", "s_akv", "s_aqr", "s_akvr", "s_akvp", "s_abd", "s_aout", "s_aao",
            "s_aT", "s_aTc"))
        XA = {}
        for k in "BE":
            XA[k] = {n: sem(f"s_{k}_{n}") for n in (
                "kv", "kt", "vrep", "kbd", "vs", "qp", "qt", "mask", "sc", "sub", "exp", "pt", "ptc", "pv", "o", "aT", "aTc")}

        NXH = 2 * NT

        used[0] = 0
        TX = dict(kt=cut(KP), kbd=cut(H * KP), vs=cut(2 * NCH * VW), vrep=cut(NPER * P), bmask=cut(NT * REP * KP // 2),
                  m=cut(2 * 8), r=cut(2 * 8), g=cut(2 * 8), ao=cut(S))
        X_KEEP = used[0]
        TX.update(d0=cut(HALF), d1=cut(HALF), pt=cut(HALF))
        X_END = used[0]
        xin = cut(NT * P).rearrange("p (i n) -> p i n", i=NT)
        bmask = TX["bmask"].bitcast(BF16).rearrange("p (t n) -> p t n", t=NT)
        vs = TX["vs"].rearrange("p (c n) -> p c n", c=2 * NCH)

        AW = P + H
        used[0] = X_KEEP
        TA = dict(qf=cut(S), kf=cut(S), v1=cut(NT * AW), bd=cut(AW), den=cut(NT * H), ao=cut(S))
        assert used[0] <= X_END

        FILL = dict(A=(8, 0), B=(14, 0), C=(14, 0), D=(14, 0), E=(14, 4), F=(24, 0), G=(14, 0))

        def pe_transpose(pe, b, k, src=xn):
            ph, g = DH[k]
            s = SH[ph]
            for _ in range(FILL[k][0]):
                nc.tensor.matmul(ps[:, FILL[k][1], :], identb[:, :], xmask[:, 0, 0:512], start=True, stop=True)
            for i in range(NT):
                pe.wait_ge(s["xn"], b * (NLN[ph] * NT) + g * NT + i + 1)
                ins = nc.tensor.transpose(ps[:, 0, i * P:(i + 1) * P], src[:, i, :], c["ident"])
            ins.then_inc(s["tr"], 1)
            pe.wait_ge(s["xT"], b * NLN[ph] + g + 1)

        def act_transpose(act, b, k):
            ph, g = DH[k]
            act.wait_ge(SH[ph]["tr"], b * NLN[ph] + g + 1)
            nc.scalar.copy(xnT[:, :], ps[:, 0, :]).then_inc(SH[ph]["xT"], 1)

        def dve_norm(dve, ch, b, k, keep=None, src=x):
            ph, g = DH[k]
            s = SH[ph]
            landed = []
            for i in range(NT):
                if ch.parts and i % 2 == 0:
                    ch.wait(ch.parts[i // 2])
                landed.append(ch.mark(nc.vector.bn_stats(stats[:, i, :], src[:, i, :])))
            ch.parts = []
            for i in range(NT):
                if i in (0, NT - 1):
                    ch.wait(landed[max(i, NT - 2)])
                    nc.vector.memset(spare[:, i % 2:i % 2 + 1], 0.0)
                ins = nc.vector.bn_aggr(mv[:, i, :], stats[:, i, :])
            ch(ins)
            nc.vector.tensor_scalar(var[:, :], mv[:, :, 1], LN_EPS, None, ALU.add).then_inc(s["var"], 1)
            dve.wait_ge(s["root"], b * NNORM[ph] + g + 1)
            ch(nc.vector.reciprocal(rstd[:, :], root[:, :]))
            for i in range(NT):
                ins = nc.vector.tensor_scalar(xn[:, i, :], src[:, i, :], mv[:, i, 0:1], rstd[:, i:i + 1],
                                        ALU.subtract, ALU.mult)
                if keep is None:
                    ins.then_inc(s["xn"], 1)
            if keep is not None:
                keep(ins)

        def act_root(act, b, k, second=0, then=None):
            ph, g = DH[k]
            g += second + (k == "G")
            nc.scalar.activation(warm[:, 2 * (ph * 5 + g):2 * (ph * 5 + g) + 1], c["ones"][:, 0:1], ACT.Sqrt)
            act.wait_ge(SH[ph]["var"], b * NNORM[ph] + g + 1)
            nc.scalar.activation(root[:, :], var[:, :], ACT.Sqrt).then_inc(SH[ph]["root"], 1)
            if then is not None:
                nc.scalar.activation(warm[:, 2 * (ph * 5 + g) + 1:2 * (ph * 5 + g) + 2], c["ones"][:, 0:1], then)

        OB = {(0, 0): 7, (0, 1): 7, (1, 0): 0, (1, 1): 7}

        def pe_project(pe, b, ph, g, wo):
            for i in range(NT):
                nc.tensor.matmul(ps[:, OB[ph, g], i * P:(i + 1) * P], aoT[:, i * P:(i + 1) * P], wo,
                                 start=False, stop=True, skip_group_check=True).then_inc(SH[ph]["wo"], 1)

        def pe_bias(ph, g, bo):
            nc.tensor.matmul(ps[:, OB[ph, g], :].rearrange("p (i n) -> p i n", i=NT), c["ones"][0:1, :],
                             row[bo][0:1, :].unsqueeze(1).to_broadcast([1, NT, P]), start=True, stop=False,
                             skip_group_check=True)

        def dve_residual(dve, ch, b, ph, g, src=x):
            dve.wait_ge(SH[ph]["wo"], b * NWO[ph] * NT + (g + 1) * NT)
            for z in (slice(0, 2), slice(2, 4)):
                ch.parts.append(ch.mark(nc.vector.tensor_tensor(
                    x[:, z, :], ps[:, OB[ph, g], :].rearrange("p (a n) -> p a n", a=NT)[:, z, :], src[:, z, :], ALU.add)))

        def pe_A(pe, b):
            pe_X_context(pe, b, "B")
            pe_transpose(pe, b, "A")
            nc.tensor.matmul(ps[:, 1, :], w["A_q"], xnT[:, :], start=True, stop=True).then_inc(s_aq, 1)
            for i in range(NT):
                o = ps[:, 2 + i // 2, (i % 2) * 256:(i % 2) * 256 + 256]
                nc.tensor.matmul(o, xnT[:, i * P:(i + 1) * P], sqw[:, 1:3, :].rearrange("p a n -> p (a n)"),
                                 start=True, stop=True).then_inc(s_akv, 1)
            pe.wait_ge(XA["B"]["kt"], b + 1)
            pe.wait_ge(XA["B"]["vrep"], b + 1)
            for i in range(NT):
                pe.wait_ge(s_akvr, b * NT + i + 1)
                ins = nc.tensor.matmul(ps[:, 4, 0:AW], TA["kf"][:, i * P:(i + 1) * P],
                                       TA["v1"][:, i * AW:(i + 1) * AW], start=(i == 0), stop=(i == NT - 1))
            ins.then_inc(s_akvp, 1)
            pe_bias(0, 0, "A_bo")
            pe.wait_ge(s_abd, b * 3 + 3)
            for i in range(NT):
                o = ps[:, 5 + i // 2, (i % 2) * 256:(i % 2) * 256 + AW]
                ins = nc.tensor.matmul(o, TA["qf"][:, i * P:(i + 1) * P], TA["bd"], start=True, stop=True)
            ins.then_inc(s_aout, 1)
            for i in range(NT):
                pe.wait_ge(s_aao, b * NT + i + 1)
                ins = nc.tensor.transpose(ps[:, 1, i * P:(i + 1) * P], TA["ao"][:, i * P:(i + 1) * P], c["ident"])
            ins.then_inc(s_aT, 1)
            pe.wait_ge(s_aTc, b + 1)
            pe_project(pe, b, 0, 0, w["A_o"])

        def act_A(act, b):
            act_root(act, b, "A")
            act_X_keys(act, b, "B")
            act_transpose(act, b, "A")
            act.wait_ge(SD["spill"], b * 64 + 64)
            act.wait_ge(s_aq, b + 1)
            nc.scalar.activation(q_t[:, :], ps[:, 1, :], ACT.Relu, bias=colb[:, 0:1]).then_inc(s_aqr, 1)
            act.wait_ge(s_aT, b + 1)
            nc.scalar.copy(aoT[:, :], ps[:, 1, :]).then_inc(s_aTc, 1)

        def dve_A(dve, ch, b):
            dve_norm(dve, ch, b, "A", src=xin)
            dve_X_values(dve, b, "B")
            v1 = TA["v1"].rearrange("p (a n) -> p a n", a=NT)
            nc.vector.memset(v1[:, :, P:AW], 1.0)
            for z in range(2):
                dve.wait_ge(s_akv, b * NT + 2 * z + 2)
                o = ps[:, 2 + z, :].rearrange("p (a n) -> p a n", a=2)
                wide = lambda n: row[n].unsqueeze(1).to_broadcast([P, 2, P])
                ch(nc.vector.tensor_tensor(tmp[:, 2 * z * P:2 * (z + 1) * P].rearrange("p (a n) -> p a n", a=2),
                                           o[:, :, 0:P], wide("A_bk"), ALU.add))
                nc.vector.tensor_tensor(v1[:, 2 * z:2 * z + 2, 0:P], o[:, :, P:2 * P], wide("A_bv"), ALU.add)
                for i in (2 * z, 2 * z + 1):
                    nc.vector.tensor_scalar(TA["kf"][:, i * P:(i + 1) * P], tmp[:, i * P:(i + 1) * P], 0.0,
                                            dec_col[:, i:i + 1], ALU.max, ALU.mult).then_inc(s_akvr, 1)
            dve.wait_ge(s_aqr, b + 1)
            nc.vector.tensor_tensor(TA["qf"], q_t[:, :], dec_row[:, :], ALU.mult).then_inc(s_abd, 1)
            dve.wait_ge(s_akvp, b + 1)
            nc.vector.tensor_tensor(TA["bd"][:, 0:P], ps[:, 4, 0:P], c["block"], ALU.mult).then_inc(s_abd, 1)
            nc.vector.tensor_tensor(TA["bd"][:, P:AW], ps[:, 4, P:AW],
                                    c["block"].rearrange("p (h e) -> p h e", h=H)[:, :, 0], ALU.mult).then_inc(s_abd, 1)
            dve.wait_ge(s_aout, b + 1)
            den = TA["den"].rearrange("p (i h) -> p i h", i=NT)
            o = ps[:, 5:7, :].rearrange("p a (z n) -> p (a z) n", z=2)
            ch(nc.vector.tensor_scalar(den, o[:, :, P:AW], ATT_EPS, None, ALU.add))
            ch(nc.vector.reciprocal(TA["den"], TA["den"]))
            for i in range(NT):
                nc.vector.tensor_tensor(TA["ao"][:, i * P:(i + 1) * P].rearrange("p (h e) -> p h e", h=H),
                                        o[:, i, 0:P].rearrange("p (h e) -> p h e", h=H),
                                        den[:, i, :].unsqueeze(2).to_broadcast([P, H, DK]), ALU.mult).then_inc(s_aao, 1)
            km = kmask[:, bass.ds(b, 1), :].to_broadcast([P, NT, KP])
            for r in range(REP):
                ins = nc.vector.tensor_tensor(bmask[:, :, r * KP:(r + 1) * KP], amask[:, :, :], km, ALU.min)
            ins.then_inc(XA["B"]["mask"], 1)
            dve_residual(dve, ch, b, 0, 0, src=xin)

        XBANK = dict(B=4, E=1)

        def pe_X_context(pe, b, k):
            s = XA[k]
            pe.wait_ge(SH[DH[k][0]]["ctx"], b * 32 + 32)
            flat = ctxT[:, :, :].rearrange("p a n -> p (a n)")
            nc.tensor.matmul(ps[:, XBANK[k], 0:KP], w[k + "_k"], flat[:, 0:KP], start=True, stop=True).then_inc(s["kv"], 1)
            for j in range(NPER):
                o = ps[:, XBANK[k] + 1 + j // 4, (j % 4) * P:(j % 4 + 1) * P]
                ins = nc.tensor.matmul(o, flat[:, j * P % KP:j * P % KP + P], w[k + "_v"], start=True, stop=True)
            ins.then_inc(s["kv"], 1)

        def pe_X(pe, b, k):
            s = XA[k]
            pe_transpose(pe, b, k)
            nc.tensor.matmul(ps[:, 4, :], w[k + "_q"], xnT[:, :], start=True, stop=True).then_inc(s["qp"], 1)
            mask = bmask if k == "B" else xmask
            pe.wait_ge(s["kbd"], b + 1)
            pe.wait_ge(s["vs"], b + 1)
            pe.wait_ge(s["qt"], b + 1)
            if k == "B":
                pe.wait_ge(s["mask"], b + 1)

            rounds = [(0, 4), (4, 8), (8, NCH)]

            def scores(n, first, last):
                i, half, bank = n // 2, n % 2, 3 * (n % 2)
                k0 = 0 if k == "B" else min(i * P, KS)
                for j in range(first, last + 1):
                    at, width = j * 512, min(512, HALF - j * 512)
                    nc.tensor.matmul(ps[:, bank + j, 0:width], q_t[:, i * P:(i + 1) * P],
                                     TX["kbd"][:, half * HALF + at:half * HALF + at + width],
                                     start=True, stop=k0 > 0, skip_group_check=True)
                    if k0 == 0:
                        out_, in_ = ps[:, bank + j, 0:width], mask[:, i, at % KP:at % KP + width]
                    else:
                        heads = [h for h in range(H // 2) if at <= h * KP + k0 < at + width]
                        assert all(h * KP + k0 >= at and (h + 1) * KP <= at + width for h in heads)
                        at0, nh = heads[0] * KP + k0 - at, len(heads)
                        out_ = ps[:, bank + j, at0:at0 + 1]
                        out_ = bass.AP(out_.tensor, out_.offset, [list(out_.ap[0]), [KP, nh], [1, KP - k0]])
                        in_ = mask[:, i, k0:KP].unsqueeze(1).to_broadcast([P, nh, KP - k0])
                    ins = nc.tensor.matmul(out_, identb[:, :], in_, start=False, stop=True, skip_group_check=True)
                if last == 2:
                    ins.then_inc(s["sc"], 1)

            def flip(n, r):
                c0, c1 = rounds[r]
                m = 3 * n + r
                if m >= 2:
                    pe.wait_ge(s["ptc"], b * 3 * NXH + m - 1)
                for cc in range(c0, c1):
                    ins = nc.tensor.transpose(ps[:, 6 + m % 2, (cc - c0) * P:(cc - c0 + 1) * P],
                                              TX["d%d" % (n % 2)][:, cc * P:(cc + 1) * P], c["ident"])
                ins.then_inc(s["pt"], 1)

            scores(0, 0, 2)
            scores(1, 0, 2)
            for n in range(NXH):
                half, bank = n % 2, 3 * (n % 2)
                for r in (0, 1):
                    pe.wait_ge(s["exp"], b * 2 * NXH + 2 * n + r + 1)
                    flip(n, r)
                if 1 <= n < NXH - 1:
                    pe.wait_ge(s["o"], b * NXH + n)
                    scores(n + 1, 2, 2)
                if n + 2 < NXH:
                    scores(n + 2, 0, 1)
                flip(n, 2)
                for r, (c0, c1) in enumerate(rounds):
                    pe.wait_ge(s["ptc"], b * 3 * NXH + 3 * n + r + 1)
                    for cc in range(c0, c1):
                        ins = nc.tensor.matmul(ps[:, bank + 2, 256:256 + VW], TX["pt"][:, cc * P:(cc + 1) * P],
                                               vs[:, half * NCH + cc, :], start=(cc == 0), stop=(cc == NCH - 1))
                ins.then_inc(s["pv"], 1)
            pe_bias(DH[k][0], 1, k + "_bo")
            for i in range(NT):
                pe.wait_ge(s["o"], b * NXH + 2 * i + 2)
                ins = nc.tensor.transpose(ps[:, 0, i * P:(i + 1) * P], TX["ao"][:, i * P:(i + 1) * P], c["ident"])
            ins.then_inc(s["aT"], 1)
            pe.wait_ge(s["aTc"], b + 1)
            pe_project(pe, b, DH[k][0], 1, w[k + "_o"])

        def act_X_keys(act, b, k):
            s = XA[k]
            kb = COLB.index(k + "_bk")
            act.wait_ge(s["kv"], b * 2 + 1)
            nc.scalar.activation(TX["kt"], ps[:, XBANK[k], 0:KP], ACT.Identity, bias=colb[:, kb:kb + 1])\
                .then_inc(s["kt"], 1)

        def act_X(act, b, k):
            s = XA[k]
            qb = COLB.index(k + "_bq")
            act_root(act, b, k, then=ACT.Exp)
            act_transpose(act, b, k)
            act.wait_ge(s["qp"], b + 1)
            nc.scalar.activation(q_t[:, :], ps[:, 4, :], ACT.Identity, bias=colb[:, qb:qb + 1]).then_inc(s["qt"], 1)
            scale = SOFT if k == "B" else 1.0 / KS ** 0.5

            def exps(n):
                for z in range(2):
                    act.wait_ge(s["sub"], b * 2 * NXH + 2 * n + z + 1)
                    d = TX["d%d" % (n % 2)][:, z * HALF // 2:(z + 1) * HALF // 2]
                    nc.scalar.activation(d, d, ACT.Exp, scale=scale).then_inc(s["exp"], 1)

            def copy(n, r):
                c0, c1 = [(0, 4), (4, 8), (8, NCH)][r]
                m = 3 * n + r
                if r == 0 and n >= 1:
                    act.wait_ge(s["pv"], b * NXH + n)
                act.wait_ge(s["pt"], b * 3 * NXH + m + 1)
                nc.scalar.copy(TX["pt"][:, c0 * P:c1 * P], ps[:, 6 + m % 2, 0:(c1 - c0) * P]).then_inc(s["ptc"], 1)

            exps(0)
            for n in range(NXH):
                for r in range(3):
                    copy(n, r)
                if n + 1 < NXH:
                    exps(n + 1)
            act.wait_ge(s["aT"], b + 1)
            nc.scalar.copy(aoT[:, :], ps[:, 0, :]).then_inc(s["aTc"], 1)

        def dve_X_values(dve, b, k):
            s = XA[k]
            dve.wait_ge(s["kv"], b * 2 + 2)
            nc.vector.tensor_tensor(TX["vrep"].rearrange("p (a n) -> p a n", a=NPER),
                                    ps[:, XBANK[k] + 1:XBANK[k] + 3, :].rearrange("p a n -> p (a n)")[:, 0:NPER * P]
                                    .rearrange("p (a n) -> p a n", a=NPER),
                                    row[k + "_bv"].unsqueeze(1).to_broadcast([P, NPER, P]), ALU.add).then_inc(s["vrep"], 1)

        def dve_X(dve, ch, b, k):
            s = XA[k]
            dve_norm(dve, ch, b, k)

            def shift(n):
                bank = 3 * (n % 2)
                sc = ps[:, bank:bank + 3, :].rearrange("p a n -> p (a n)")[:, 0:HALF].rearrange("p (h k) -> p h k", h=8)
                m = TX["m"][:, 8 * (n % 2):8 * (n % 2) + 8]
                dve.wait_ge(s["sc"], b * NXH + n + 1)
                ch(nc.vector.tensor_reduce(m, sc, AX.X, ALU.max))
                if n >= 2:
                    dve.wait_ge(s["pt"], b * 3 * NXH + 3 * (n - 1))
                for z in range(2):
                    hh = slice(4 * z, 4 * z + 4)
                    nc.vector.tensor_tensor(TX["d%d" % (n % 2)].rearrange("p (h k) -> p h k", h=8)[:, hh, :],
                                            sc[:, hh, :], m[:, hh].unsqueeze(2).to_broadcast([P, 4, KP]), ALU.subtract)\
                        .then_inc(s["sub"], 1)
                gg = TX["g"][:, 8 * (n % 2):8 * (n % 2) + 8]
                rr = TX["r"][:, 8 * (n % 2):8 * (n % 2) + 8]
                ch(nc.vector.tensor_scalar(gg, m, MASKED / 2, None, ALU.is_gt))
                ch(nc.vector.reciprocal(rr, gg))
                ch(nc.vector.tensor_tensor(gg, gg, rr, ALU.mult))

            def normalise(n):
                i, half, bank = n // 2, n % 2, 3 * (n % 2)
                o = ps[:, bank + 2, 256:256 + VW]
                gg = TX["g"][:, 8 * (n % 2):8 * (n % 2) + 8]
                rr = TX["r"][:, 8 * (n % 2):8 * (n % 2) + 8]
                dve.wait_ge(s["pv"], b * NXH + n + 1)
                ch(nc.vector.reciprocal(rr, o[:, VH:VW]))
                ch(nc.vector.tensor_tensor(rr, rr, gg, ALU.mult))
                nc.vector.tensor_tensor(
                    TX["ao"][:, i * P + half * 64:i * P + half * 64 + 64].rearrange("p (h e) -> p h e", h=8),
                    o[:, 0:VH].rearrange("p (h e) -> p h e", h=8),
                    rr.unsqueeze(2).to_broadcast([P, 8, DK]), ALU.mult).then_inc(s["o"], 1)

            for n in range(NXH + 1):
                if n < NXH:
                    shift(n)
                if n >= 1:
                    normalise(n - 1)
            dve_residual(dve, ch, b, DH[k][0], 1)

        def pool_X(pool, b, k):
            s = XA[k]
            pool.wait_ge(s["kt"], b + 1)
            nc.gpsimd.tensor_tensor(TX["kbd"].rearrange("p (h k) -> p h k", h=H),
                                    TX["kt"].unsqueeze(1).to_broadcast([P, H, KP]),
                                    c["block"].rearrange("p (h e) -> p h e", h=H)[:, :, 0:1].to_broadcast([P, H, KP]),
                                    ALU.mult).then_inc(s["kbd"], 1)
            pool.wait_ge(s["vrep"], b + 1)
            for j in range(2 * NCH // NPER):
                half = j * NPER // NCH
                mask = vmask[:, :, 96 - 32 * j + VH * half:96 - 32 * j + VH * half + VH]
                ins = nc.gpsimd.tensor_tensor(vs[:, j * NPER:(j + 1) * NPER, 0:VH],
                                              TX["vrep"].rearrange("p (a n) -> p a n", a=NPER)
                                              [:, :, half * VH:(half + 1) * VH], mask, ALU.mult)
                ins = nc.gpsimd.tensor_copy(vs[:, j * NPER:(j + 1) * NPER, VH:VW],
                                            mask.rearrange("p a (h e) -> p a h e", h=H // 2)[:, :, :, 0])
            ins.then_inc(s["vs"], 1)

        def bc(a, *shape):
            return a.to_broadcast([P, *shape])

        gt = {n: sb("gt_" + n, [P, NT, E1]) for n in ("logit", "eq", "oh1", "oh2", "sel", "pos", "junk")}
        gs = {n: sb("gs_" + n, [P, NT]) for n in ("m1", "m2", "top", "e2", "s1", "s2", "t1", "t2", "a1", "a2", "cy", "cz")}

        def dve_first(ch, logits, best, oh, done=None, then=None):
            ch(nc.vector.tensor_reduce(best[:, :], logits, AX.X, ALU.max))
            if then:
                then()
            ch(nc.vector.tensor_tensor(gt["eq"][:, :, :], logits, bc(best[:, :].unsqueeze(2), NT, E1), ALU.is_ge))
            ch(nc.vector.tensor_tensor(gt["eq"][:, :, :], gt["eq"][:, :, :],
                                       bc(row["rank"][:, 0:E1].unsqueeze(1), NT, E1), ALU.mult))
            ch(nc.vector.tensor_reduce(gs["top"][:, :], gt["eq"][:, :, :], AX.X, ALU.max))
            (done or ch)(nc.vector.tensor_tensor(oh, gt["eq"][:, :, :], bc(gs["top"][:, :].unsqueeze(2), NT, E1), ALU.is_equal))

        SC = {n: sem("s_c_" + n) for n in ("gate", "oh", "ohT", "ohTc", "b2", "h", "hs", "y", "acc")}
        used[0] = 0
        TC = dict(h0=cut(4 * S), h1=cut(4 * S), ohT=cut(S))
        NC1 = HID1 // P

        def pe_C(pe, b):
            pe_transpose(pe, b, "C")
            for i in range(NT):
                ins = nc.tensor.matmul(ps[:, 1, i * E1:(i + 1) * E1], xnT[:, i * P:(i + 1) * P], cwg[:, :],
                                       start=True, stop=True)
            ins.then_inc(SC["gate"], 1)

            def hidden(e):
                for j in range(NC1):
                    m = e * NC1 + j
                    if m >= 2:
                        pe.wait_ge(SC["hs"], b * E1 * NC1 + m - 1)
                    nc.tensor.matmul(ps[:, 4 + m % 2, :], cw1[:, e, j * P:(j + 1) * P], xnT[:, :],
                                     start=True, stop=True).then_inc(SC["h"], 1)

            hidden(0)
            pe.wait_ge(SC["oh"], b + 1)
            for i in range(NT):
                ins = nc.tensor.transpose(ps[:, 2, i * P:(i + 1) * P], onehot[:, i, :], c["ident"])
            ins.then_inc(SC["ohT"], 1)
            pe.wait_ge(SC["ohTc"], b + 1)
            for i in range(NT):
                ins = nc.tensor.matmul(ps[:, 3, i * P:(i + 1) * P], TC["ohT"][:, i * P:(i + 1) * P], cb2[:, :],
                                       start=True, stop=True)
            ins.then_inc(SC["b2"], 1)
            for e in range(E1):
                if e + 1 < E1:
                    hidden(e + 1)
                pe.wait_ge(SC["hs"], b * E1 * NC1 + (e + 1) * NC1)
                if e >= 2:
                    pe.wait_ge(SC["acc"], b * E1 + e - 1)
                for i in range(NT):
                    for j in range(NC1):
                        ins = nc.tensor.matmul(ps[:, 6 + e % 2, i * P:(i + 1) * P],
                                               TC["h%d" % (e % 2)][:, j * S + i * P:j * S + (i + 1) * P],
                                               cw2[:, e * NC1 + j, :], start=(j == 0), stop=(j == NC1 - 1))
                ins.then_inc(SC["y"], 1)

        def act_C(act, b):
            act_root(act, b, "C", then=ACT.Gelu)
            act_transpose(act, b, "C")
            for e in range(E1):
                if e == 1:
                    act.wait_ge(SC["ohT"], b + 1)
                    nc.scalar.copy(TC["ohT"], ps[:, 2, :]).then_inc(SC["ohTc"], 1)
                if e >= 2:
                    act.wait_ge(SC["y"], b * E1 + e - 1)
                for j in range(NC1):
                    m = e * NC1 + j
                    act.wait_ge(SC["h"], b * E1 * NC1 + m + 1)
                    nc.scalar.activation(TC["h%d" % (e % 2)][:, j * S:(j + 1) * S], ps[:, 4 + m % 2, :], ACT.Gelu,
                                         bias=colb[:, len(COLB) + m:len(COLB) + m + 1]).then_inc(SC["hs"], 1)

        def dve_C(dve, ch, b):
            dve_norm(dve, ch, b, "C")
            dve.wait_ge(SC["gate"], b + 1)
            dve_first(ch, ps[:, 1, 0:NT * E1].rearrange("p (i e) -> p i e", i=NT), gs["m1"], onehot[:, :, 0:E1],
                      lambda ins: ins.then_inc(SC["oh"], 1))
            dve.wait_ge(SC["oh"], b + 1)
            dve.wait_ge(SC["b2"], b + 1)
            ch(nc.vector.tensor_tensor(x[:, :, :], ps[:, 3, :].rearrange("p (i n) -> p i n", i=NT), x[:, :, :], ALU.add))
            for e in range(E1):
                dve.wait_ge(SC["y"], b * E1 + e + 1)
                for i in range(NT):
                    ins = nc.vector.scalar_tensor_tensor(x[:, i, :], ps[:, 6 + e % 2, i * P:(i + 1) * P],
                                                         onehot[:, i, e:e + 1], x[:, i, :], ALU.mult, ALU.add)
                ins.then_inc(SC["acc"], 1)
                dve.wait_ge(SC["acc"], b * E1 + e + 1)

        SD = {n: sem("s_d_" + n) for n in ("kp", "kt", "qt", "v", "spill", "ld", "a", "sc", "max", "exp", "t", "ptc", "pv",
                                           "win", "rk", "own", "sum", "y", "yst", "ao", "at")}
        used[0] = 0
        RW = P + DK * DK
        TD = [dict(q=q, kt=cut(S), vr0=cut(NT * RW), vr1=cut(NT * RW), qi=cut(H * NU), y1=cut(S), y2=cut(S)) for q in (q_t, xnT)]
        TD0 = dict(kt=TX["ao"], v=TX["bmask"][:, 0:S])
        TU = dict(nmax=cut(NU), rsum=cut(NU),
                  **{n + str(i): cut(z) for n, z in (("a", P), ("p", S), ("pt", S), ("wt", P + 64), ("w", 16), ("r", 1))
                     for i in range(2)})
        ai = sb("ai", [P, 2, P])
        q_s, k_s, v_s, x_s, y1_s, y2_s = (nc.dram_tensor(n, (B, P, S), F32, kind="Internal").ap()
                                          for n in ("q_s", "k_s", "v_s", "x_s", "y1_s", "y2_s"))

        RU = P // DK

        def near(m):
            return (0, m + 2) if m < NT // 2 else (m - 1, NT)

        def turns_D(eng, first, last, body):
            groups = [[(g + d) // RU for d in range(-1, 7)] for g in range(first, last, 4)]
            g = 0
            while g < len(groups):
                n = 1
                while g + n < len(groups) and groups[g + n] == groups[g]:
                    n += 1

                def four(v, tiles=groups[g]):
                    for k in range(4):
                        body(4 * v + first + k, first + k, lambda d, k=k: tiles[k + d + 1])

                if n == 1:
                    four(g)
                else:
                    with eng.Fori(g, g + n) as v:
                        four(v)
                g += n

        def DS(s):
            return (0, 1, 6, 7)[s % 4]

        def pe_D0(pe, b):
            pe_transpose(pe, b, "D")
            nc.tensor.matmul(ps[:, 1, :], w["D_q"], xnT[:, :], start=True, stop=True).then_inc(SD["kp"], 1)
            nc.tensor.matmul(ps[:, 2, :], w["D_k"], xnT[:, :], start=True, stop=True).then_inc(SD["kp"], 1)
            for i in range(NT):
                o = (NT - 1 - i) * P
                ins = nc.tensor.matmul(ps[:, 3, o:o + P], xnT[:, i * P:(i + 1) * P], w["D_v"],
                                       start=True, stop=True)
            ins.then_inc(SD["kp"], 1)

        def act_D0(act, b):
            act_root(act, b, "D")
            act_transpose(act, b, "D")
            kb = COLB.index("D_bk")
            act.wait_ge(SD["kp"], b * 3 + 2)
            nc.scalar.activation(TD0["kt"], ps[:, 2, :], ACT.Identity, bias=colb[:, kb:kb + 1]).then_inc(SD["kt"], 1)

        def dve_D0(dve, ch, b):
            dve_norm(dve, ch, b, "D")
            qb = COLB.index("D_bq")
            dve.wait_ge(SD["kp"], b * 3 + 1)
            nc.vector.tensor_scalar(q_t[:, :].rearrange("p (i u) -> p u i", i=DK),
                                    ps[:, 1, :].rearrange("p (u i) -> p u i", i=DK),
                                    colb[:, qb:qb + 1], SOFT, ALU.add, ALU.mult)\
                .then_inc(SD["qt"], 1)
            dve.wait_ge(SD["kp"], b * 3 + 3)
            nc.vector.tensor_tensor(TD0["v"].rearrange("p (i n) -> p i n", i=NT),
                                    ps[:, 3, :].rearrange("p (i n) -> p i n", i=NT),
                                    row["D_bv"].unsqueeze(1).to_broadcast([P, NT, P]), ALU.add).then_inc(SD["v"], 1)

        def sp_D0(sp, b):
            one = lambda a: a[bass.ds(b, 1)].rearrange("o p n -> p (o n)")
            sp.wait_ge(SD["qt"], b + 1)
            sp.dma_start(one(q_s), q_t[:, :]).then_inc(SD["spill"], 16)
            sp.dma_start(one(x_s), x[:, :, :].rearrange("p i n -> p (i n)")).then_inc(SD["spill"], 16)
            sp.wait_ge(SD["kt"], b + 1)
            sp.dma_start(one(k_s), TD0["kt"]).then_inc(SD["spill"], 16)
            sp.wait_ge(SD["v"], b + 1)
            sp.dma_start(one(v_s), TD0["v"]).then_inc(SD["spill"], 16)
            sp.wait_ge(SD["spill"], b * 64 + 128)

        LD = 16 * (4 + DK)

        def sp_D_load(sp, b):
            T = TD[b % 2]
            one = lambda a: a[b:b + 1].rearrange("o p n -> p (o n)")
            other = q_s.rearrange("c p q -> (c p) q").rearrange("(h b d) q -> b d h q", b=B, d=DK)
            for i in range(DK):
                sp.dma_start(T["qi"][i * DK:(i + 1) * DK, :].rearrange("d (h u) -> d h u", h=H),
                             other[b:b + 1, :, :, i * NU:(i + 1) * NU].rearrange("o d h u -> (o d) h u"))\
                    .then_inc(SD["ld"], 16)
            sp.dma_start(T["q"][:, :], one(q_s)).then_inc(SD["ld"], 16)
            sp.dma_start(T["kt"], one(k_s)).then_inc(SD["ld"], 16)
            for s in range(2):
                sp.dma_start(T["vr%d" % s].rearrange("p (j n) -> p j n", j=NT)[:, :, 0:P],
                             one(v_s).rearrange("p (j n) -> p j n", j=NT)).then_inc(SD["ld"], 16)
            sp.wait_ge(SD["ld"], b * LD + LD)

        def sp_D_store(sp, b):
            T = TD[b % 2]
            one = lambda a: a[b:b + 1].rearrange("o p n -> p (o n)")
            sp.wait_ge(SD["y"], b * NU + NU)
            sp.dma_start(one(y1_s), T["y1"]).then_inc(SD["yst"], 16)
            sp.dma_start(one(y2_s), T["y2"]).then_inc(SD["yst"], 16)
            sp.wait_ge(SD["yst"], b * 32 + 32)

        def pe_D(pe, b, slot):
            T = TD[slot]
            pe.wait_ge(SD["ld"], b * LD + LD)

            def scores(u, s, m):
                lo, hi = near(m)
                pe.wait_ge(SD["a"], b * (2 * NU) + u * 2 + 2)
                nc.tensor.matmul(ps[:, DS(s), :], TU["a%d" % (s % 2)], T["kt"], start=True, stop=False,
                                 skip_group_check=True)
                nc.tensor.matmul(ps[:, DS(s), lo * P:hi * P], ai[:, s % 2, :],
                                 rk[:, m // (NT // 2), bass.ds((NU - 1) * DK - REL0 + lo * P - u * DK, (hi - lo) * P)],
                                 start=False, stop=True, skip_group_check=True).then_inc(SD["sc"], 1)

            def flip(u, s):
                pe.wait_ge(SD["exp"], b * NU + u + 1)
                for j in range(NT):
                    ins = nc.tensor.transpose(ps[:, 2 + s % 2, j * P:(j + 1) * P],
                                              TU["p%d" % (s % 2)][:, j * P:(j + 1) * P], c["ident"])
                ins.then_inc(SD["t"], 1)

            def values(u, s, m):
                pe.wait_ge(SD["ptc"], b * NU + u + 1)
                pe.wait_ge(SD["win"], b * NU + u + 1)
                pe.wait_ge(SD["own"], b * NU + u + 1)
                tiles = list(range(*near(m)))
                width = {j: RW if j in tiles else P for j in range(NT)}
                tiles += [j for j in range(NT) if j not in tiles]
                for j in tiles:
                    o = (NT - 1 - j) * RW
                    ins = nc.tensor.matmul(ps[:, 4 + s % 2, 0:width[j]], TU["pt%d" % (s % 2)][:, j * P:(j + 1) * P],
                                           T["vr%d" % (s % 2)][:, o:o + width[j]],
                                           start=(j == tiles[0]), stop=(j == tiles[-1]), skip_group_check=True)
                ins.then_inc(SD["pv"], 1)

            def step(u, s, tile):
                scores(u + 2, s + 2, tile(2))
                flip(u, s)
                values(u - 1, s - 1, tile(-1))

            for u in range(3):
                scores(u, u, 0)
            flip(0, 0)
            step(1, 1, lambda d: 0)
            turns_D(pe, 2, NU - 2, step)
            for u in (NU - 2, NU - 1):
                flip(u, u)
                values(u - 1, u - 1, NT - 1)
            values(NU - 1, NU - 1, NT - 1)

        def act_D(act, b, slot):
            T = TD[slot]
            def body(u, s, tile):
                act.wait_ge(SD["max"], b * NU + u + 1)
                nc.scalar.activation(TU["p%d" % (s % 2)], ps[:, DS(s), :], ACT.Exp, bias=TU["nmax"][:, bass.ds(u, 1)],
                                     accum_out=TU["rsum"][:, bass.ds(u, 1)]).then_inc(SD["exp"], 1)
                act.wait_ge(SD["pv"], b * NU + u + 1)
                act.wait_ge(SD["t"], b * NU + u + 1)
                nc.scalar.copy(TU["pt%d" % (s % 2)], ps[:, 2 + s % 2, :]).then_inc(SD["ptc"], 1)

            turns_D(act, 0, NU, body)

        def dve_D(dve, b, slot):
            T = TD[slot]
            y1 = T["y1"].rearrange("p (d u) -> p d u", d=DK)
            y2 = T["y2"].rearrange("p (d u) -> p d u", d=DK)

            def top(u, s):
                dve.wait_ge(SD["sc"], b * NU + u + 3)
                nc.vector.tensor_reduce(TU["nmax"][:, bass.ds(u, 1)], ps[:, DS(s), :], AX.X, ALU.max, negate=True)\
                    .then_inc(SD["max"], 1)

            def masked(u, s):
                dve.wait_ge(SD["pv"], b * NU + u + 3)
                nc.vector.tensor_tensor(TU["wt%d" % (s % 2)], ps[:, 4 + s % 2, 0:RW], rmask[:, :], ALU.mult)\
                    .then_inc(SD["own"], 1)

            def added(u, s):
                wt, wv = TU["wt%d" % (s % 2)], TU["w%d" % (s % 2)]
                dve.wait_ge(SD["own"], b * NU + u + 3)
                nc.vector.reciprocal(TU["r%d" % (s % 2)], TU["rsum"][:, bass.ds(u, 1)])
                nc.vector.tensor_reduce(wv[:, 0:DK], wt[:, 0:P].rearrange("p (h e) -> p e h", h=H), AX.X, ALU.add)
                nc.vector.tensor_reduce(wv[:, DK:16], wt[:, P:RW].rearrange("p (i d) -> p d i", i=DK), AX.X, ALU.add)\
                    .then_inc(SD["sum"], 1)

            def scaled(u, s, m):
                wv, r = TU["w%d" % (s % 2)], TU["r%d" % (s % 2)]
                dve.wait_ge(SD["sum"], b * NU + u + 1)
                nc.vector.tensor_scalar(y1[:, :, bass.ds(u, 1)].rearrange("p d o -> p (d o)"), wv[:, 0:DK],
                                        r, None, ALU.mult)
                nc.vector.scalar_tensor_tensor(y2[:, :, bass.ds(u, 1)].rearrange("p d o -> p (d o)"), wv[:, DK:16],
                                               r, rvc[:, m // (NT // 2), :], ALU.mult, ALU.add).then_inc(SD["y"], 1)

            def step(u, s, tile):
                masked(u, s)
                scaled(u - 1, s - 1, tile(-1))
                top(u + 3, s + 3)
                added(u, s)

            for u in range(3):
                top(u, u)
            masked(0, 0)
            top(3, 3)
            added(0, 0)
            turns_D(dve, 1, NU - 3, step)
            for u in range(NU - 3, NU):
                masked(u, u)
                scaled(u - 1, u - 1, NT - 1)
                added(u, u)
            scaled(NU - 1, NU - 1, NT - 1)

        def pool_D(pool, b, slot):
            T = TD[slot]
            qu = T["q"][:, :].rearrange("p (i u) -> p u i", i=DK)
            qi = T["qi"].rearrange("p (h u) -> p h u", h=H)

            def window(u, s, m):
                lo, hi = near(m)
                pool.wait_ge(SD["pv"], b * NU + u + 1)
                w0 = rv[:, bass.ds(u * (DK * DK) + (NT - hi) * P * DK, DK)]
                src = bass.AP(w0.tensor, w0.offset, [list(w0.ap[0]), [P * DK, hi - lo], [DK, DK], [1, DK]])
                k0 = rvc[:, m // (NT // 2), :]
                const = bass.AP(k0.tensor, k0.offset, [list(k0.ap[0]), [0, hi - lo], [0, DK], [1, DK]])
                nc.gpsimd.tensor_tensor(T["vr%d" % (s % 2)].rearrange("p (j n) -> p j n", j=NT)[:, NT - hi:NT - lo, P:RW]
                                        .rearrange("p j (i d) -> p j i d", i=DK), src, const, ALU.subtract)\
                    .then_inc(SD["win"], 1)

            def spread(u, s):
                pool.wait_ge(SD["ld"], b * LD + LD)
                pool.wait_ge(SD["sc"], b * NU + u + 1)
                nc.gpsimd.tensor_tensor(TU["a%d" % (s % 2)].rearrange("p (h i) -> p h i", h=H),
                                        qu[:, bass.ds(u, 1), :].to_broadcast([P, H, DK]),
                                        c["block"].rearrange("p (h i) -> p h i", h=H), ALU.mult).then_inc(SD["a"], 1)
                nc.gpsimd.tensor_tensor(ai[0:64, s % 2, :].rearrange("p (h i) -> p h i", h=H),
                                        qi[0:64, :, bass.ds(u, 1)].to_broadcast([64, H, DK]),
                                        c["mask_i"][0:64, :].rearrange("p (h i) -> p h i", h=H), ALU.mult)\
                    .then_inc(SD["a"], 1)

            def step(u, s, tile):
                spread(u + 2, s + 2)
                window(u, s, tile(0))

            spread(0, 0)
            spread(1, 1)
            turns_D(pool, 0, NU - 4, step)
            for u in (NU - 4, NU - 3):
                step(u, u, lambda d: NT - 1)
            for u in (NU - 2, NU - 1):
                window(u, u, NT - 1)

        own4, other4, x4 = (rv[:, i * B * S:(i + 1) * B * S] for i in range(3))
        D1 = 16 * (2 * DK + 1)

        def sp_D1(sp, b):
            own = y1_s[b:b + 1].rearrange("o (h i) (d u) -> i (o h) d u", i=DK, d=DK)
            other = y2_s.rearrange("c p n -> (c p) n").rearrange("(h z i) (d u) -> z i h d u", z=B, i=DK, d=DK)[b:b + 1]
            other = other.rearrange("o i h d u -> i (o h) d u")
            for dst, src in ((own4, own), (other4, other)):
                for i in range(DK):
                    sp.dma_start(dst[:, b * S + i * NU:b * S + (i + 1) * NU],
                                 src[i:i + 1].rearrange("o h d u -> (o h) d u")).then_inc(SD["ao"], 16)
            sp.dma_start(x4[:, b * S:(b + 1) * S], x_s[b:b + 1].rearrange("o p n -> p (o n)")).then_inc(SD["ao"], 16)
            sp.wait_ge(SD["ao"], b * D1 + D1)

        def pe_D1(pe, b):
            pe_X_context(pe, b, "E")
            pe_bias(1, 0, "D_bo")
            pe.wait_ge(SD["at"], b + 1)
            pe_project(pe, b, 1, 0, w["D_o"])

        def pool_D1(pool, b):
            pool.wait_ge(SD["ao"], b * D1 + D1)
            by_unit = lambda a: a[:, bass.ds(b * S, S)].rearrange("p (i u) -> p i u", i=DK)
            nc.gpsimd.tensor_tensor(aoT[:, :].rearrange("p (u i) -> p i u", i=DK), by_unit(own4), by_unit(other4), ALU.add)\
                .then_inc(SD["at"], 1)

        def dve_D1(dve, ch, b):
            dve_X_values(dve, b, "E")
            dve_residual(dve, ch, b, 1, 0, src=x4[:, bass.ds(b * S, S)].rearrange("p (i n) -> p i n", i=NT))

        SF = {n: sem("s_f_" + n) for n in ("kp", "kr", "vp", "v", "qp", "qm", "qr", "sc", "max", "exp", "nrm", "t",
                                           "ptc", "pv", "ao", "wo")}
        used[0] = 0
        TF = dict(t0=cut(S), t1=cut(S), u0=cut(S), u1=cut(S), v=cut(NT * HKV * KD), nmax=cut(4), rsum=cut(4), rinv=cut(4),
                  p0=cut(S), p1=cut(S), p2=cut(S), pt0=cut(S), pt1=cut(S), **{f"q{i}": cut(S) for i in range(4)},
                  **{f"ao{i}": cut(S) for i in range(2)})
        krz = cut(HKV * S).rearrange("p (h s) -> p h s", h=HKV)
        assert used[0] <= ARENA - S
        yn = arena[:, ARENA - S:ARENA].rearrange("p (i n) -> p i n", i=NT)
        NTQ = HQ * KD // P

        def FS(n):
            return (1, 6, 0)[n % 3]

        def FQ(a, m):
            return (7, 0, 5, 7)[2 * a + m] if a < 2 else 5

        NUF = HQ * NT
        ORDER = [(0, 0), (0, 3), (1, 0), (1, 3), (0, 1), (0, 2), (1, 1), (1, 2)]

        def unit(n):
            hh, i = ORDER[n % len(ORDER)]
            return 2 * (n // len(ORDER)) + hh, i

        def dve_rms(dve, ch, b, g, src, dst, gamma):
            s = SH[1]
            ch(nc.vector.tensor_tensor(tmp[:, :].rearrange("p (i n) -> p i n", i=NT), src, src, ALU.mult))
            ch(nc.vector.tensor_reduce(mv[:, :, 0], tmp[:, :].rearrange("p (i n) -> p i n", i=NT), AX.X, ALU.add))
            nc.vector.tensor_scalar(var[:, :], mv[:, :, 0], 1.0 / P, RMS_EPS, ALU.mult, ALU.add).then_inc(s["var"], 1)
            dve.wait_ge(s["root"], b * NNORM[1] + g + 1)
            ch(nc.vector.reciprocal(rstd[:, :], root[:, :]))
            for i in range(NT):
                nc.vector.scalar_tensor_tensor(dst[:, i, :], src[:, i, :], rstd[:, i:i + 1], gamma,
                                               ALU.mult, ALU.mult).then_inc(s["xn"], 1)

        def pe_F(pe, b):
            pe_transpose(pe, b, "F", yn)
            for a in range(HKV * KD // P):
                for m in range(2):
                    nc.tensor.matmul(ps[:, 1 + 2 * a + m, :], fwk[:, m, a * P:(a + 1) * P], xnT[:, :],
                                     start=True, stop=True).then_inc(SF["kp"], 1)
            for i in range(NT):
                ins = nc.tensor.matmul(ps[:, 5 + i // 2, i % 2 * 256:i % 2 * 256 + 256], xnT[:, i * P:(i + 1) * P],
                                       fwv[:, :], start=True, stop=True)
            ins.then_inc(SF["vp"], 1)

            def queries(a, m):
                if (a, m) == (1, 0):
                    pe.wait_ge(SF["v"], b + 1)
                elif (a, m) == (1, 1):
                    pe.wait_ge(SF["qm"], b * 2 * NTQ + 1)
                elif a > 1:
                    pe.wait_ge(SF["qm"], b * 2 * NTQ + 2 * a + m)
                nc.tensor.matmul(ps[:, FQ(a, m), :], fwq[:, m, a * P:(a + 1) * P], xnT[:, :],
                                 start=True, stop=True).then_inc(SF["qp"], 1)

            def scores(n):
                h, i = unit(n)
                if n % len(ORDER) == 0:
                    pe.wait_ge(SF["qr"], b * NTQ + h // 2 + 1)
                wd = (i + 1) * P
                o = ps[:, FS(n), :]
                nc.tensor.matmul(o[:, 0:wd], TF["q%d" % (h // 2 % 4)][:, i * P:(i + 1) * P],
                                 krz[:, h % HKV, 0:wd], start=True, stop=False, skip_group_check=True)
                nc.tensor.matmul(o[:, i * P:wd], identb[:, :], causal[:, :], start=False, stop=True,
                                 skip_group_check=True).then_inc(SF["sc"], 1)

            def flip(n):
                i = unit(n)[1]
                pe.wait_ge(SF["nrm"], b * NUF + n + 1)
                for j in range(i + 1):
                    ins = nc.tensor.transpose(ps[:, 2 + n % 2, j * P:(j + 1) * P], TF["p%d" % (n % 3)][:, j * P:(j + 1) * P],
                                              c["ident"])
                ins.then_inc(SF["t"], 1)

            def values(n):
                h, i = unit(n)
                pe.wait_ge(SF["ptc"], b * NUF + n + 1)
                if n % (2 * NT) == 0 and n:
                    pe.wait_ge(SF["ao"], b * NTQ + h // 2)
                r0 = h % 2 * KD
                for j in range(i + 1):
                    v0 = j * HKV * KD + h % HKV * KD
                    ins = nc.tensor.matmul(ps[r0:r0 + KD, 4, i * P:(i + 1) * P], TF["v"][:, v0:v0 + KD],
                                           TF["pt%d" % (n % 2)][:, j * P:(j + 1) * P], start=(j == 0), stop=(j == i),
                                           skip_group_check=True)
                ins.then_inc(SF["pv"], 1)

            def project(a):
                pe.wait_ge(SF["ao"], b * NTQ + a + 1)
                for i in range(NT):
                    ins = nc.tensor.matmul(ps[:, 7, i * P:(i + 1) * P], TF["ao%d" % (a % 2)][:, i * P:(i + 1) * P],
                                           fwo[:, a, :], start=(a == 0 and i == 0), stop=(a == NTQ - 1),
                                           skip_group_check=True)
                ins.then_inc(SF["wo"], 1)

            for a in range(2):
                for m in range(2):
                    queries(a, m)
            pe.wait_ge(SF["kr"], b * 2 + 2)
            for n in range(3):
                scores(n)
            for n in range(NUF):
                a, r = n // (2 * NT), n % (2 * NT)
                if r in (2, 5) and a + 2 < NTQ:
                    queries(a + 2, r // 4)
                flip(n)
                if n + 3 < NUF:
                    scores(n + 3)
                if n >= 1:
                    values(n - 1)
                if r == 3 and a >= 1:
                    project(a - 1)
            values(NUF - 1)
            project(NTQ - 1)

        def act_F(act, b):
            act_root(act, b, "F")
            act_root(act, b, "F", 1, then=ACT.Exp)
            act_transpose(act, b, "F")
            act.wait_ge(SF["vp"], b + 1)
            nc.scalar.copy(TF["v"], ps[:, 5:7, :].rearrange("p a n -> p (a n)")).then_inc(SF["v"], 1)

            def exps(n):
                wd = (unit(n)[1] + 1) * P
                act.wait_ge(SF["max"], b * NUF + n + 1)
                if n >= 3:
                    act.wait_ge(SF["t"], b * NUF + n - 2)
                nc.scalar.activation(TF["p%d" % (n % 3)][:, 0:wd], ps[:, FS(n), 0:wd], ACT.Exp,
                                     bias=TF["nmax"][:, n % 4:n % 4 + 1],
                                     accum_out=TF["rsum"][:, n % 4:n % 4 + 1]).then_inc(SF["exp"], 1)

            def copy(n):
                wd = (unit(n)[1] + 1) * P
                act.wait_ge(SF["t"], b * NUF + n + 1)
                if n >= 2:
                    act.wait_ge(SF["pv"], b * NUF + n - 1)
                nc.scalar.copy(TF["pt%d" % (n % 2)][:, 0:wd], ps[:, 2 + n % 2, 0:wd]).then_inc(SF["ptc"], 1)

            exps(0)
            exps(1)
            for n in range(NUF):
                if n % (2 * NT) == 1 and n > 2 * NT:
                    gather(act, b, n // (2 * NT) - 1)
                if n + 2 < NUF:
                    exps(n + 2)
                copy(n)
            gather(act, b, NTQ - 1)

        def gather(act, b, a):
            act.wait_ge(SF["pv"], b * NUF + (a + 1) * 2 * NT)
            if a >= 2:
                act.wait_ge(SF["wo"], b * NTQ + a - 1)
            nc.scalar.copy(TF["ao%d" % (a % 2)], ps[:, 4, :]).then_inc(SF["ao"], 1)

        def dve_F(dve, ch, b):
            dve_norm(dve, ch, b, "F", ch)
            dve_rms(dve, ch, b, 2, xn[:, :, :], yn, row["F_g1"])
            for m in range(2):
                nc.vector.memset(krz[KD - m * KD:2 * KD - m * KD, m:HKV:2, :], 0.0)
            for a in range(HKV * KD // P):
                dve.wait_ge(SF["kp"], b * 4 + 2 * a + 2)
                nc.vector.tensor_tensor(TF["t%d" % a], ps[:, 1 + 2 * a, :], rot[:, 2, :], ALU.mult)
                ch(nc.vector.tensor_tensor(TF["u%d" % a], ps[:, 2 + 2 * a, :], rot[:, 3, :], ALU.mult))
                for m in range(2):
                    r0 = m * KD
                    ins = nc.vector.tensor_tensor(krz[r0:r0 + KD, 2 * a + m, :], TF["t%d" % a][r0:r0 + KD, :],
                                                  TF["u%d" % a][r0:r0 + KD, :], ALU.add)
                ins.then_inc(SF["kr"], 1)

            def rotate(a, m):
                dve.wait_ge(SF["qp"], b * 2 * NTQ + 2 * a + m + 1)
                if a >= 2 and m == 0:
                    dve.wait_ge(SF["qr"], b * NTQ + a - 1)
                elif a < 2 and m == 0:
                    dve.wait_ge(SF["kr"], b * 2 + a + 1)
                nc.vector.tensor_tensor(TF["tu"[m] + str(a % 2)], ps[:, FQ(a, m), :], rot[:, m, :], ALU.mult)\
                    .then_inc(SF["qm"], 1)

            def top(n):
                wd = (unit(n)[1] + 1) * P
                dve.wait_ge(SF["sc"], b * NUF + n + 1)
                nc.vector.tensor_reduce(TF["nmax"][:, n % 4:n % 4 + 1], ps[:, FS(n), 0:wd], AX.X, ALU.max, negate=True)\
                    .then_inc(SF["max"], 1)

            def norm(n):
                wd = (unit(n)[1] + 1) * P
                k4 = slice(n % 4, n % 4 + 1)
                dve.wait_ge(SF["exp"], b * NUF + n + 1)
                ch(nc.vector.reciprocal(TF["rinv"][:, k4], TF["rsum"][:, k4]))
                nc.vector.tensor_scalar(TF["p%d" % (n % 3)][:, 0:wd], TF["p%d" % (n % 3)][:, 0:wd],
                                        TF["rinv"][:, k4], None, ALU.mult).then_inc(SF["nrm"], 1)

            for m in range(2):
                rotate(0, m)
            for n in range(3):
                top(n)
            norm(0)
            norm(1)
            for n in range(NUF):
                if n < 2:
                    rotate(1, n)
                a, r = n // (2 * NT), n % (2 * NT)
                if r in (2, 5) and a + 2 < NTQ:
                    rotate(a + 2, r // 4)
                if n + 3 < NUF:
                    top(n + 3)
                if n + 2 < NUF:
                    norm(n + 2)
            dve.wait_ge(SF["wo"], b * NTQ + NTQ)
            ch(nc.vector.tensor_tensor(xn[:, :, :], ps[:, 7, :].rearrange("p (i n) -> p i n", i=NT), xn[:, :, :], ALU.add))

        def pool_F(pool, b):
            for a in range(NTQ):
                pool.wait_ge(SF["qm"], b * 2 * NTQ + 2 * a + 2)
                if a >= 4:
                    pool.wait_ge(SF["pv"], b * NUF + (a - 3) * 2 * NT)
                nc.gpsimd.tensor_tensor(TF["q%d" % (a % 4)], TF["t%d" % (a % 2)], TF["u%d" % (a % 2)], ALU.add)\
                    .then_inc(SF["qr"], 1)

        SG = {n: sem("s_g_" + n) for n in ("gate", "d", "e2", "oh", "cum", "h", "a", "p", "hs", "y", "acc")}
        used[0] = 0
        TG = dict(**{n + str(i): cut(S) for n in ("a", "p") for i in range(2)}, h0=cut(2 * S), h1=cut(2 * S),
                  oh=cut(NT * 2 * E2), sum=cut(2 * E2))
        NC2 = HID2 // P
        NM2 = E2 * NC2

        def pe_G(pe, b):
            pe_transpose(pe, b, "G", yn)
            for i in range(NT):
                ins = nc.tensor.matmul(ps[:, 1, i * E2:(i + 1) * E2], xnT[:, i * P:(i + 1) * P], gwr[:, :],
                                       start=True, stop=True)
            ins.then_inc(SG["gate"], 1)

            def hidden(e):
                for j in range(NC2):
                    m = e * NC2 + j
                    if m >= 2:
                        pe.wait_ge(SG["a"], b * NM2 + m - 1)
                    nc.tensor.matmul(ps[:, 2 + m % 2, :], gw2[:, e, j * P:(j + 1) * P], xnT[:, :],
                                     start=True, stop=True).then_inc(SG["h"], 1)
                    if m >= 2:
                        pe.wait_ge(SG["p"], b * NM2 + m - 1)
                    nc.tensor.matmul(ps[:, 4 + m % 2, :], gw1[:, e, j * P:(j + 1) * P], xnT[:, :],
                                     start=True, stop=True).then_inc(SG["h"], 1)

            hidden(0)
            hidden(1)
            pe.wait_ge(SG["oh"], b + 1)
            CE = 2 * E2
            cum = ps[:, 1, 64:64 + NT * CE]
            nc.tensor.matmul(cum, c["tri"], TG["oh"], start=True, stop=False, skip_group_check=True)
            nc.tensor.matmul(cum.rearrange("p (i n) -> p i n", i=NT), c["ones"],
                             ohsum[:, :].unsqueeze(1).to_broadcast([P, NT, CE]), start=False, stop=False,
                             skip_group_check=True)
            for i in range(1, NT):
                ins = nc.tensor.matmul(cum[:, i * CE:NT * CE].rearrange("p (i n) -> p i n", n=CE), c["ones"],
                                       TG["oh"][:, (i - 1) * CE:i * CE].unsqueeze(1).to_broadcast([P, NT - i, CE]),
                                       start=False, stop=(i == NT - 1), skip_group_check=True)
            ins.then_inc(SG["cum"], 1)
            for e in range(E2):
                if 1 <= e < E2 - 1:
                    hidden(e + 1)
                pe.wait_ge(SG["hs"], b * NM2 + (e + 1) * NC2)
                if e >= 2:
                    pe.wait_ge(SG["acc"], b * E2 + e - 1)
                for i in range(NT):
                    for j in range(NC2):
                        ins = nc.tensor.matmul(ps[:, 6 + e % 2, i * P:(i + 1) * P],
                                               TG["h%d" % (e % 2)][:, j * S + i * P:j * S + (i + 1) * P],
                                               gw3[:, e * NC2 + j, :], start=(j == 0), stop=(j == NC2 - 1))
                ins.then_inc(SG["y"], 1)

        def act_G(act, b):
            act_root(act, b, "G", then=ACT.Exp)
            act_transpose(act, b, "G")

            def linear(m):
                act.wait_ge(SG["h"], b * 2 * NM2 + 2 * m + 1)
                if m >= 2:
                    act.wait_ge(SG["p"], b * NM2 + m - 1)
                nc.scalar.copy(TG["a%d" % (m % 2)], ps[:, 2 + m % 2, :]).then_inc(SG["a"], 1)

            linear(0)
            linear(1)
            act.wait_ge(SG["d"], b + 1)
            nc.scalar.activation(gs["e2"][:, :], gs["t1"][:, :], ACT.Exp).then_inc(SG["e2"], 1)
            nc.scalar.activation(warm[:, 19:20], c["ones"][:, 0:1], ACT.Gelu)
            for m in range(NM2):
                if 1 <= m < NM2 - 1:
                    linear(m + 1)
                e = m // NC2
                if m % NC2 == 0 and e >= 2:
                    act.wait_ge(SG["y"], b * E2 + e - 1)
                act.wait_ge(SG["p"], b * NM2 + m + 1)
                nc.scalar.activation(TG["h%d" % (e % 2)][:, m % NC2 * S:(m % NC2 + 1) * S], TG["p%d" % (m % 2)],
                                     ACT.Gelu).then_inc(SG["hs"], 1)

        def dve_G(dve, ch, b):
            V = nc.vector
            dve_rms(dve, ch, b, 3, xn[:, :, :], yn, row["F_g2"])
            ch(nc.vector.tensor_tensor(x[:, :, :], x[:, :, :], xn[:, :, :], ALU.add))
            dve.wait_ge(SG["gate"], b + 1)
            lg, oh1, oh2, pos, junk, sel = (gt[n][:, :, :] for n in ("logit", "oh1", "oh2", "pos", "junk", "sel"))
            S_ = {n: a[:, :] for n, a in gs.items()}
            wide = lambda a: a.unsqueeze(2).to_broadcast([P, NT, E2])
            ohk = TG["oh"].rearrange("p (i k e) -> p i k e", i=NT, k=2)

            def product(m):
                dve.wait_ge(SG["a"], b * NM2 + m + 1)
                dve.wait_ge(SG["h"], b * 2 * NM2 + 2 * m + 2)
                if m >= 2:
                    dve.wait_ge(SG["hs"], b * NM2 + m - 1)
                V.tensor_tensor(TG["p%d" % (m % 2)], ps[:, 4 + m % 2, :], TG["a%d" % (m % 2)], ALU.mult)\
                    .then_inc(SG["p"], 1)

            product(0)
            product(1)
            ch(V.tensor_tensor(lg, ps[:, 1, 0:NT * E2].rearrange("p (i e) -> p i e", i=NT),
                               row["G_rb"][:, 0:E2].unsqueeze(1).to_broadcast([P, NT, E2]), ALU.add))
            dve_first(ch, lg, gs["m1"], ohk[:, :, 0, :])
            ch(V.scalar_tensor_tensor(junk, ohk[:, :, 0, :], -3e38, lg, ALU.mult, ALU.add))
            dve_first(ch, junk, gs["m2"], ohk[:, :, 1, :], lambda ins: ins.then_inc(SG["oh"], 1),
                      lambda: V.tensor_tensor(S_["t1"], S_["m2"], S_["m1"], ALU.subtract).then_inc(SG["d"], 1))
            product(2)
            product(3)
            dve.wait_ge(SG["e2"], b + 1)
            ch(V.tensor_scalar(S_["t1"], S_["e2"], 1.0, None, ALU.add))
            ch(V.reciprocal(S_["s1"], S_["t1"]))
            ch(V.tensor_tensor(S_["s2"], S_["e2"], S_["s1"], ALU.mult))
            dve.wait_ge(SG["cum"], b + 1)
            cum = ps[:, 1, 64:64 + NT * 2 * E2].rearrange("p (i k e) -> p i k e", i=NT, k=2)
            ch(V.tensor_copy(pos, cum[:, :, 0, :]))
            V.scalar_tensor_tensor(oh1, pos, float(CAP), ohk[:, :, 0, :], ALU.is_lt, ALU.mult)
            V.tensor_reduce(TG["sum"], TG["oh"].rearrange("p (i n) -> p n i", i=NT), AX.X, ALU.add)
            ch(V.tensor_tensor(junk, pos, cum[:, :, 1, :], ALU.add))
            V.tensor_tensor(ohsum[:, :], ohsum[:, :], TG["sum"], ALU.add)
            ch(V.scalar_tensor_tensor(oh2, junk, float(CAP), ohk[:, :, 1, :], ALU.is_lt, ALU.mult))
            idx = row["index"][:, 0:E2].unsqueeze(1).to_broadcast([P, NT, E2])
            V.tensor_reduce(S_["t1"], oh1, AX.X, ALU.add)
            V.tensor_reduce(S_["t2"], oh2, AX.X, ALU.add)
            V.tensor_tensor(pos, oh1, idx, ALU.mult)
            ch(V.tensor_tensor(lg, oh2, idx, ALU.mult))
            V.tensor_reduce(S_["a1"], pos, AX.X, ALU.add)
            V.tensor_reduce(S_["a2"], lg, AX.X, ALU.add)
            V.tensor_tensor(S_["cy"], S_["s1"], S_["t1"], ALU.mult)
            ch(V.tensor_tensor(S_["cz"], S_["s2"], S_["t2"], ALU.mult))
            V.tensor_tensor(S_["a1"], S_["a1"], S_["a2"], ALU.max)
            V.tensor_tensor(S_["m1"], S_["s1"], S_["cy"], ALU.subtract)
            V.tensor_tensor(S_["m2"], S_["s2"], S_["cz"], ALU.subtract)
            ch(V.tensor_tensor(S_["cy"], S_["cy"], S_["cz"], ALU.add))
            V.tensor_tensor(sel, idx, wide(S_["a1"]), ALU.is_equal)
            ch(V.tensor_tensor(S_["cz"], S_["m1"], S_["m2"], ALU.add))
            ch(V.tensor_tensor(sel, sel, wide(S_["cy"]), ALU.mult))
            for i in range(NT):
                ins = V.scalar_tensor_tensor(x[:, i, :], yn[:, i, :], gs["cz"][:, i:i + 1], x[:, i, :], ALU.mult, ALU.add)
            ch(ins)
            for e in range(E2):
                for m in range(NC2 * (e + 1), NC2 * (e + 2)):
                    if 4 <= m < NM2:
                        product(m)
                dve.wait_ge(SG["y"], b * E2 + e + 1)
                for i in range(NT):
                    o = x[:, i, :] if e + 1 < E2 else x4[:, bass.ds(b * S + i * P, P)]
                    ins = V.scalar_tensor_tensor(o, ps[:, 6 + e % 2, i * P:(i + 1) * P],
                                                 sel[:, i, e:e + 1], x[:, i, :], ALU.mult, ALU.add)
                ins.then_inc(SG["acc"], 1)
                dve.wait_ge(SG["acc"], b * E2 + e + 1)

        block = ctx.enter_context(nc.Block())
        GROUPS = [["sqc", "sqw_a", "colb", "rowb", "amask_in", "kmask_in", "xmask_in", "dec_row", "dec_col"],
                  ["sqw_b", "vmask"], ["cwg", "cw1", "cw2", "cb2"], ["rmask", "rk", "rkc", "rv", "rvc"],
                  ["fwq", "fwk", "fwv", "fwo", "rot", "gwr", "gw1", "gw2", "gw3"]]
        tiles = dict(sqw_a=sqw[:, 0:4, :], sqw_b=sqw[:, 4:len(SQW), :], sqc=sqc, colb=colb, rowb=rowb, dec_row=dec_row,
                     dec_col=dec_col, vmask=vmask, rmask=rmask, xmask_in=xmask_in, amask_in=amask_in, kmask_in=kmask_in,
                     rk=rk[:, 1, :], rkc=rkc, rv=rv, rvc=rvc,
                     cwg=cwg, cw1=cw1, cw2=cw2, cb2=cb2, fwq=fwq, fwk=fwk, fwv=fwv, fwo=fwo, rot=rot, gwr=gwr,
                     gw1=gw1, gw2=gw2, gw3=gw3)

        @block.sync
        def _(sp):
            def load_ctx(b, ph):
                for a in range(2):
                    sp.dma_start(ctxT[:, a, :], t["ctxT"][b:b + 1].rearrange("o d k -> d (o k)"))\
                        .then_inc(SH[ph]["ctx"], 16)

            def load_x(b):
                sp.dma_start(xin[:, :, :], t["x"][b:b + 1].rearrange("o (t p) d -> p (o t) d", p=P))\
                    .then_inc(SH[0]["x"], 16)

            load_x(0)
            load_ctx(0, 0)
            for names, landed in zip(GROUPS, s_const):
                for name in names:
                    if name in ("rowb", "kmask_in"):
                        src = t[name].unsqueeze(0).to_broadcast([P] + list(t[name].shape))
                    else:
                        src = t[name]
                    dst = tiles[name]
                    sp.dma_start(dst[tuple(slice(None) for _ in dst.shape)], src).then_inc(landed, 16)
            for b in range(B):
                if b + 1 < B:
                    sp.wait_ge(SH[0]["xn"], (b * NLN[0] + DH["B"][1]) * NT + 1)
                    load_x(b + 1)
                    load_ctx(b + 1, 0)
                sp_D0(sp, b)
            sp_D_load(sp, 0)
            load_ctx(0, 1)
            sp_D_load(sp, 1)
            for b in range(B):
                sp_D_store(sp, b)
                if b + 2 < B:
                    sp_D_load(sp, b + 2)
            for b in range(B):
                sp_D1(sp, b)
            for b in range(B):
                if b + 1 < B:
                    sp.wait_ge(XA["E"]["kv"], b * 2 + 2)
                    load_ctx(b + 1, 1)
                if last == "G":
                    sp.wait_ge(SG["acc"], b * E2 + E2)
                else:
                    sp.wait_ge(s_xout, b + 1)
                sp.dma_start(out[b:b + 1].rearrange("o (t p) d -> p (o t) d", p=P),
                             x4[:, b * S:(b + 1) * S].rearrange("p (i n) -> p i n", i=NT)).then_inc(s_store, 16)
            sp.wait_ge(s_store, B * 16)

        @block.tensor
        def _(pe):
            pe.wait_ge(s_const[0], 16 * len(GROUPS[0]))
            pe.wait_ge(s_zero, 1)
            pe.wait_ge(s_prep, 1)
            pe.wait_ge(s_const[1], 16 * len(GROUPS[1]))
            with pe.Fori(0, B) as b:
                pe_A(pe, b)
                pe_X(pe, b, "B")
                pe.wait_ge(s_const[2], 16 * len(GROUPS[2]))
                pe_C(pe, b)
                pe_D0(pe, b)
            pe.wait_ge(SD["rk"], 2)
            with pe.Fori(0, B // 2) as bb:
                for s in range(2):
                    pe_D(pe, 2 * bb + s, s)
            pe.wait_ge(s_const[4], 16 * len(GROUPS[4]))
            with pe.Fori(0, B) as b:
                pe_D1(pe, b)
                if "E" in stages:
                    pe_X(pe, b, "E")
                if "F" in stages:
                    pe_F(pe, b)
                if "G" in stages:
                    pe_G(pe, b)

        @block.scalar
        def _(act):
            act.wait_ge(s_const[0], 16 * len(GROUPS[0]))
            with act.Fori(0, B) as b:
                act_A(act, b)
                act_X(act, b, "B")
                act_C(act, b)
                act_D0(act, b)
            with act.Fori(0, B // 2) as bb:
                for s in range(2):
                    act_D(act, 2 * bb + s, s)
            with act.Fori(0, B) as b:
                act_X_keys(act, b, "E")
                if "E" in stages:
                    act_X(act, b, "E")
                if "F" in stages:
                    act_F(act, b)
                if "G" in stages:
                    act_G(act, b)

        @block.vector
        def _(dve):
            dve.wait_ge(s_const[0], 16 * len(GROUPS[0]))
            nc.vector.tensor_copy(identb[:, :], c["ident"])
            nc.vector.tensor_copy(causal[:, :], c["causal"])
            for r in range(REP):
                nc.vector.tensor_copy(xmask[:, :, r * KP:(r + 1) * KP], xmask_in)
            nc.vector.memset(amask[:, :, KS:KP], MASKED)
            nc.vector.memset(kmask[:, :, KS:KP], MASKED)
            nc.vector.tensor_scalar(amask[:, :, 0:KS], amask_in[:, :, :], MASKED, None, ALU.mult)
            nc.vector.tensor_scalar(kmask[:, :, 0:KS], kmask_in[:, :, :], MASKED, None, ALU.mult).then_inc(s_prep, 1)
            dve.wait_ge(s_prep, 1)
            dve.wait_ge(s_zero, 1)
            ch = Chain(dve, SH[0]["ch"], CH["first"])
            with dve.Fori(0, B) as b:
                ch.turn(b)
                dve.wait_ge(SH[0]["x"], b * 16 + 16)
                dve_A(dve, ch, b)
                dve_X(dve, ch, b, "B")
                dve_C(dve, ch, b)
                dve_D0(dve, ch, b)
                ch.end()
            dve.wait_ge(s_const[3], 16 * len(GROUPS[3]))
            nc.vector.tensor_scalar(rk[:, 0, :], rk[:, 1, :], rkc[:, 0:1], None, ALU.subtract).then_inc(SD["rk"], 1)
            dve.wait_ge(SD["rk"], 1)
            nc.vector.tensor_scalar(rk[:, 1, :], rk[:, 1, :], rkc[:, 1:2], None, ALU.subtract).then_inc(SD["rk"], 1)
            with dve.Fori(0, B // 2) as bb:
                for s in range(2):
                    dve_D(dve, 2 * bb + s, s)
            dve.wait_ge(s_const[4], 16 * len(GROUPS[4]))
            ch = Chain(dve, SH[1]["ch"], CH[last])
            with dve.Fori(0, B) as b:
                ch.turn(b)
                dve_D1(dve, ch, b)
                if "E" in stages:
                    dve_X(dve, ch, b, "E")
                if "F" in stages:
                    dve_F(dve, ch, b)
                if "G" in stages:
                    dve_G(dve, ch, b)
                if last != "G":
                    nc.vector.tensor_copy(tmp[:, 0:1], x[:, 0, 0:1]).then_inc(s_xout, 1)
                ch.end()

        @block.gpsimd
        def _(pool):
            pool.wait_ge(s_const[0], 16 * len(GROUPS[0]))
            nc.gpsimd.memset(onehot[:, :, :], 0.0).then_inc(SD["sc"], 2)
            nc.gpsimd.memset(ohsum[:, :], 0.0).then_inc(SD["pv"], 2)
            nc.gpsimd.memset(ai[:, :, :], 0.0).then_inc(s_zero, 1)
            nc.gpsimd.memset(spare2[:, 0:1], 0.0).then_inc(SD["own"], 2)
            nc.gpsimd.memset(spare2[:, 1:2], 0.0).then_inc(SD["spill"], 64)
            pool.wait_ge(s_const[1], 16 * len(GROUPS[1]))
            with pool.Fori(0, B) as b:
                pool_X(pool, b, "B")
            pool.wait_ge(s_const[3], 16 * len(GROUPS[3]))
            with pool.Fori(0, B // 2) as bb:
                for s in range(2):
                    pool_D(pool, 2 * bb + s, s)
            with pool.Fori(0, B) as b:
                pool_D1(pool, b)
                if "E" in stages:
                    pool_X(pool, b, "E")
                if "F" in stages:
                    pool_F(pool, b)


CH = {"first": 85, "D": 0, "E": 55, "F": 130, "G": 162}


def arrays_of(inputs):
    import numpy as np

    g = {k: np.asarray(v) for k, v in inputs.items()}
    f = np.float32
    d = {}
    d["x"] = g["x"]
    ctxT = np.zeros((B, P, KP), f)
    ctxT[:, :, :KS] = g["ctx_1024"].transpose(0, 2, 1)
    d["ctxT"] = ctxT
    sq = {"A_q": g["L0_attn_W_q"].T, "A_k": g["L0_attn_W_k"].T, "A_v": g["L0_attn_W_v"].T, "A_o": g["L0_attn_W_o"].T}
    for k, n, tr in (("B", "L0_xattn", True), ("D", "L1_attn", True), ("E", "L1_xattn", False)):
        for m in "qkvo":
            a = g[f"{n}_W{m}"]
            sq[f"{k}_{m}"] = a.T if tr else a
    sqw = np.stack([sq[n] for n in SQW], 1)
    d["sqw_a"], d["sqw_b"] = sqw[:, :4], sqw[:, 4:]
    r = np.arange(P)
    con = {"ident": np.eye(P), "block": r[:, None] // DK == r[None] // DK,
           "mask_i": (r[:, None] // DK == r[None] % DK) & (r[:, None] < 64),
           "tri": r[:, None] <= r[None], "ones": np.ones((P, P)),
           "causal": np.where(r[:, None] < r[None], MASKED, 0.0)}
    d["sqc"] = np.stack([con[n] for n in SQC], 1).astype(f)
    names = {"A": "L0_attn_b_", "B": "L0_xattn_b", "D": "L1_attn_b", "E": "L1_xattn_b"}
    vec = {f"{k}_b{m}": g[names[k] + m] for k in names for m in "qkvo"}
    d["colb"] = np.concatenate([np.stack([vec[n] for n in COLB], 1),
                                g["L0_ffn_b1"].reshape(-1, P).T], 1)
    rb = np.zeros(P, f)
    rb[:E2] = g["L1_ffn_router_b"]
    vec.update(F_g1=g["L1_ffn_g1"], F_g2=g["L1_ffn_g2"], G_rb=rb, rank=(E1 - r).astype(f), index=r.astype(f))
    d["rowb"] = np.stack([vec[n] for n in ROWB], 0)
    dec = np.exp(-np.arange(S, dtype=f) / S).astype(f)
    d["dec_row"] = np.broadcast_to(dec, (P, S))
    d["dec_col"] = dec.reshape(NT, P).T
    vm = np.zeros((P, NPER, P + 96), f)
    for j in range(NPER):
        at = j * P + r
        vm[:, j, 96:] = ((at // KP)[:, None] == (r // DK)[None]) & ((at % KP) < KS)[:, None]
    d["vmask"] = vm
    rm = np.zeros((P, P + 64), f)
    rm[:, :P] = con["block"]
    rm[:, P:] = (r % DK)[:, None] == (np.arange(64) // DK)[None]
    d["rmask"] = rm
    q = np.arange(S)
    xm = np.full((S, KP), MASKED, f)
    xm[:, :KS] = np.where(np.arange(KS)[None] > q[:, None], MASKED, 0.0)
    d["xmask_in"] = xm.reshape(NT, P, KP).transpose(1, 0, 2)
    d["amask_in"] = g["mask_SxS2_bk1"].astype(np.int32).reshape(NT, P, KS).transpose(1, 0, 2)
    d["kmask_in"] = g["mask_BxS2_bf0"].astype(np.int32)
    M = (len(g["L1_attn_rel_k"]) - 1) // 2
    assert M <= P
    dist = np.arange(DK)[:, None] + DK * (NU - 1) - REL0 - np.arange(RELW)[None]
    rk = np.zeros((P, RELW), f)
    rk[:DK * DK] = g["L1_attn_rel_k"][np.clip(dist, -M, M) + M].transpose(0, 2, 1).reshape(DK * DK, RELW)
    d["rk"] = rk
    rkc = np.zeros((P, 2), f)
    rkc[:DK * DK] = np.tile(g["L1_attn_rel_k"][[0, 2 * M]].T, (DK, 1))
    d["rkc"] = rkc
    dist = np.arange(RVS)[None] - r[:, None] - (S - P)
    d["rv"] = g["L1_attn_rel_v"][np.clip(dist, -M, M) + M].reshape(P, RVS * DK)
    d["rvc"] = np.broadcast_to(g["L1_attn_rel_v"][[0, 2 * M]], (P, 2, DK))
    d["cwg"] = g["L0_ffn_Wg"].T
    d["cw1"] = g["L0_ffn_W1"].transpose(1, 0, 2)
    d["cw2"] = g["L0_ffn_W2"].reshape(-1, P, P).transpose(1, 0, 2)
    cb2 = np.zeros((P, P), f)
    cb2[:E1] = g["L0_ffn_b2"]
    d["cb2"] = cb2
    half = KD // 2
    swap = lambda a: a.reshape(P, -1, 2, half)[:, :, ::-1].reshape(P, -1)
    d["fwq"] = np.stack([g["L1_ffn_wq"], swap(g["L1_ffn_wq"])], 1)
    d["fwk"] = np.stack([g["L1_ffn_wk"], swap(g["L1_ffn_wk"])], 1)
    d["fwv"] = g["L1_ffn_wv"]
    d["fwo"] = g["L1_ffn_wo"].reshape(-1, P, P).transpose(1, 0, 2)
    th = 10000.0 ** (-np.arange(0, KD, 2, dtype=f) / KD)
    tick = np.tile(np.outer(np.arange(S, dtype=f), th), (1, 2)).astype(f).T
    sign = np.where(np.arange(KD) < half, -1.0, 1.0)[:, None].astype(f)
    cos, sin = np.cos(tick), np.sin(tick) * sign
    two = lambda a: np.concatenate([a, a], 0)
    d["rot"] = np.stack([two(cos) / 8, two(sin) / 8, two(cos), two(sin)], 1).astype(f)
    d["gwr"] = g["L1_ffn_router_w"]
    for n in ("1", "2"):
        d["gw" + n] = g["L1_ffn_w" + n].transpose(1, 0, 2)
    d["gw3"] = g["L1_ffn_w3"].reshape(-1, P, P).transpose(1, 0, 2)
    return {k: np.ascontiguousarray(v) for k, v in d.items()}


def program(nc, arrays, last="G"):
    t = {n: nc.dram_tensor(f"in_{n}", a.shape, mybir.dt.from_np(a.dtype), kind="ExternalInput").ap()
         for n, a in arrays.items()}
    out = nc.dram_tensor("out", (B, S, P), F32, kind="ExternalOutput").ap()
    decoder(nc, t, out, last)


def kernel(**inputs):
    import concourse.bacc as _bacc
    from concourse.bass_utils import run_bass_kernel_spmd as _run

    arrays = arrays_of(inputs)
    nc = _bacc.Bacc("TRN2", target_bir_lowering=False, num_devices=1)
    program(nc, arrays)
    r = _run(nc, [{f"in_{n}": a for n, a in arrays.items()}], core_ids=[0])
    return r.results[0]["out"]
```
